# Optimizing a Trainium2 kernel written in Bass

```python
import numpy as np
import jax
import jax.numpy as jnp

def _softmax(x, axis=-1):
    return jax.nn.softmax(x, axis=axis)

def _gelu(x):
    return jax.nn.gelu(x, approximate=True)

def _silu(x):
    return jax.nn.silu(x)

def _sigmoid(x):
    return jax.nn.sigmoid(x)

def _layernorm(x, axis=-1, eps=1e-05):
    m = jnp.mean(x, axis=axis, keepdims=True)
    v = jnp.var(x, axis=axis, keepdims=True)
    return (x - m) / jnp.sqrt(v + eps)

def _scatter_add(tgt, idx, src, axis=0):
    return tgt.at[idx].add(src)

def _segment_sum(src, seg, n):
    return jax.ops.segment_sum(src, seg, n)
kernel_name = 'mk_gnn_ffn_d2_gnn_r16_2277e5'

def setup_inputs(seed: int=0):
    np.random.seed(seed)
    _w = jnp.asarray

    def _rec_inputs():
        import jax
        import jax.numpy as jnp
        _gk = jax.random.key(seed)
        x = -0.0003713 + 1 * jax.random.normal(jax.random.fold_in(_gk, 1), (3125, 256), jnp.float32)
        src = jax.random.randint(jax.random.fold_in(_gk, 2), (100000,), 0, 3125, jnp.int32)
        dst = jnp.minimum((3125 * jax.random.uniform(jax.random.fold_in(_gk, 3), (100000,)) ** 2.0).astype(jnp.int32), 49999)
        _o = jnp.argsort(dst, stable=True)
        src = src[_o]
        dst = dst[_o]
        return (x, src, dst)
    x, src, dst = _rec_inputs()

    def _L0_gnn_setup():
        import jax, jax.numpy as jnp
        import numpy as np
        NEG_SLOPE = 0.2

        def _gat(x, src, dst, W, a_src, a_dst, b, heads, concat):
            N = x.shape[0]
            D = a_src.shape[-1]
            h = (x @ W).reshape(N, heads, D)
            es = jnp.sum(h * a_src, axis=-1)
            ed = jnp.sum(h * a_dst, axis=-1)
            e = jax.nn.leaky_relu(es[src] + ed[dst], NEG_SLOPE)
            emax = jax.lax.stop_gradient(jax.ops.segment_max(e, dst, num_segments=N))
            ex = jnp.exp(e - emax[dst])
            denom = jax.ops.segment_sum(ex, dst, num_segments=N)
            alpha = ex / denom[dst]
            out = jax.ops.segment_sum(h[src] * alpha[:, :, None], dst, num_segments=N)
            out = out.reshape(N, heads * D) if concat else out.mean(axis=1)
            return out + b
        key = jax.random.key(seed)
        ks = jax.random.split(key, 10)
        N, E, F_in = (3125, 50000, 256)
        H, Dh, F_out = (8, 32, 256)
        x = jax.random.normal(ks[0], (N, F_in), dtype=jnp.float32)
        edge_index = jax.random.randint(ks[1], (2, E), 0, N, dtype=jnp.int32)
        s = 0.1
        return {'x': x, 'edge_index': edge_index, 'W1': jax.random.normal(ks[2], (F_in, H * Dh), dtype=jnp.float32) * s, 'a_src1': jax.random.normal(ks[3], (H, Dh), dtype=jnp.float32) * s, 'a_dst1': jax.random.normal(ks[4], (H, Dh), dtype=jnp.float32) * s, 'b1': jnp.zeros((H * Dh,), dtype=jnp.float32), 'W2': jax.random.normal(ks[5], (H * Dh, F_out), dtype=jnp.float32) * s, 'a_src2': jax.random.normal(ks[6], (1, F_out), dtype=jnp.float32) * s, 'a_dst2': jax.random.normal(ks[7], (1, F_out), dtype=jnp.float32) * s, 'b2': jnp.zeros((F_out,), dtype=jnp.float32)}
    _L0_gnn_all = _L0_gnn_setup()
    _L0_gnn_in = {k: v for k, v in _L0_gnn_all.items() if k in ('W1', 'a_src1', 'a_dst1', 'b1', 'W2', 'a_src2', 'a_dst2', 'b2')}
    del _L0_gnn_all

    def _L0_ffn_setup():
        import jax, jax.numpy as jnp
        import numpy as np
        E = 8
        K = 2
        D = 256
        H = 512
        DOUT = 256
        EPS = 1e-05
        key = jax.random.key(seed)
        ks = jax.random.split(key, 9)
        s = 0.02
        return {'x': jax.random.normal(ks[0], (4, 512, D), jnp.float32), 'gamma': 1.0 + 0.05 * jax.random.normal(ks[1], (D,), jnp.float32), 'beta': 0.05 * jax.random.normal(ks[2], (D,), jnp.float32), 'Wr': 0.01 * jax.random.normal(ks[3], (D, E), jnp.float32), 'br': jnp.zeros((E,), jnp.float32), 'W1': s * jax.random.normal(ks[4], (E, D, H), jnp.float32), 'b1': s * jax.random.normal(ks[5], (E, H), jnp.float32), 'W2': s * jax.random.normal(ks[6], (E, H, DOUT), jnp.float32), 'b2': s * jax.random.normal(ks[7], (E, DOUT), jnp.float32)}
    _L0_ffn_all = _L0_ffn_setup()
    _L0_ffn_in = {k: v for k, v in _L0_ffn_all.items() if k in ('gamma', 'beta', 'Wr', 'br', 'W1', 'b1', 'W2', 'b2')}
    del _L0_ffn_all

    def _L1_gnn_setup():
        import jax, jax.numpy as jnp
        import numpy as np
        import math
        N_NODES = 3125
        N_EDGES = 100000
        C = 256
        H = 8
        HD = C // H

        def _layernorm(x, g, b, eps=1e-05):
            mu = jnp.mean(x, axis=-1, keepdims=True)
            var = jnp.mean(jnp.square(x - mu), axis=-1, keepdims=True)
            return (x - mu) * jax.lax.rsqrt(var + eps) * g + b
        key = jax.random.key(seed)
        ks = jax.random.split(key, 16)
        s = 0.02
        d = {'feat': jax.random.normal(ks[0], (N_NODES, C), jnp.float32), 'edge_src': jax.random.randint(ks[1], (N_EDGES,), 0, N_NODES), 'edge_dst': jax.random.randint(ks[2], (N_EDGES,), 0, N_NODES), 'Wq': jax.random.normal(ks[3], (C, C), jnp.float32) * s, 'bq': jnp.zeros((C,), jnp.float32), 'Wk': jax.random.normal(ks[4], (C, C), jnp.float32) * s, 'bk': jnp.zeros((C,), jnp.float32), 'Wv': jax.random.normal(ks[5], (C, C), jnp.float32) * s, 'bv': jnp.zeros((C,), jnp.float32), 'Wp': jax.random.normal(ks[6], (C, C), jnp.float32) * s, 'bp': jnp.zeros((C,), jnp.float32), 'ln_g': jnp.ones((C,), jnp.float32), 'ln_b': jnp.zeros((C,), jnp.float32), 'W1': jax.random.normal(ks[7], (4 * C, C), jnp.float32) * s, 'b1': jnp.zeros((4 * C,), jnp.float32), 'W2': jax.random.normal(ks[8], (C, 4 * C), jnp.float32) * s, 'b2': jnp.zeros((C,), jnp.float32)}
        return d
    _L1_gnn_all = _L1_gnn_setup()
    _L1_gnn_in = {k: v for k, v in _L1_gnn_all.items() if k in ('Wq', 'bq', 'Wk', 'bk', 'Wv', 'bv', 'Wp', 'bp', 'ln_g', 'ln_b', 'W1', 'b1', 'W2', 'b2')}
    del _L1_gnn_all

    def _L1_ffn_setup():
        import jax, jax.numpy as jnp
        import numpy as np
        B, A = (256, 8)
        IN, OUT = (256, 256)
        SH1, SH2 = (256, 128)
        EH1, EH2 = (128, 64)
        E, TOPK = (4, 2)

        def _shared_mlp(x, W1, b1, W2, b2, W3, b3):
            h = jax.nn.relu(x @ W1 + b1)
            h = jax.nn.relu(h @ W2 + b2)
            return h @ W3 + b3

        def _experts_mlp(x, eW1, eb1, eW2, eb2, eW3, eb3):
            h = jax.nn.relu(jnp.einsum('baf,efh->ebah', x, eW1) + eb1[:, None, None, :])
            h = jax.nn.relu(jnp.einsum('ebah,ehg->ebag', h, eW2) + eb2[:, None, None, :])
            o = jnp.einsum('ebag,ego->ebao', h, eW3) + eb3[:, None, None, :]
            return jnp.moveaxis(o, 0, -1)
        key = jax.random.key(seed)
        ks = jax.random.split(key, 16)
        s = 0.05
        return {'x': jax.random.normal(ks[0], (B, A, IN), jnp.float32), 'sW1': jax.random.normal(ks[1], (IN, SH1), jnp.float32) * s, 'sb1': jnp.zeros((SH1,), jnp.float32), 'sW2': jax.random.normal(ks[2], (SH1, SH2), jnp.float32) * s, 'sb2': jnp.zeros((SH2,), jnp.float32), 'sW3': jax.random.normal(ks[3], (SH2, OUT), jnp.float32) * s, 'sb3': jnp.zeros((OUT,), jnp.float32), 'eW1': jax.random.normal(ks[4], (E, IN, EH1), jnp.float32) * s, 'eb1': jnp.zeros((E, EH1), jnp.float32), 'eW2': jax.random.normal(ks[5], (E, EH1, EH2), jnp.float32) * s, 'eb2': jnp.zeros((E, EH2), jnp.float32), 'eW3': jax.random.normal(ks[6], (E, EH2, OUT), jnp.float32) * s, 'eb3': jnp.zeros((E, OUT), jnp.float32), 'gW': jax.random.normal(ks[7], (IN, E), jnp.float32) * s, 'gb': jnp.zeros((E,), jnp.float32)}
    _L1_ffn_all = _L1_ffn_setup()
    _L1_ffn_in = {k: v for k, v in _L1_ffn_all.items() if k in ('sW1', 'sb1', 'sW2', 'sb2', 'sW3', 'sb3', 'eW1', 'eb1', 'eW2', 'eb2', 'eW3', 'eb3', 'gW', 'gb')}
    del _L1_ffn_all
    return {'x': x, 'src': src, 'dst': dst, 'L0_gnn_W1': _L0_gnn_in['W1'], 'L0_gnn_a_src1': _L0_gnn_in['a_src1'], 'L0_gnn_a_dst1': _L0_gnn_in['a_dst1'], 'L0_gnn_b1': _L0_gnn_in['b1'], 'L0_gnn_W2': _L0_gnn_in['W2'], 'L0_gnn_a_src2': _L0_gnn_in['a_src2'], 'L0_gnn_a_dst2': _L0_gnn_in['a_dst2'], 'L0_gnn_b2': _L0_gnn_in['b2'], 'L0_ffn_gamma': _L0_ffn_in['gamma'], 'L0_ffn_beta': _L0_ffn_in['beta'], 'L0_ffn_Wr': _L0_ffn_in['Wr'], 'L0_ffn_br': _L0_ffn_in['br'], 'L0_ffn_W1': _L0_ffn_in['W1'], 'L0_ffn_b1': _L0_ffn_in['b1'], 'L0_ffn_W2': _L0_ffn_in['W2'], 'L0_ffn_b2': _L0_ffn_in['b2'], 'L1_gnn_Wq': _L1_gnn_in['Wq'], 'L1_gnn_bq': _L1_gnn_in['bq'], 'L1_gnn_Wk': _L1_gnn_in['Wk'], 'L1_gnn_bk': _L1_gnn_in['bk'], 'L1_gnn_Wv': _L1_gnn_in['Wv'], 'L1_gnn_bv': _L1_gnn_in['bv'], 'L1_gnn_Wp': _L1_gnn_in['Wp'], 'L1_gnn_bp': _L1_gnn_in['bp'], 'L1_gnn_ln_g': _L1_gnn_in['ln_g'], 'L1_gnn_ln_b': _L1_gnn_in['ln_b'], 'L1_gnn_W1': _L1_gnn_in['W1'], 'L1_gnn_b1': _L1_gnn_in['b1'], 'L1_gnn_W2': _L1_gnn_in['W2'], 'L1_gnn_b2': _L1_gnn_in['b2'], 'L1_ffn_sW1': _L1_ffn_in['sW1'], 'L1_ffn_sb1': _L1_ffn_in['sb1'], 'L1_ffn_sW2': _L1_ffn_in['sW2'], 'L1_ffn_sb2': _L1_ffn_in['sb2'], 'L1_ffn_sW3': _L1_ffn_in['sW3'], 'L1_ffn_sb3': _L1_ffn_in['sb3'], 'L1_ffn_eW1': _L1_ffn_in['eW1'], 'L1_ffn_eb1': _L1_ffn_in['eb1'], 'L1_ffn_eW2': _L1_ffn_in['eW2'], 'L1_ffn_eb2': _L1_ffn_in['eb2'], 'L1_ffn_eW3': _L1_ffn_in['eW3'], 'L1_ffn_eb3': _L1_ffn_in['eb3'], 'L1_ffn_gW': _L1_ffn_in['gW'], 'L1_ffn_gb': _L1_ffn_in['gb']}

def reference(x, src, dst, L0_gnn_W1, L0_gnn_a_src1, L0_gnn_a_dst1, L0_gnn_b1, L0_gnn_W2, L0_gnn_a_src2, L0_gnn_a_dst2, L0_gnn_b2, L0_ffn_gamma, L0_ffn_beta, L0_ffn_Wr, L0_ffn_br, L0_ffn_W1, L0_ffn_b1, L0_ffn_W2, L0_ffn_b2, L1_gnn_Wq, L1_gnn_bq, L1_gnn_Wk, L1_gnn_bk, L1_gnn_Wv, L1_gnn_bv, L1_gnn_Wp, L1_gnn_bp, L1_gnn_ln_g, L1_gnn_ln_b, L1_gnn_W1, L1_gnn_b1, L1_gnn_W2, L1_gnn_b2, L1_ffn_sW1, L1_ffn_sb1, L1_ffn_sW2, L1_ffn_sb2, L1_ffn_sW3, L1_ffn_sb3, L1_ffn_eW1, L1_ffn_eb1, L1_ffn_eW2, L1_ffn_eb2, L1_ffn_eW3, L1_ffn_eb3, L1_ffn_gW, L1_ffn_gb):
    import jax
    import jax.numpy as jnp

    def _L0_gnn_ref(x, edge_index, W1, a_src1, a_dst1, b1, W2, a_src2, a_dst2, b2):
        import jax, jax.numpy as jnp
        import numpy as np
        NEG_SLOPE = 0.2

        def _gat(x, src, dst, W, a_src, a_dst, b, heads, concat):
            N = x.shape[0]
            D = a_src.shape[-1]
            h = (x @ W).reshape(N, heads, D)
            es = jnp.sum(h * a_src, axis=-1)
            ed = jnp.sum(h * a_dst, axis=-1)
            e = jax.nn.leaky_relu(es[src] + ed[dst], NEG_SLOPE)
            emax = jax.lax.stop_gradient(jax.ops.segment_max(e, dst, num_segments=N))
            ex = jnp.exp(e - emax[dst])
            denom = jax.ops.segment_sum(ex, dst, num_segments=N)
            alpha = ex / denom[dst]
            out = jax.ops.segment_sum(h[src] * alpha[:, :, None], dst, num_segments=N)
            out = out.reshape(N, heads * D) if concat else out.mean(axis=1)
            return out + b
        N = x.shape[0]
        loop = jnp.arange(N, dtype=edge_index.dtype)
        src = jnp.concatenate([edge_index[0], loop])
        dst = jnp.concatenate([edge_index[1], loop])
        x1 = jax.nn.elu(_gat(x, src, dst, W1, a_src1, a_dst1, b1, heads=8, concat=True))
        x2 = jax.nn.elu(_gat(x1, src, dst, W2, a_src2, a_dst2, b2, heads=1, concat=False))
        return x2

    def _L0_ffn_ref(x, gamma, beta, Wr, br, W1, b1, W2, b2):
        import jax, jax.numpy as jnp
        import numpy as np
        E = 8
        K = 2
        D = 256
        H = 512
        DOUT = 256
        EPS = 1e-05
        mu = jnp.mean(x, axis=-1, keepdims=True)
        var = jnp.mean(jnp.square(x - mu), axis=-1, keepdims=True)
        xn = (x - mu) * jax.lax.rsqrt(var + EPS) * gamma + beta
        logits = jnp.einsum('bsd,de->bse', xn, Wr) + br
        top_vals, top_idx = jax.lax.top_k(logits, K)
        w = jax.nn.softmax(top_vals, axis=-1)
        w_full = jnp.einsum('bsk,bske->bse', w, jax.nn.one_hot(top_idx, E, dtype=w.dtype))
        y = jnp.zeros(x.shape[:-1] + (DOUT,), x.dtype)
        for e in range(E):
            h = jax.nn.gelu(jnp.einsum('bsd,dh->bsh', xn, W1[e]) + b1[e], approximate=False)
            y_e = jnp.einsum('bsh,hd->bsd', h, W2[e]) + b2[e]
            y = y + y_e * w_full[..., e, None]
        return y

    def _L1_gnn_ref(feat, edge_src, edge_dst, Wq, bq, Wk, bk, Wv, bv, Wp, bp, ln_g, ln_b, W1, b1, W2, b2):
        import jax, jax.numpy as jnp
        import numpy as np
        import math
        N_NODES = 3125
        N_EDGES = 100000
        C = 256
        H = 8
        HD = C // H

        def _layernorm(x, g, b, eps=1e-05):
            mu = jnp.mean(x, axis=-1, keepdims=True)
            var = jnp.mean(jnp.square(x - mu), axis=-1, keepdims=True)
            return (x - mu) * jax.lax.rsqrt(var + eps) * g + b
        n = feat.shape[0]
        q = (feat @ Wq.T + bq).reshape(n, H, HD)
        k = (feat @ Wk.T + bk).reshape(n, H, HD)
        v = (feat @ Wv.T + bv).reshape(n, H, HD)
        score = jnp.einsum('ehd,ehd->eh', q[edge_dst], k[edge_src])
        score = jnp.clip(score / math.sqrt(HD), -10.0, 10.0)
        smax = jax.ops.segment_max(score, edge_dst, num_segments=n)
        smax = jnp.where(jnp.isfinite(smax), smax, 0.0)
        ex = jnp.exp(score - smax[edge_dst])
        den = jax.ops.segment_sum(ex, edge_dst, num_segments=n)
        alpha = ex / den[edge_dst]
        wv = jax.ops.segment_sum(alpha[:, :, None] * v[edge_src], edge_dst, num_segments=n).reshape(n, C)
        y = wv @ Wp.T + bp
        x = feat + y
        h = _layernorm(x, ln_g, ln_b)
        h = jax.nn.gelu(h @ W1.T + b1, approximate=False) @ W2.T + b2
        return x + h

    def _L1_ffn_ref(x, sW1, sb1, sW2, sb2, sW3, sb3, eW1, eb1, eW2, eb2, eW3, eb3, gW, gb):
        import jax, jax.numpy as jnp
        import numpy as np
        B, A = (256, 8)
        IN, OUT = (256, 256)
        SH1, SH2 = (256, 128)
        EH1, EH2 = (128, 64)
        E, TOPK = (4, 2)

        def _shared_mlp(x, W1, b1, W2, b2, W3, b3):
            h = jax.nn.relu(x @ W1 + b1)
            h = jax.nn.relu(h @ W2 + b2)
            return h @ W3 + b3

        def _experts_mlp(x, eW1, eb1, eW2, eb2, eW3, eb3):
            h = jax.nn.relu(jnp.einsum('baf,efh->ebah', x, eW1) + eb1[:, None, None, :])
            h = jax.nn.relu(jnp.einsum('ebah,ehg->ebag', h, eW2) + eb2[:, None, None, :])
            o = jnp.einsum('ebag,ego->ebao', h, eW3) + eb3[:, None, None, :]
            return jnp.moveaxis(o, 0, -1)
        all_out = _experts_mlp(x, eW1, eb1, eW2, eb2, eW3, eb3)
        shared = _shared_mlp(x, sW1, sb1, sW2, sb2, sW3, sb3)
        gates = jax.nn.softmax(x @ gW + gb, axis=-1)
        topv, topi = jax.lax.top_k(gates, TOPK)
        topw = jax.nn.softmax(topv, axis=-1)
        sel = jnp.take_along_axis(all_out, topi[:, :, None, :], axis=-1)
        gated = jnp.sum(sel * topw[:, :, None, :], axis=-1)
        return shared + gated
    edge_index = jnp.stack([src, dst])
    x = x + _L0_gnn_ref(_layernorm(x, axis=-1), edge_index, L0_gnn_W1, L0_gnn_a_src1, L0_gnn_a_dst1, L0_gnn_b1, L0_gnn_W2, L0_gnn_a_src2, L0_gnn_a_dst2, L0_gnn_b2)
    x = x + _L0_ffn_ref(_layernorm(x, axis=-1)[None], L0_ffn_gamma, L0_ffn_beta, L0_ffn_Wr, L0_ffn_br, L0_ffn_W1, L0_ffn_b1, L0_ffn_W2, L0_ffn_b2)[0]
    x = x + _L1_gnn_ref(_layernorm(x, axis=-1), src, dst, L1_gnn_Wq, L1_gnn_bq, L1_gnn_Wk, L1_gnn_bk, L1_gnn_Wv, L1_gnn_bv, L1_gnn_Wp, L1_gnn_bp, L1_gnn_ln_g, L1_gnn_ln_b, L1_gnn_W1, L1_gnn_b1, L1_gnn_W2, L1_gnn_b2)
    x = x + _L1_ffn_ref(_layernorm(x, axis=-1)[None], L1_ffn_sW1, L1_ffn_sb1, L1_ffn_sW2, L1_ffn_sb2, L1_ffn_sW3, L1_ffn_sb3, L1_ffn_eW1, L1_ffn_eb1, L1_ffn_eW2, L1_ffn_eb2, L1_ffn_eW3, L1_ffn_eb3, L1_ffn_gW, L1_ffn_gb)[0]
    return x

_drawn_inputs = setup_inputs


def setup_inputs(seed=0):
    import zlib

    import numpy as np

    out = dict(_drawn_inputs(seed))
    spreads = {'L0_gnn_b1': (0.0, 0.1),
     'L0_gnn_b2': (0.0, 0.1),
     'L0_ffn_br': (0.0, 0.1),
     'L1_gnn_bq': (0.0, 0.8),
     'L1_gnn_bk': (0.0, 0.8),
     'L1_gnn_bv': (0.0, 0.485),
     'L1_gnn_bp': (0.0, 0.1),
     'L1_gnn_ln_g': (1.0, 0.6),
     'L1_gnn_ln_b': (0.0, 0.8),
     'L1_gnn_b1': (0.0, 0.452),
     'L1_gnn_b2': (0.0, 0.1),
     'L1_ffn_sb1': (0.0, 0.75),
     'L1_ffn_sb2': (0.0, 0.423),
     'L1_ffn_sb3': (0.0, 0.1),
     'L1_ffn_eb1': (0.0, 2.0),
     'L1_ffn_eb2': (0.0, 0.8),
     'L1_ffn_eb3': (0.0, 0.1),
     'L1_ffn_gb': (0.0, 0.719)}
    factors = {'L0_ffn_gamma': 6.94,
     'L0_ffn_beta': 5.476,
     'L0_ffn_b1': 8.0,
     'L0_ffn_b2': 4.366,
     'L1_gnn_Wq': 8.0,
     'L1_gnn_Wk': 8.0,
     'L1_gnn_Wv': 2.905}
    for name, (base, spread) in spreads.items():
        noise = np.random.default_rng([zlib.crc32(name.encode()), seed]).standard_normal(out[name].shape)
        drawn = base * np.exp(spread * noise) if base else spread * noise
        out[name] = jnp.asarray(drawn.astype(out[name].dtype))
    for name, factor in factors.items():
        out[name] = (out[name] * factor).astype(out[name].dtype)
    return out
```

```python
from contextlib import ExitStack

import concourse.bass as bass
from concourse import mybir

P = 128
N = 3125
NT = -(-N // P)
NP = NT * P
LAST = N - (NT - 1) * P
F = 256
KF = F // P
E = 100000
EP = 125
EJ = E // EP
EG = 4
CELLS = NP * NP
CH = 400
NCH = NP // CH
ST = 5
NL = NT // ST
TC = 5
TN = TC * P
TH = TN // 2
NTC = NT // TC
EPS = 1e-5
DUP = 4096.0

F32 = mybir.dt.float32
U32 = mybir.dt.uint32
ALU = mybir.AluOpType
ACT = mybir.ActivationFunctionType
AX = mybir.AxisListType
RMAX = bass.bass_isa.ReduceOp.max


class Chain:

    def __init__(self, eng, sem):
        self.eng, self.sem, self.n, self.base = eng, sem, 0, 0

    def __call__(self, ins):
        ins.then_inc(self.sem, 1)
        self.n += 1
        self.eng.wait_ge(self.sem, self.base + self.n)


class Core:

    def __init__(self, nc, ctx):
        self.nc, self.ctx, self.count, self.used = nc, ctx, 0, []

    def lasting_sem(self, name):
        self.count += 1
        return self.nc.alloc_semaphore(name=f"{name}_{self.count}")

    def sem(self, name):
        self.count += 1
        self.used.append(self.nc.alloc_semaphore(name=f"{name}_{self.count}"))
        return self.used[-1]

    def stage_ends(self):
        for s in self.used:
            self.nc.gpsimd.sem_clear(s)
            self.nc.release_semaphore(s)
        self.used = []

    def sb(self, ctx, name, shape, dt=F32):
        self.count += 1
        return ctx.enter_context(self.nc.sbuf_tensor(f"{name}_{self.count}", shape, dt))

    def ps(self, ctx, name, shape, dt=F32):
        self.count += 1
        return ctx.enter_context(self.nc.psum_tensor(f"{name}_{self.count}", shape, dt))


def stage_load(core, x_in):
    nc = core.nc
    X, ident, onescol, C = core.X, core.ident, core.ones, core.C
    with ExitStack() as ctx:
        zero = core.sb(ctx, "zero", [P, NP])
        s_zero, s_xpad, s_x, s_clear, s_diag, s_id = (core.sem(n) for n in (
            "zero_made", "x_pad_cleared", "x_in", "c_cleared", "diag_set", "ident"))
        c_rows = C[0:CELLS, 0:1].rearrange("(t p d) o -> t p (d o)", p=P, d=NP)
        with nc.Block() as block:
            @block.sync
            def _(sp):
                sp.wait_ge(s_xpad, 1)
                sp.dma_start(X[:, 0:NT - 1, :], x_in[0:(NT - 1) * P, :].rearrange("(t p) f -> p t f", p=P)).then_inc(s_x, 16)
                sp.dma_start(X[0:LAST, NT - 1, :], x_in[(NT - 1) * P:N, :]).then_inc(s_x, 16)
                sp.wait_ge(s_zero, 1)
                for t in range(NT):
                    sp.dma_start(c_rows[t], zero[:, :]).then_inc(s_clear, 16)
                sp.wait_ge(s_clear, 16 * NT)
                diag = bass.AP(C.tensor, 0, [[NP + 1, NP], [1, 1]])
                sp.dma_start(diag.rearrange("(p t) o -> p t o", p=P), onescol[:, 0:NT].unsqueeze(2),
                             allow_slow_non_contiguous=True).then_inc(s_diag, 16)
                sp.wait_ge(s_diag, 16)
                sp.wait_ge(s_x, 32)

            @block.vector
            def _(dve):
                nc.vector.memset(X[:, NT - 1, :], 0.0).then_inc(s_xpad, 1)
                nc.vector.memset(onescol[:, :], 1.0)
                nc.vector.memset(zero[:, :], 0.0).then_inc(s_zero, 1)

            @block.gpsimd
            def _(pool):
                nc.gpsimd.memset(ident[:, :], 0.0).then_inc(s_id, 1)
                pool.wait_ge(s_id, 1)
                nc.gpsimd.affine_select(out=ident[:, :], in_=ident[:, :], compare_op=ALU.not_equal, fill=1.0,
                                        base=0, pattern=[[-1, P]], channel_multiplier=1).then_inc(s_id, 1)
    core.stage_ends()


def stage_edges(core, src, dst):
    nc = core.nc
    ident, onesm, C = core.ident, core.ones, core.C
    R = 2
    GN = EJ // EG
    W = EG * EP
    with ExitStack() as ctx:
        ei = core.sb(ctx, "edge_ids", [EP, 2, EJ], mybir.dt.int32)
        ef = core.sb(ctx, "edge_ids_f", [EP, 2, EJ])
        cell = core.sb(ctx, "cell", [EP, EJ + EG])
        spare = core.sb(ctx, "spare", [EP, EG])
        rank = core.sb(ctx, "rank", [EP, EG, W])
        diag = core.sb(ctx, "diag", [EP, R, W])
        same = core.sb(ctx, "same", [EP, EG, W])
        here = core.sb(ctx, "here", [EP, R, EG])
        cnt = core.sb(ctx, "cnt", [EP, R, EG])
        away = core.sb(ctx, "away", [EP, EG])
        idx = core.sb(ctx, "idx", [EP, R, EG], U32)
        rows = core.ps(ctx, "rows", [EP, R, W // 500, 512])
        s_spare, s_cell, s_rank, s_dve, s_first = (core.sem(n) for n in (
            "spare_made", "cells_made", "rank_made", "dve", "first_cells"))
        s_here, s_diag, s_rows, s_idx = ([core.sem(n) for _ in range(R)] for n in (
            "here_made", "diag_made", "rows_made", "idx_made"))
        s_scat = [core.lasting_sem("scattered") for _ in range(R)]
        with nc.Block() as block:
            @block.gpsimd
            def _(pool):
                for r, e in enumerate((src, dst)):
                    pool.dma_start(ei[:, r, :], e.rearrange("(p j) -> p j", p=EP)).then_inc(s_scat[r], 16)
                nc.gpsimd.iota(spare[:, :], pattern=[[EP, EG]], base=CELLS, channel_multiplier=1,
                               allow_small_or_imprecise_dtypes=True).then_inc(s_spare, 1)
                nc.gpsimd.memset(rank[:, :, :], 1.0).then_inc(s_rank, 1)
                pool.wait_ge(s_rank, 1)
                nc.gpsimd.affine_select(out=rank[:, :, :], in_=rank[:, :, :], compare_op=ALU.is_ge, fill=DUP,
                                        base=0, pattern=[[-EP, EG], [1, W]], channel_multiplier=-1).then_inc(s_rank, 1)
                with pool.Fori(0, GN // R) as i:
                    for r in range(R):
                        pool.wait_ge(s_idx[r], i + 2)
                        pool.wait_ge(s_scat[r - 1], (i + (r > 0)) * (16 * EG) + 16)
                        bound = pool.snap(i + (CELLS + W - 1 + r))
                        for g in range(EG):
                            nc.gpsimd.indirect_dma_start(
                                out=C[:, :], out_offset=bass.IndirectOffsetOnAxis(idx[:, r, g:g + 1], 0),
                                in_=cnt[:, r, g:g + 1], in_offset=None, bounds_check=bound,
                                compute_op=ALU.add).then_inc(s_scat[r], 16)
                for r in range(R):
                    pool.wait_ge(s_scat[r], GN // R * 16 * EG + 16)

            @block.scalar
            def _(act):
                with act.Fori(0, GN // R) as i:
                    for r in range(R):
                        act.wait_ge(s_here[r], i + 1)
                        act.wait_ge(s_rows[r], i + 1)
                        for g in range(EG):
                            ins = nc.scalar.activation(diag[:, r, g * EP:(g + 1) * EP], ident[0:EP, 0:EP], ACT.Copy,
                                                       scale=here[:, r, g:g + 1])
                        ins.then_inc(s_diag[r], 1)

            @block.tensor
            def _(pe):
                for r in range(R):
                    nc.tensor.sem_inc(s_rows[r], 1)
                with pe.Fori(0, GN // R) as i:
                    for r in range(R):
                        pe.wait_ge(s_diag[r], i + 1)
                        pe.wait_ge(s_idx[r], i + 1)
                        for b in range(0, W, 500):
                            ins = nc.tensor.matmul(rows[:, r, b // 500, 0:500], onesm[0:EP, 0:EP], diag[:, r, b:b + 500],
                                                   start=True, stop=True)
                        ins.then_inc(s_rows[r], 1)

            @block.vector
            def _(dve):
                link = Chain(dve, s_dve)
                for r in range(R):
                    nc.vector.sem_inc(s_idx[r], 1)
                    dve.wait_ge(s_scat[r], 16)
                link(nc.vector.tensor_copy(ef[:, :, :], ei[:, :, :]))
                nc.vector.memset(cell[:, EJ:EJ + EG], 0.0).then_inc(s_cell, 1)
                nc.vector.scalar_tensor_tensor(out=cell[:, 0:EJ], in0=ef[:, 0, :], scalar=float(NP), in1=ef[:, 1, :],
                                               op0=ALU.mult, op1=ALU.add).then_inc(s_cell, 1)
                dve.wait_ge(s_cell, 2)
                dve.wait_ge(s_rank, 2)
                dve.wait_ge(s_spare, 1)
                nc.vector.tensor_copy(here[:, 0, :], cell[:, 0:EG]).then_inc(s_here[0], 1)
                with dve.Fori(0, GN // R) as i:
                    link.n, link.base = 0, i * (R * 3) + 1
                    for r in range(R):
                        q = (r + 1) % R
                        dve.wait_ge(s_idx[q], i + 1 + (q == 0))
                        nc.vector.tensor_copy(here[:, q, :], cell[:, bass.ds((i * R + r + 1) * EG, EG)]).then_inc(s_here[q], 1)
                        dve.wait_ge(s_here[r], i + 1)
                        dve.wait_ge(s_rows[r], i + 2)
                        dve.wait_ge(s_scat[r], i * (16 * EG) + 16)
                        for g in range(EG):
                            ins = nc.vector.scalar_tensor_tensor(
                                out=same[:, g, :].rearrange("p (b w) -> p b w", w=500), in0=rows[:, r, :, 0:500], scalar=here[:, r, g:g + 1],
                                in1=rank[:, g, :].rearrange("p (b w) -> p b w", w=500),
                                op0=ALU.is_equal, op1=ALU.mult, accum_out=cnt[:, r, g:g + 1])
                        link(ins)
                        link(nc.vector.tensor_tensor(away[:, :], spare[:, :], here[:, r, :], ALU.subtract))
                        link(nc.vector.scalar_tensor_tensor(out=away[:, :], in0=cnt[:, r, :], scalar=DUP, in1=away[:, :],
                                                            op0=ALU.is_ge, op1=ALU.mult))
                        nc.vector.tensor_tensor(idx[:, r, :], away[:, :], here[:, r, :], ALU.add).then_inc(s_idx[r], 1)
    core.stage_ends()


def stage_norm(core, src, dst, gamma=None, beta=None, times=1, park=None):
    nc, XT, ident = core.nc, core.XT, core.ident
    with ExitStack() as ctx:
        tmp = core.sb(ctx, "squares", [P, NT, F])
        mean = core.sb(ctx, "mean", [P, NT])
        var = core.sb(ctx, "var", [P, NT])
        std = core.sb(ctx, "std", [P, NT])
        gb = core.sb(ctx, "gamma_beta", [P, 2, F])
        flip = core.ps(ctx, "flip", [P, 8, 512])
        s_gb, s_dve, s_var, s_std, s_flip = (core.sem(n) for n in (
            "gamma_in", "dve", "var_made", "std_made", "flipped"))
        s_evac = [core.sem("evacuated_by_vector"), core.sem("evacuated_by_scalar")]
        s_norm, s_park = core.sem("norm_made"), core.sem("parked")
        turns = [(k, t0, min(4, NT - t0)) for k in range(KF) for t0 in range(0, NT, 4)]
        with nc.Block() as block:
            @block.sync
            def _(sp):
                if gamma is not None:
                    for k, row in enumerate((gamma, beta)):
                        sp.dma_start(gb[:, k, :], row.partition_broadcast(P)).then_inc(s_gb, 16)
                    sp.wait_ge(s_gb, 32)
                if park is not None:
                    sp.wait_ge(s_norm, 1)
                    sp.dma_start(park, dst[:, :, :]).then_inc(s_park, 16)
                    sp.wait_ge(s_park, 16)

            @block.vector
            def _(dve):
                link = Chain(dve, s_dve)
                a = src
                for n in range(times):
                    link(nc.vector.tensor_reduce(mean[:, :], a[:, :, :], AX.X, ALU.add))
                    link(nc.vector.tensor_scalar(mean[:, :], mean[:, :], -1.0 / F, None, ALU.mult))
                    link(nc.vector.tensor_tensor(dst[:, :, :], a[:, :, :], mean[:, :].unsqueeze(2).to_broadcast([P, NT, F]), ALU.add))
                    link(nc.vector.tensor_tensor(tmp[:, :, :], dst[:, :, :], dst[:, :, :], ALU.mult))
                    link(nc.vector.tensor_reduce(var[:, :], tmp[:, :, :], AX.X, ALU.add))
                    nc.vector.tensor_scalar(var[:, :], var[:, :], 1.0 / F, EPS, ALU.mult, ALU.add).then_inc(s_var, 1)
                    dve.wait_ge(s_std, n + 1)
                    link(nc.vector.reciprocal(std[:, :], std[:, :]))
                    link(nc.vector.tensor_tensor(dst[:, :, :], dst[:, :, :], std[:, :].unsqueeze(2).to_broadcast([P, NT, F]), ALU.mult))
                    a = dst
                if gamma is not None:
                    dve.wait_ge(s_gb, 32)
                    link(nc.vector.tensor_tensor(dst[:, :, :], dst[:, :, :], gb[:, 0:1, :].to_broadcast([P, NT, F]), ALU.mult))
                    link(nc.vector.tensor_tensor(dst[:, :, :], dst[:, :, :], gb[:, 1:2, :].to_broadcast([P, NT, F]), ALU.add))
                nc.vector.tensor_copy(mean[:, 0:1], dst[:, 0, 0:1]).then_inc(s_norm, 1)
                for n, (k, t0, m) in enumerate(turns):
                    if n % 2 == 0:
                        dve.wait_ge(s_flip, n + 1)
                        nc.vector.tensor_copy(XT[:, k, t0 * P:(t0 + m) * P], flip[:, n % 8, 0:m * P]).then_inc(s_evac[n % 2], 1)

            @block.scalar
            def _(act):
                for n in range(times):
                    act.wait_ge(s_var, n + 1)
                    nc.scalar.activation(std[:, :], var[:, :], ACT.Sqrt).then_inc(s_std, 1)
                for n, (k, t0, m) in enumerate(turns):
                    if n % 2:
                        act.wait_ge(s_flip, n + 1)
                        nc.scalar.copy(XT[:, k, t0 * P:(t0 + m) * P], flip[:, n % 8, 0:m * P]).then_inc(s_evac[n % 2], 1)

            @block.tensor
            def _(pe):
                pe.wait_ge(s_norm, 1)
                for n, (k, t0, m) in enumerate(turns):
                    if n >= 8:
                        pe.wait_ge(s_evac[n % 2], (n - 8) // 2 + 1)
                    for j in range(m):
                        ins = nc.tensor.transpose(flip[:, n % 8, j * P:(j + 1) * P], dst[:, t0 + j, k * P:(k + 1) * P],
                                                  ident[:, :])
                    ins.then_inc(s_flip, 1)
    core.stage_ends()


def stage_gat_weights(core, g, W, a_src, a_dst, H):
    nc, XT = core.nc, core.XT
    D = F // H
    R = g.rep
    wx, wdb, msg, kap, bias = g.wx, g.wdb, g.msg, g.kap, g.bias
    with ExitStack() as ctx:
        h = core.sb(ctx, "h", [P, NT, F + H])
        ab = core.sb(ctx, "a_rows", [P, 2, F])
        wa = core.sb(ctx, "w_times_a", [P, KF, F])
        wd = core.sb(ctx, "w_dst", [P, KF, H])
        es = core.sb(ctx, "es", [P, NT, H])
        pad = core.sb(ctx, "pad", [P, NT])
        top = core.sb(ctx, "top", [P, H])
        allm = core.sb(ctx, "greatest", [P, H])
        av = core.sb(ctx, "a_factor", [P, NT, H])
        bA = core.sb(ctx, "bias_a", [P, H])
        proj = core.ps(ctx, "proj", [P, 8, 512])
        s_w, s_dve, s_wx, s_proj, s_h, s_pad, s_top, s_all, s_bias, s_exp = (core.sem(n) for n in (
            "w_in", "dve", "wx_made", "projected", "h_made", "pad_made", "top_made", "greatest_made", "bias_made", "exp_made"))
        with nc.Block() as block:
            @block.sync
            def _(sp):
                sp.dma_start(wx[:, :, 0:F], W.rearrange("(k p) n -> p k n", p=P)).then_inc(s_w, 16)
                for k, row in enumerate((a_src, a_dst)):
                    sp.dma_start(ab[:, k, :], row.rearrange("h d -> (h d)").partition_broadcast(P)).then_inc(s_w, 16)
                sp.wait_ge(s_w, 48)

            @block.gpsimd
            def _(pool):
                nc.gpsimd.memset(pad[:, :], 0.0).then_inc(s_pad, 1)
                pool.wait_ge(s_pad, 1)
                nc.gpsimd.affine_select(out=pad[:, :], in_=pad[:, :], compare_op=ALU.is_ge, fill=-1e30, base=N - 1,
                                        pattern=[[-P, NT]], channel_multiplier=-1).then_inc(s_pad, 1)
                pool.wait_ge(s_top, 1)
                nc.gpsimd.partition_all_reduce(allm[:, :], top[:, :], P, RMAX).then_inc(s_all, 1)

            @block.vector
            def _(dve):
                link = Chain(dve, s_dve)
                dve.wait_ge(s_w, 48)
                for k, out in ((0, wx[:, :, F:F + H]), (1, wd[:, :, :])):
                    link(nc.vector.tensor_tensor(wa[:, :, :], wx[:, :, 0:F], ab[:, k:k + 1, :].to_broadcast([P, KF, F]), ALU.mult))
                    link(nc.vector.tensor_reduce(out, wa[:, :, :].rearrange("p k (h d) -> p k h d", h=H), AX.X, ALU.add))
                nc.vector.tensor_copy(wdb[:, :, :, :], wd[:, :, :].unsqueeze(3).to_broadcast([P, KF, H, P])).then_inc(s_wx, 1)
                dve.wait_ge(s_h, NT)
                dve.wait_ge(s_pad, 2)
                link(nc.vector.tensor_tensor(es[:, :, :], h[:, :, F:F + H], pad[:, :].unsqueeze(2).to_broadcast([P, NT, H]), ALU.add))
                nc.vector.tensor_reduce(top[:, :], es[:, :, :].rearrange("p t h -> p h t"), AX.X, ALU.max).then_inc(s_top, 1)
                dve.wait_ge(s_all, 1)
                link(nc.vector.tensor_tensor(es[:, :, :], h[:, :, F:F + H], allm[:, :].unsqueeze(1).to_broadcast([P, NT, H]), ALU.min))
                link(nc.vector.tensor_scalar(bA[:, :], allm[:, :], -0.2, BIAS_A, ALU.mult, ALU.add))
                nc.vector.tensor_scalar(bias[:, :], allm[:, :], -0.8, BIAS_K, ALU.mult, ALU.add).then_inc(s_bias, 1)
                dve.wait_ge(s_exp, 2 * H)
                m = msg[:, :, :, 0:D]
                link(nc.vector.tensor_tensor(m, h[:, :, 0:F].rearrange("p t (h d) -> p t h d", h=H),
                                             av[:, :, :].unsqueeze(3).to_broadcast([P, NT, H, D]), ALU.mult))
                link(nc.vector.tensor_copy(msg[:, :, :, D:D + R], av[:, :, :].unsqueeze(3).to_broadcast([P, NT, H, R])))

            @block.scalar
            def _(act):
                for t in range(NT):
                    act.wait_ge(s_proj, t + 1)
                    nc.scalar.copy(h[:, t, :], proj[:, t % 8, 0:F + H]).then_inc(s_h, 1)
                act.wait_ge(s_bias, 1)
                for j in range(H):
                    nc.scalar.activation(av[:, :, j], es[:, :, j], ACT.Exp, bias=bA[:, j:j + 1], scale=0.2).then_inc(s_exp, 1)
                    nc.scalar.activation(kap[:, :, j], es[:, :, j], ACT.Exp, bias=bias[:, j:j + 1], scale=0.8).then_inc(s_exp, 1)

            @block.tensor
            def _(pe):
                pe.wait_ge(s_wx, 1)
                for t in range(NT):
                    if t >= 8:
                        pe.wait_ge(s_h, t - 7)
                    for k in range(KF):
                        ins = nc.tensor.matmul(proj[:, t % 8, 0:F + H], XT[:, k, t * P:(t + 1) * P], wx[:, k, :],
                                               start=(k == 0), stop=(k == KF - 1))
                    ins.then_inc(s_proj, 1)
    core.stage_ends()


BIAS_A = 30.0
BIAS_K = 35.0
RHO_MAX = 1.5860134523134308e15


def load_counts(core, sp, cbuf, s_c, s_w, per):
    nc, C = core.nc, core.C
    rows = C[0:CELLS, 0:1].rearrange("(l t p d) o -> l p t (d o)", t=ST, p=P, d=NP)
    for n in range(NL):
        sp.dma_start(cbuf[:, n, :, :], rows[n][:, :, 0:CH]).then_inc(s_c[n], 16)
    with sp.Fori(1, NCH) as i:
        for n in range(NL):
            sp.wait_ge(s_w, i * per - (per - per // NL * (n + 1)) + 1)
            sp.dma_start(cbuf[:, n, :, :], rows[n][:, :, bass.ds(i * CH, CH)]).then_inc(s_c[n], 16)


def stage_gat_aggregate(core, g, b, H):
    nc, XT = core.nc, core.XT
    D = F // H
    WR = 8
    per = NT * H
    msg, kap, bias, wdb = g.msg, g.kap, g.bias, g.wdb
    with ExitStack() as ctx:
        cbuf = core.sb(ctx, "counts", [P, NL, ST, CH])
        rho = core.sb(ctx, "rho", [P, H, CH])
        w = core.sb(ctx, "weights", [P, WR, CH])
        inv = core.sb(ctx, "inv", [P, 8, CH])
        y = core.sb(ctx, "y", [P, KF, CH])
        ey = core.sb(ctx, "exp_y", [P, KF, CH])
        bcol = core.sb(ctx, "bias_cols", [P, KF])
        acc = core.ps(ctx, "acc", [P, 4, 512])
        row = core.ps(ctx, "row", [P, 4, 512])
        s_c = [core.sem("counts_in") for _ in range(NL)]
        s_b, s_row, s_exp, s_rho, s_w, s_used, s_dve, s_neg, s_ey, s_y = (core.sem(n) for n in (
            "bias_in", "rows_made", "rho_raw", "rho_made", "w_made", "w_used", "dve", "neg_made", "exp_y_made", "y_done"))
        with nc.Block() as block:
            @block.sync
            def _(sp):
                sp.dma_start(bcol[:, :], b.rearrange("(k p) -> p k", p=P), allow_slow_non_contiguous=True).then_inc(s_b, 16)
                load_counts(core, sp, cbuf, s_c, s_w, per)

            @block.tensor
            def _(pe):
                with pe.Fori(0, NCH) as i:
                    for j in range(H):
                        if j < 4:
                            pe.wait_ge(s_exp, i * H + 1)
                        else:
                            pe.wait_ge(s_exp, i * H + j - 2)
                        for k in range(KF):
                            ins = nc.tensor.matmul(row[:, j % 4, 0:CH], wdb[:, k, j, :], XT[:, k, bass.ds(i * CH, CH)],
                                                   start=(k == 0), stop=(k == KF - 1))
                        ins.then_inc(s_row, 1)
                    pe.wait_ge(s_y, i + 1)
                    for t in range(NT):
                        for j in range(H):
                            n = t * H + j
                            pe.wait_ge(s_w, i * per + n + 2)
                            if H == 1:
                                for q in range(3):
                                    ins = nc.tensor.matmul(acc[:, q, 0:CH], msg[:, t, 0, q * P:(q + 1) * P], w[:, n % WR, :],
                                                           start=(t == 0), stop=(t == NT - 1))
                            else:
                                o = 64 * (j % 2)
                                ins = nc.tensor.matmul(acc[o:o + 64, j // 2, 0:CH], msg[:, t, j, :], w[:, n % WR, :],
                                                       start=(t == 0), stop=(t == NT - 1))
                            ins.then_inc(s_used, 1)

            @block.scalar
            def _(act):
                nc.scalar.sem_inc(s_exp, 1)
                with act.Fori(0, NCH) as i:
                    act.wait_ge(s_w, i * per + 1)
                    for j in range(H):
                        act.wait_ge(s_row, i * H + j + 1)
                        nc.scalar.activation(rho[:, j, :], row[:, j % 4, 0:CH], ACT.Exp, bias=bias[:, j:j + 1],
                                             scale=-0.8).then_inc(s_exp, 1)
                    act.wait_ge(s_neg, i + 1)
                    nc.scalar.activation(ey[:, :, :], ey[:, :, :], ACT.Exp).then_inc(s_ey, 1)

            @block.vector
            def _(dve):
                link = Chain(dve, s_dve)
                nc.vector.sem_inc(s_w, 1)
                nc.vector.sem_inc(s_y, 1)
                dve.wait_ge(s_b, 16)
                with dve.Fori(0, NCH) as i:
                    NLINK = 4 if H == 1 else 3 + H
                    link.n, link.base = 0, i * NLINK
                    dve.wait_ge(s_exp, (i + 1) * H + 1)
                    nc.vector.tensor_scalar(rho[:, :, :], rho[:, :, :], RHO_MAX, None, ALU.min).then_inc(s_rho, 1)
                    dve.wait_ge(s_rho, i + 1)
                    for t in range(NT):
                        if t % ST == 0:
                            dve.wait_ge(s_c[t // ST], (i + 1) * 16)
                        for j in range(H):
                            n = t * H + j
                            if n >= WR:
                                dve.wait_ge(s_used, i * per + n - WR + 1)
                            nc.vector.scalar_tensor_tensor(out=w[:, n % WR, :], in0=rho[:, j, :], scalar=kap[:, t, j:j + 1],
                                                           in1=cbuf[:, t // ST, t % ST, :], op0=ALU.max, op1=ALU.mult
                                                           ).then_inc(s_w, 1)
                    if H == 1:
                        dve.wait_ge(s_used, (i + 1) * per)
                        link(nc.vector.reciprocal(inv[:, 0, :], acc[:, 2, 0:CH]))
                        ins = nc.vector.tensor_tensor(y[:, :, :], acc[:, 0:KF, 0:CH], inv[:, 0:1, :].to_broadcast([P, KF, CH]), ALU.mult)
                        link(ins)
                    else:
                        for j in range(H):
                            o = 64 * (j % 2)
                            dve.wait_ge(s_used, i * per + (NT - 1) * H + j + 1)
                            link(nc.vector.reciprocal(inv[0:D, j, :], acc[o + D:o + 2 * D, j // 2, 0:CH]))
                            ins = nc.vector.tensor_tensor(y[D * (j % 4):D * (j % 4) + D, j // 4, :], acc[o:o + D, j // 2, 0:CH],
                                                          inv[0:D, j, :], ALU.mult)
                        link(ins)
                    for k in range(KF):
                        ins = nc.vector.tensor_scalar(y[:, k, :], y[:, k, :], bcol[:, k:k + 1], None, ALU.add)
                    link(ins)
                    nc.vector.tensor_scalar(ey[:, :, :], y[:, :, :], 0.0, None, ALU.min).then_inc(s_neg, 1)
                    dve.wait_ge(s_ey, i + 1)
                    link(nc.vector.scalar_tensor_tensor(out=y[:, :, :], in0=y[:, :, :], scalar=0.0, in1=ey[:, :, :],
                                                        op0=ALU.max, op1=ALU.add))
                    nc.vector.tensor_scalar(XT[:, :, bass.ds(i * CH, CH)], y[:, :, :], -1.0, None, ALU.add).then_inc(s_y, 1)
                    dve.wait_ge(s_y, i + 2)
                    assert link.n == NLINK
    core.stage_ends()


class Gat:

    def __init__(self, core, ctx, H):
        D = F // H
        self.rep = P if H == 1 else D
        self.wx = core.sb(ctx, "wx", [P, KF, F + H])
        self.wdb = core.sb(ctx, "w_dst_columns", [P, KF, H, P])
        self.msg = core.sb(ctx, "messages", [P, NT, H, D + self.rep])
        self.kap = core.sb(ctx, "kappa", [P, NT, H])
        self.bias = core.sb(ctx, "bias_k", [P, H])


def stage_back(core, s_name="back"):
    nc, XT, X, ident = core.nc, core.XT, core.X, core.ident
    with ExitStack() as ctx:
        flip = core.ps(ctx, "flip", [P, 8, 512])
        s_flip, s_add = core.sem("flipped"), core.sem("added")
        with nc.Block() as block:
            @block.tensor
            def _(pe):
                for t in range(NT):
                    if t >= 8:
                        pe.wait_ge(s_add, t - 7)
                    for k in range(KF):
                        ins = nc.tensor.transpose(flip[:, t % 8, k * P:(k + 1) * P], XT[:, k, t * P:(t + 1) * P], ident[:, :])
                    ins.then_inc(s_flip, 1)

            @block.vector
            def _(dve):
                for t in range(NT):
                    dve.wait_ge(s_flip, t + 1)
                    nc.vector.tensor_tensor(X[:, t, :], X[:, t, :], flip[:, t % 8, 0:F], ALU.add).then_inc(s_add, 1)
    core.stage_ends()


def stage_ones_off(core):
    nc, C = core.nc, core.C
    with ExitStack() as ctx:
        d = core.sb(ctx, "diagonal", [P, NT])
        s_in, s_sub, s_out = core.sem("diag_in"), core.sem("diag_less"), core.sem("diag_out")
        diag = bass.AP(C.tensor, 0, [[NP + 1, NP], [1, 1]]).rearrange("(p t) o -> p t o", p=P)
        with nc.Block() as block:
            @block.sync
            def _(sp):
                sp.dma_start(d[:, :].unsqueeze(2), diag, allow_slow_non_contiguous=True).then_inc(s_in, 16)
                sp.wait_ge(s_sub, 1)
                sp.dma_start(diag, d[:, :].unsqueeze(2), allow_slow_non_contiguous=True).then_inc(s_out, 16)
                sp.wait_ge(s_out, 16)

            @block.vector
            def _(dve):
                dve.wait_ge(s_in, 16)
                nc.vector.tensor_scalar(d[:, :], d[:, :], -1.0, None, ALU.add).then_inc(s_sub, 1)
    core.stage_ends()


def top_two(nc, link, L, E_, vals, ids, idf, iota, w, wf, hot, exp_pair):
    for t in range(NT):
        link(nc.vector.max(vals[:, t, :], L[:, t, :]))
        link(nc.vector.max_index(ids[:, t, :], vals[:, t, :], L[:, t, :]))
    link(nc.vector.tensor_copy(idf[:, :, :], ids[:, :, 0:2]))
    link(nc.vector.tensor_tensor(w[:, :, :], vals[:, :, 0:2], vals[:, :, 0:1].to_broadcast([P, NT, 2]), ALU.subtract))
    exp_pair(w)
    link(nc.vector.tensor_reduce(vals[:, :, 7], w[:, :, :], AX.X, ALU.add))
    link(nc.vector.reciprocal(vals[:, :, 6], vals[:, :, 7]))
    link(nc.vector.tensor_tensor(w[:, :, :], w[:, :, :], vals[:, :, 6:7].to_broadcast([P, NT, 2]), ALU.mult))
    for j in range(2):
        link(nc.vector.tensor_tensor(hot[:, j, :, :], iota[:, :].unsqueeze(1).to_broadcast([P, NT, E_]),
                                     idf[:, :, j:j + 1].to_broadcast([P, NT, E_]), ALU.is_equal))
        link(nc.vector.tensor_tensor(hot[:, j, :, :], hot[:, j, :, :], w[:, :, j:j + 1].to_broadcast([P, NT, E_]), ALU.mult))
    link(nc.vector.tensor_tensor(wf[:, :, :], hot[:, 0, :, :], hot[:, 1, :, :], ALU.add))


def stage_route(core, Wr, br, b2, wf, E_, softmax_first):
    nc, XT, X, ident = core.nc, core.XT, core.X, core.ident
    EL = 8
    with ExitStack() as ctx:
        wr = core.sb(ctx, "w_router", [P, KF, E_])
        brb = core.sb(ctx, "b_router", [P, E_])
        b2s = core.sb(ctx, "b_out", [E_, F])
        L = core.sb(ctx, "logits", [P, NT, EL])
        vals = core.sb(ctx, "vals", [P, NT, 8])
        ids = core.sb(ctx, "ids", [P, NT, 8], U32)
        idf = core.sb(ctx, "ids_f", [P, NT, 2])
        iota = core.sb(ctx, "iota", [P, E_])
        w = core.sb(ctx, "pair", [P, NT, 2])
        hot = core.sb(ctx, "hot", [P, 2, NT, E_])
        one = core.sb(ctx, "per_node", [P, 2, NT])
        wft = core.sb(ctx, "weights_t", [E_, NT, P])
        lg = core.ps(ctx, "logits_ps", [P, 512])
        tp = core.ps(ctx, "flip", [P, 7, 512])
        s_w, s_lg, s_dve, s_pair, s_e, s_iota, s_wf, s_tp, s_wft, s_bias, s_add = (core.sem(n) for n in (
            "w_in", "logits_made", "dve", "pair_made", "exp_made", "iota", "wf_made", "flipped", "wft_made", "bias_made", "added"))
        with nc.Block() as block:
            @block.sync
            def _(sp):
                sp.dma_start(wr[:, :, :], Wr.rearrange("(k p) e -> p k e", p=P)).then_inc(s_w, 16)
                sp.dma_start(brb[:, :], br.partition_broadcast(P)).then_inc(s_w, 16)
                sp.dma_start(b2s[:, :], b2).then_inc(s_w, 16)
                sp.wait_ge(s_w, 48)

            @block.gpsimd
            def _(pool):
                nc.gpsimd.iota(iota[:, :], pattern=[[1, E_]], base=0, channel_multiplier=0,
                               allow_small_or_imprecise_dtypes=True).then_inc(s_iota, 1)

            @block.tensor
            def _(pe):
                pe.wait_ge(s_w, 48)
                for t in range(NT):
                    for k in range(KF):
                        ins = nc.tensor.matmul(lg[:, t * E_:(t + 1) * E_], XT[:, k, t * P:(t + 1) * P], wr[:, k, :],
                                               start=(k == 0), stop=(k == KF - 1))
                ins.then_inc(s_lg, 1)
                pe.wait_ge(s_wf, 1)
                for t in range(NT):
                    ins = nc.tensor.transpose(tp[0:E_, t // 4, (t % 4) * P:(t % 4 + 1) * P], wf[:, t, :], ident[:, :])
                ins.then_inc(s_tp, 1)
                for t in range(NT):
                    pe.wait_ge(s_wft, 7)
                    if t >= 7:
                        pe.wait_ge(s_add, t - 6)
                    nc.tensor.matmul(tp[:, t % 7, 0:F], wft[:, t, :], b2s[:, :], start=True, stop=True).then_inc(s_bias, 1)

            @block.scalar
            def _(act):
                if softmax_first:
                    act.wait_ge(s_pair, 1)
                    nc.scalar.activation(L[:, :, 0:E_], L[:, :, 0:E_], ACT.Exp).then_inc(s_e, 1)
                act.wait_ge(s_pair, 1 + softmax_first)
                nc.scalar.activation(w[:, :, :], w[:, :, :], ACT.Exp).then_inc(s_e, 1)

            @block.vector
            def _(dve):
                link = Chain(dve, s_dve)
                if E_ < EL:
                    link(nc.vector.memset(L[:, :, E_:EL], -1e30))
                dve.wait_ge(s_lg, 1)
                dve.wait_ge(s_w, 48)
                dve.wait_ge(s_iota, 1)
                real = L[:, :, 0:E_]
                link(nc.vector.tensor_tensor(real, lg[:, 0:NT * E_].rearrange("p (t e) -> p t e", e=E_),
                                             brb[:, :].unsqueeze(1).to_broadcast([P, NT, E_]), ALU.add))
                if softmax_first:
                    link(nc.vector.tensor_reduce(one[:, 0, :], real, AX.X, ALU.max))
                    nc.vector.tensor_tensor(real, real, one[:, 0, :].unsqueeze(2).to_broadcast([P, NT, E_]), ALU.subtract
                                            ).then_inc(s_pair, 1)
                    dve.wait_ge(s_e, 1)
                    link(nc.vector.tensor_reduce(one[:, 0, :], real, AX.X, ALU.add))
                    link(nc.vector.reciprocal(one[:, 1, :], one[:, 0, :]))
                    link(nc.vector.tensor_tensor(real, real, one[:, 1, :].unsqueeze(2).to_broadcast([P, NT, E_]), ALU.mult))

                def exp_pair(w):
                    nc.vector.tensor_copy(one[:, 0, :], w[:, :, 0]).then_inc(s_pair, 1)
                    dve.wait_ge(s_e, 1 + softmax_first)

                top_two(nc, link, L, E_, vals, ids, idf, iota, w, wf, hot, exp_pair)
                nc.vector.tensor_copy(one[:, 0, :], wf[:, :, 0]).then_inc(s_wf, 1)
                dve.wait_ge(s_tp, 1)
                for b in range(7):
                    m = min(4, NT - 4 * b)
                    nc.vector.tensor_copy(wft[:, 4 * b:4 * b + m, :], tp[0:E_, b, 0:m * P].rearrange("e (t p) -> e t p", p=P)
                                          ).then_inc(s_wft, 1)
                for t in range(NT):
                    dve.wait_ge(s_bias, t + 1)
                    nc.vector.tensor_tensor(X[:, t, :], X[:, t, :], tp[:, t % 7, 0:F], ALU.add).then_inc(s_add, 1)
    core.stage_ends()


class Net:

    def __init__(self, layers, column=None):
        self.layers, self.column = layers, column


def stage_nets(core, nets, wf=None, out_bias=None):
    nc, XT, X = core.nc, core.XT, core.X
    with ExitStack() as ctx:
        tiles, nload = [], 0
        for net in nets:
            lay = []
            for W, b, fn in net.layers:
                K, M = W.shape
                kp = min(K, P)
                wt = core.sb(ctx, "w", [kp, K // kp, M])
                bt = core.sb(ctx, "b", [min(M, P), -(-M // P)]) if b is not None else None
                nload += 1 + (b is not None)
                lay.append((wt, bt, fn, K // kp, kp, M))
            tiles.append(lay)
        width = max(-(-l[5] // P) for t in tiles for l in t[:-1])
        depth = max(len(t) - 1 for t in tiles)
        hbuf = core.sb(ctx, "hidden", [P, 2, depth, width, TN])
        yc = core.sb(ctx, "y", [P, TC, F])
        wc = core.sb(ctx, "weights_chunk", [P, TC, 8])
        ob = core.sb(ctx, "out_bias", [P, F])
        up = core.ps(ctx, "up", [P, 4, 512])
        down = core.ps(ctx, "down", [P, 4, 512])
        s_w, s_up, s_act, s_down, s_y, s_dve, s_x = (core.sem(n) for n in (
            "w_in", "up_made", "hidden_made", "down_made", "y_added", "dve", "x_added"))
        if out_bias is not None:
            nload += 1
        ups = [(e, l, m, hf) for e, t in enumerate(tiles) for l in range(len(t) - 1)
               for m in range(-(-t[l][5] // P)) for hf in range(2)]
        NU, ND = len(ups), len(tiles) * TC
        last_of = {}
        for n, (e, l, m, hf) in enumerate(ups):
            last_of[(e, l)] = n
        with nc.Block() as block:
            @block.sync
            def _(sp):
                with nc.allow_non_contiguous_dma(reason="bias columns"):
                    for net, t in zip(nets, tiles):
                        for (W, b, _), (wt, bt, _, _, kp, M) in zip(net.layers, t):
                            sp.dma_start(wt[:, :, :], W.rearrange("(k p) m -> p k m", p=kp)).then_inc(s_w, 16)
                            if b is not None:
                                sp.dma_start(bt[:, :], b.rearrange("(k p) -> p k", p=min(M, P))).then_inc(s_w, 16)
                    if out_bias is not None:
                        sp.dma_start(ob[:, :], out_bias.partition_broadcast(P)).then_inc(s_w, 16)
                sp.wait_ge(s_w, 16 * nload)

            @block.tensor
            def _(pe):
                pe.wait_ge(s_w, 16 * nload)
                nc.tensor.sem_inc(s_down, 1)
                with pe.Fori(0, NTC) as i:
                    def up_step(n):
                        e, l, m, hf = ups[n]
                        wt, bt, fn, nk, kp, M = tiles[e][l]
                        mw = min(P, M - m * P)
                        if l:
                            pe.wait_ge(s_act, i * NU + last_of[(e, l - 1)] + 2)
                        if n >= 4:
                            pe.wait_ge(s_act, i * NU + n - 2)
                        else:
                            pe.wait_ge(s_act, i * NU + 1)
                        for k in range(nk):
                            rhs = (XT[:, k, bass.ds(i * TN + hf * TH, TH)] if l == 0 else
                                   hbuf[0:kp, e % 2, l - 1, k, hf * TH:(hf + 1) * TH])
                            ins = nc.tensor.matmul(up[0:mw, n % 4, 0:TH], wt[:, k, m * P:m * P + mw], rhs,
                                                   start=(k == 0), stop=(k == nk - 1))
                        ins.then_inc(s_up, 1)

                    def down_step(e):
                        wt, _, _, nk, kp, _ = tiles[e][-1]
                        pe.wait_ge(s_act, i * NU + last_of[(e, len(tiles[e]) - 2)] + 2)
                        for j in range(TC):
                            n = e * TC + j
                            if n >= 4:
                                pe.wait_ge(s_y, i * ND + n - 2)
                            else:
                                pe.wait_ge(s_y, i * ND + 1)
                            for k in range(nk):
                                ins = nc.tensor.matmul(down[:, n % 4, 0:F],
                                                       hbuf[0:kp, e % 2, len(tiles[e]) - 2, k, j * P:(j + 1) * P], wt[:, k, :],
                                                       start=(k == 0), stop=(k == nk - 1))
                            ins.then_inc(s_down, 1)

                    for e in range(len(tiles)):
                        for n, u in enumerate(ups):
                            if u[0] == e:
                                up_step(n)
                        if e:
                            down_step(e - 1)
                    down_step(len(tiles) - 1)

            @block.scalar
            def _(act):
                act.wait_ge(s_w, 16 * nload)
                nc.scalar.sem_inc(s_act, 1)
                with act.Fori(0, NTC) as i:
                    for n, (e, l, m, hf) in enumerate(ups):
                        _, bt, fn, _, _, M = tiles[e][l]
                        mw = min(P, M - m * P)
                        act.wait_ge(s_up, i * NU + n + 1)
                        if e >= 2:
                            act.wait_ge(s_down, i * ND + (e - 1) * TC + 1)
                        else:
                            act.wait_ge(s_down, i * ND + 1)
                        nc.scalar.activation(hbuf[0:mw, e % 2, l, m, hf * TH:(hf + 1) * TH], up[0:mw, n % 4, 0:TH], fn,
                                             bias=bt[0:mw, m:m + 1]).then_inc(s_act, 1)

            @block.vector
            def _(dve):
                link = Chain(dve, s_dve)
                dve.wait_ge(s_w, 16 * nload)
                nc.vector.sem_inc(s_y, 1)
                nc.vector.sem_inc(s_x, 1)
                with dve.Fori(0, NTC) as i:
                    NLINK = 1
                    link.n, link.base = 0, i * NLINK
                    dve.wait_ge(s_x, i + 1)
                    if wf is not None:
                        link(nc.vector.tensor_copy(wc[:, :, 0:wf.shape[2]], wf[:, bass.ds(i * TC, TC), :]))
                    for e, net in enumerate(nets):
                        if e:
                            dve.wait_ge(s_y, i * ND + e * TC + 1)
                        for j in range(TC):
                            n = e * TC + j
                            dve.wait_ge(s_down, i * ND + n + 2)
                            o, y = down[:, n % 4, 0:F], yc[:, j, :]
                            if net.column is None and e == 0 and out_bias is not None:
                                ins = nc.vector.tensor_tensor(y, o, ob[:, :], ALU.add)
                            elif e == 0:
                                ins = nc.vector.tensor_scalar(y, o, wc[:, j, net.column:net.column + 1], None, ALU.mult)
                            else:
                                ins = nc.vector.scalar_tensor_tensor(out=y, in0=o, scalar=wc[:, j, net.column:net.column + 1],
                                                                     in1=y, op0=ALU.mult, op1=ALU.add)
                            ins.then_inc(s_y, 1)
                    dve.wait_ge(s_y, (i + 1) * ND + 1)
                    nc.vector.tensor_tensor(X[:, bass.ds(i * TC, TC), :], X[:, bass.ds(i * TC, TC), :], yc[:, :, :], ALU.add
                                            ).then_inc(s_x, 1)
    core.stage_ends()


def stage_qkv(core, a, kT, msg):
    nc, XT = core.nc, core.XT
    HD, H = 32, 8
    with ExitStack() as ctx:
        w = core.sb(ctx, "w_qkv", [P, 3, KF, F])
        bqk = core.sb(ctx, "b_qk", [P, 2, KF])
        bv = core.sb(ctx, "b_v", [P, F])
        ps = core.ps(ctx, "proj", [P, 8, 512])
        s_w, s_ps = core.sem("w_in"), core.sem("projected")
        s_out = [core.sem("evacuated_by_scalar"), core.sem("evacuated_by_vector")]
        s_one = core.sem("ones_made")
        jobs = ([(1, m, c) for m in range(KF) for c in range(NCH)] + [(2, t, 0) for t in range(NT)]
                + [(0, m, c) for c in range(NCH) for m in range(KF)])
        with nc.Block() as block:
            @block.sync
            def _(sp):
                with nc.allow_non_contiguous_dma(reason="bias columns"):
                    for o, n in enumerate("qkv"):
                        sp.dma_start(w[:, o, :, :], a["L1_gnn_W" + n].rearrange("(k p) m -> p k m", p=P)).then_inc(s_w, 16)
                    for o, n in enumerate("qk"):
                        sp.dma_start(bqk[:, o, :], a["L1_gnn_b" + n].rearrange("(k p) -> p k", p=P)).then_inc(s_w, 16)
                sp.dma_start(bv[:, :], a["L1_gnn_bv"].partition_broadcast(P)).then_inc(s_w, 16)
                sp.wait_ge(s_w, 96)

            @block.gpsimd
            def _(pool):
                nc.gpsimd.memset(msg[:, :, :, HD:2 * HD], 1.0).then_inc(s_one, 1)

            @block.tensor
            def _(pe):
                pe.wait_ge(s_w, 96)
                for n, (o, m, c) in enumerate(jobs):
                    if n >= 8:
                        v = jobs[n - 8][0] == 2
                        pe.wait_ge(s_out[v], sum((x[0] == 2) == v for x in jobs[:n - 7]))
                    for k in range(KF):
                        if o < 2:
                            ins = nc.tensor.matmul(ps[:, n % 8, 0:CH], w[:, o, k, m * P:(m + 1) * P], XT[:, k, c * CH:(c + 1) * CH],
                                                   start=(k == 0), stop=(k == KF - 1))
                        else:
                            ins = nc.tensor.matmul(ps[:, n % 8, 0:F], XT[:, k, m * P:(m + 1) * P], w[:, 2, k, :],
                                                   start=(k == 0), stop=(k == KF - 1))
                    ins.then_inc(s_ps, 1)

            @block.scalar
            def _(act):
                act.wait_ge(s_w, 96)
                for n, (o, m, c) in enumerate(jobs):
                    if o < 2:
                        act.wait_ge(s_ps, n + 1 + (o == 0 and m == 0))
                        nc.scalar.activation((XT, kT)[o][:, m, c * CH:(c + 1) * CH], ps[:, n % 8, 0:CH], ACT.Identity,
                                             bias=bqk[:, o, m:m + 1]).then_inc(s_out[0], 1)

            @block.vector
            def _(dve):
                dve.wait_ge(s_w, 96)
                for n, (o, m, c) in enumerate(jobs):
                    if o == 2:
                        dve.wait_ge(s_ps, n + 1)
                        nc.vector.tensor_tensor(msg[:, m, :, 0:HD], ps[:, n % 8, 0:F].rearrange("p (h d) -> p h d", h=H),
                                                bv[:, :].rearrange("p (h d) -> p h d", h=H), ALU.add).then_inc(s_out[1], 1)
    core.stage_ends()


SCORE_HI = 22026.465794806718
SCORE_LO = 4.5399929762484854e-05


def stage_attention(core, kT, msg):
    nc, XT = core.nc, core.XT
    D, H = 32, 8
    WR, LAG = 8, 3
    per = NT * H
    with ExitStack() as ctx:
        cbuf = core.sb(ctx, "counts", [P, NL, ST, CH])
        qc = core.sb(ctx, "q_chunk", [P, KF, CH])
        ex = core.sb(ctx, "exps", [P, 4, CH])
        cl = core.sb(ctx, "clipped", [P, 4, CH])
        w = core.sb(ctx, "weights", [P, WR, CH])
        inv = core.sb(ctx, "inv", [P, 8, CH])
        acc = core.ps(ctx, "acc", [P, 4, 512])
        sc = core.ps(ctx, "scores", [P, 4, 512])
        s_c = [core.sem("counts_in") for _ in range(NL)]
        s_q, s_sc, s_ex, s_cl, s_w, s_used, s_dve, s_y = (core.sem(n) for n in (
            "q_chunk", "scores_made", "exp_made", "clipped", "w_made", "w_used", "dve", "y_done"))
        with nc.Block() as block:
            @block.sync
            def _(sp):
                load_counts(core, sp, cbuf, s_c, s_w, per)

            @block.tensor
            def _(pe):
                nc.tensor.sem_inc(s_sc, 1)
                with pe.Fori(0, NCH) as i:
                    pe.wait_ge(s_q, i + 1)
                    pe.wait_ge(s_y, i + 1)
                    for n in range(per + LAG):
                        if n < per:
                            t, j = n // H, n % H
                            if n >= 4:
                                pe.wait_ge(s_ex, i * per + n - 3)
                            nc.tensor.matmul(sc[:, n % 4, 0:CH], kT[D * (j % 4):D * (j % 4) + D, j // 4, t * P:(t + 1) * P],
                                             qc[D * (j % 4):D * (j % 4) + D, j // 4, :], start=True, stop=True).then_inc(s_sc, 1)
                        if n >= LAG:
                            m = n - LAG
                            t, j = m // H, m % H
                            o = 64 * (j % 2)
                            pe.wait_ge(s_w, i * per + m + 2)
                            nc.tensor.matmul(acc[o:o + 64, j // 2, 0:CH], msg[:, t, j, :], w[:, m % WR, :],
                                             start=(t == 0), stop=(t == NT - 1)).then_inc(s_used, 1)

            @block.scalar
            def _(act):
                with act.Fori(0, NCH) as i:
                    act.wait_ge(s_sc, i * per + 1)
                    nc.scalar.copy(qc[:, :, :], XT[:, :, bass.ds(i * CH, CH)]).then_inc(s_q, 1)
                    for n in range(per):
                        act.wait_ge(s_sc, i * per + n + 2)
                        if n >= 4:
                            act.wait_ge(s_cl, i * per + n - 2)
                        else:
                            act.wait_ge(s_cl, i * per + 1)
                        nc.scalar.activation(ex[:, n % 4, :], sc[:, n % 4, 0:CH], ACT.Exp, scale=D ** -0.5).then_inc(s_ex, 1)

            @block.vector
            def _(dve):
                link = Chain(dve, s_dve)
                for s in (s_cl, s_w, s_y):
                    nc.vector.sem_inc(s, 1)
                with dve.Fori(0, NCH) as i:
                    NLINK = H + 1
                    link.n, link.base = 0, i * NLINK
                    dve.wait_ge(s_w, i * per + 1)
                    for n in range(per + 1):
                        if n < per:
                            dve.wait_ge(s_ex, i * per + n + 1)
                            if n >= 4:
                                dve.wait_ge(s_w, i * per + n - 2)
                            nc.vector.tensor_scalar(cl[:, n % 4, :], ex[:, n % 4, :], SCORE_HI, SCORE_LO, ALU.min, ALU.max
                                                    ).then_inc(s_cl, 1)
                        if n:
                            m = n - 1
                            t = m // H
                            if m % (H * ST) == 0:
                                dve.wait_ge(s_c[t // ST], (i + 1) * 16)
                            dve.wait_ge(s_cl, i * per + m + 2)
                            if m >= WR:
                                dve.wait_ge(s_used, i * per + m - WR + 1)
                            nc.vector.tensor_tensor(w[:, m % WR, :], cl[:, m % 4, :], cbuf[:, t // ST, t % ST, :], ALU.mult
                                                    ).then_inc(s_w, 1)
                    for j in range(H):
                        o = 64 * (j % 2)
                        dve.wait_ge(s_used, i * per + (NT - 1) * H + j + 1)
                        link(nc.vector.tensor_scalar(inv[0:D, j, :], acc[o + D:o + 2 * D, j // 2, 0:CH], 1e-20, None, ALU.max))
                    link(nc.vector.reciprocal(inv[0:D, :, :], inv[0:D, :, :]))
                    for j in range(H):
                        o = 64 * (j % 2)
                        ins = nc.vector.tensor_tensor(XT[D * (j % 4):D * (j % 4) + D, j // 4, bass.ds(i * CH, CH)],
                                                      acc[o:o + D, j // 2, 0:CH], inv[0:D, j, :], ALU.mult)
                    ins.then_inc(s_y, 1)
                    dve.wait_ge(s_y, i + 2)
    core.stage_ends()


def stage_out_proj(core, a, T, parked):
    nc, XT, X = core.nc, core.XT, core.X
    with ExitStack() as ctx:
        w = core.sb(ctx, "w_p", [P, KF, F])
        bp = core.sb(ctx, "b_p", [P, F])
        ps = core.ps(ctx, "proj", [P, 8, 512])
        s_w, s_ps, s_add, s_dve = core.sem("w_in"), core.sem("projected"), core.sem("added"), core.sem("dve")
        with nc.Block() as block:
            @block.sync
            def _(sp):
                sp.dma_start(w[:, :, :], a["L1_gnn_Wp"].rearrange("(k p) m -> p k m", p=P)).then_inc(s_w, 16)
                sp.dma_start(bp[:, :], a["L1_gnn_bp"].partition_broadcast(P)).then_inc(s_w, 16)
                sp.dma_start(T[:, :, :], parked).then_inc(s_w, 16)
                sp.wait_ge(s_w, 48)

            @block.tensor
            def _(pe):
                pe.wait_ge(s_w, 48)
                for t in range(NT):
                    if t >= 8:
                        pe.wait_ge(s_add, t - 7)
                    for k in range(KF):
                        ins = nc.tensor.matmul(ps[:, t % 8, 0:F], XT[:, k, t * P:(t + 1) * P], w[:, k, :],
                                               start=(k == 0), stop=(k == KF - 1))
                    ins.then_inc(s_ps, 1)

            @block.vector
            def _(dve):
                link = Chain(dve, s_dve)
                dve.wait_ge(s_w, 48)
                link(nc.vector.tensor_tensor(T[:, :, :], T[:, :, :], bp[:, :].unsqueeze(1).to_broadcast([P, NT, F]), ALU.add))
                for t in range(NT):
                    dve.wait_ge(s_ps, t + 1)
                    nc.vector.tensor_tensor(T[:, t, :], T[:, t, :], ps[:, t % 8, 0:F], ALU.add).then_inc(s_add, 1)
                dve.wait_ge(s_add, NT)
                link(nc.vector.tensor_tensor(X[:, :, :], X[:, :, :], T[:, :, :], ALU.add))
    core.stage_ends()


def rest(core, a, stop):
    stage_ones_off(core)
    NE0, NE1 = a["L0_ffn_W1"].shape[0], a["L1_ffn_eW1"].shape[0]
    with ExitStack() as c:
        wf = core.sb(c, "expert_weights", [P, NT, NE0])
        with ExitStack() as c2:
            T = core.sb(c2, "t", [P, NT, F])
            stage_norm(core, core.X, T, a["L0_ffn_gamma"], a["L0_ffn_beta"], times=2)
        stage_route(core, a["L0_ffn_Wr"], a["L0_ffn_br"], a["L0_ffn_b2"], wf, NE0, 0)
        stage_nets(core, [Net([(a["L0_ffn_W1"][e], a["L0_ffn_b1"][e], ACT.Gelu), (a["L0_ffn_W2"][e], None, None)], e)
                          for e in range(NE0)], wf)
    if stop == "moe":
        return
    parked = core.nc.dram_tensor("parked", (P, NT, F), F32, kind="Internal").ap()
    with ExitStack() as c:
        T = core.sb(c, "t", [P, NT, F])
        stage_norm(core, core.X, T, park=parked)
    with ExitStack() as c:
        kT = core.sb(c, "kt", [P, KF, NP])
        msg = core.sb(c, "values", [P, NT, 8, 64])
        stage_qkv(core, a, kT, msg)
        stage_attention(core, kT, msg)
    with ExitStack() as c:
        T = core.sb(c, "t", [P, NT, F])
        stage_out_proj(core, a, T, parked)
        stage_norm(core, T, T, a["L1_gnn_ln_g"], a["L1_gnn_ln_b"])
    stage_nets(core, [Net([(a["L1_gnn_W1"], a["L1_gnn_b1"], ACT.Gelu), (a["L1_gnn_W2"], None, None)])],
               out_bias=a["L1_gnn_b2"])
    if stop == "attn":
        return
    with ExitStack() as c:
        wf = core.sb(c, "expert_weights", [P, NT, NE1])
        with ExitStack() as c2:
            T = core.sb(c2, "t", [P, NT, F])
            stage_norm(core, core.X, T)
        stage_route(core, a["L1_ffn_gW"], a["L1_ffn_gb"], a["L1_ffn_eb3"], wf, NE1, 1)
        shared = Net([(a["L1_ffn_sW1"], a["L1_ffn_sb1"], ACT.Relu), (a["L1_ffn_sW2"], a["L1_ffn_sb2"], ACT.Relu),
                      (a["L1_ffn_sW3"], None, None)])
        stage_nets(core, [shared] + [Net([(a["L1_ffn_eW1"][e], a["L1_ffn_eb1"][e], ACT.Relu),
                                          (a["L1_ffn_eW2"][e], a["L1_ffn_eb2"][e], ACT.Relu),
                                          (a["L1_ffn_eW3"][e], None, None)], e) for e in range(NE1)],
                   wf, out_bias=a["L1_ffn_sb3"])


_HOST_T = ("L1_gnn_Wq", "L1_gnn_Wk", "L1_gnn_Wv", "L1_gnn_Wp", "L1_gnn_W1", "L1_gnn_W2")


def stage_store(core, out):
    nc, X = core.nc, core.X
    s_out = core.sem("stored")
    with nc.Block() as block:
        @block.sync
        def _(sp):
            sp.dma_start(out[0:(NT - 1) * P, :].rearrange("(t p) f -> p t f", p=P), X[:, 0:NT - 1, :]).then_inc(s_out, 16)
            sp.dma_start(out[(NT - 1) * P:N, :], X[0:LAST, NT - 1, :]).then_inc(s_out, 16)
            sp.wait_ge(s_out, 32)
    core.stage_ends()


def program(nc, a, out, stop="all"):
    with ExitStack() as ctx:
        core = Core(nc, ctx)
        core.X = core.sb(ctx, "x", [P, NT, F])
        core.XT = core.sb(ctx, "xt", [P, KF, NP])
        core.ident = core.sb(ctx, "identity", [P, P])
        core.ones = core.sb(ctx, "ones", [P, P])
        core.C = nc.dram_tensor("edge_counts", (CELLS + EG * EP + EJ, 1), F32, kind="Internal").ap()
        stage_load(core, a["x"])
        stage_edges(core, a["src"], a["dst"])
        with ExitStack() as c2:
            T = core.sb(c2, "t", [P, NT, F])
            stage_norm(core, core.X, T)
        for layer, H in (("1", F // 32), ("2", 1)):
            with ExitStack() as c2:
                g = Gat(core, c2, H)
                stage_gat_weights(core, g, a["L0_gnn_W" + layer], a["L0_gnn_a_src" + layer], a["L0_gnn_a_dst" + layer], H)
                stage_gat_aggregate(core, g, a["L0_gnn_b" + layer], H)
        stage_back(core)
        if stop != "gat":
            rest(core, a, stop)
        stage_store(core, out)


def kernel(**inputs):
    import numpy as _np
    import concourse.bacc as _bacc
    from concourse import mybir as _mybir
    from concourse.bass_utils import run_bass_kernel_spmd as _run

    nc = _bacc.Bacc("TRN2", target_bir_lowering=False, num_devices=1)
    arrays, args = {}, {}
    for name in inputs:
        v = _np.asarray(inputs[name])
        v = _np.ascontiguousarray(v.T if name in _HOST_T else v)
        arrays[f"in_{name}_dram"] = v
        args[name] = nc.dram_tensor(f"in_{name}_dram", v.shape, _mybir.dt.from_np(v.dtype), kind="ExternalInput").ap()
    out = nc.dram_tensor("out_0_dram", (N, F), _mybir.dt.float32, kind="ExternalOutput").ap()
    program(nc, args, out)
    return _run(nc, [arrays], core_ids=[0]).results[0]["out_0_dram"]
```

```python
from contextlib import ExitStack

import concourse.bass as bass
from concourse import mybir

P = 128
N = 3125
NT = -(-N // P)
NP = NT * P
LAST = N - (NT - 1) * P
F = 256
KF = F // P
E = 100000
EP = 125
EJ = E // EP
EG = 4
CELLS = NP * NP
CH = 400
NCH = NP // CH
ST = 5
NL = NT // ST
TC = 5
TN = TC * P
TH = TN // 2
NTC = NT // TC
EPS = 1e-5
DUP = 4096.0

F32 = mybir.dt.float32
U32 = mybir.dt.uint32
BF16 = mybir.dt.bfloat16
ALU = mybir.AluOpType
ACT = mybir.ActivationFunctionType
AX = mybir.AxisListType
RMAX = bass.bass_isa.ReduceOp.max


class Chain:

    def __init__(self, eng, sem):
        self.eng, self.sem, self.n, self.base = eng, sem, 0, 0

    def __call__(self, ins):
        ins.then_inc(self.sem, 1)
        self.n += 1
        self.eng.wait_ge(self.sem, self.base + self.n)


class Core:

    def __init__(self, nc, ctx):
        self.nc, self.ctx, self.count, self.used = nc, ctx, 0, []

    def lasting_sem(self, name):
        self.count += 1
        return self.nc.alloc_semaphore(name=f"{name}_{self.count}")

    def sem(self, name):
        self.count += 1
        self.used.append(self.nc.alloc_semaphore(name=f"{name}_{self.count}"))
        return self.used[-1]

    def stage_ends(self):
        for s in self.used:
            self.nc.gpsimd.sem_clear(s)
            self.nc.release_semaphore(s)
        self.used = []

    def sb(self, ctx, name, shape, dt=F32):
        self.count += 1
        return ctx.enter_context(self.nc.sbuf_tensor(f"{name}_{self.count}", shape, dt))

    def ps(self, ctx, name, shape, dt=F32):
        self.count += 1
        return ctx.enter_context(self.nc.psum_tensor(f"{name}_{self.count}", shape, dt))


def stage_load(core, x_in):
    nc = core.nc
    X, ident, onescol, C = core.X, core.ident, core.ones, core.C
    with ExitStack() as ctx:
        zero = core.sb(ctx, "zero", [P, NP])
        s_zero, s_xpad, s_x, s_clear, s_diag, s_id = (core.sem(n) for n in (
            "zero_made", "x_pad_cleared", "x_in", "c_cleared", "diag_set", "ident"))
        c_rows = C[0:CELLS, 0:1].rearrange("(t p d) o -> t p (d o)", p=P, d=NP)
        with nc.Block() as block:
            @block.sync
            def _(sp):
                sp.wait_ge(s_xpad, 1)
                sp.dma_start(X[:, 0:NT - 1, :], x_in[0:(NT - 1) * P, :].rearrange("(t p) f -> p t f", p=P)).then_inc(s_x, 16)
                sp.dma_start(X[0:LAST, NT - 1, :], x_in[(NT - 1) * P:N, :]).then_inc(s_x, 16)
                sp.wait_ge(s_zero, 1)
                for t in range(NT):
                    sp.dma_start(c_rows[t], zero[:, :]).then_inc(s_clear, 16)
                sp.wait_ge(s_clear, 16 * NT)
                diag = bass.AP(C.tensor, 0, [[NP + 1, NP], [1, 1]])
                sp.dma_start(diag.rearrange("(p t) o -> p t o", p=P), onescol[:, 0:NT].unsqueeze(2),
                             allow_slow_non_contiguous=True).then_inc(s_diag, 16)
                sp.wait_ge(s_diag, 16)
                sp.wait_ge(s_x, 32)

            @block.vector
            def _(dve):
                nc.vector.memset(X[:, NT - 1, :], 0.0).then_inc(s_xpad, 1)
                nc.vector.memset(onescol[:, :], 1.0)
                nc.vector.memset(core.XT[:, :, NP:NP + CH], 0.0)
                nc.vector.memset(zero[:, :], 0.0).then_inc(s_zero, 1)

            @block.gpsimd
            def _(pool):
                nc.gpsimd.memset(ident[:, :], 0.0).then_inc(s_id, 1)
                pool.wait_ge(s_id, 1)
                nc.gpsimd.affine_select(out=ident[:, :], in_=ident[:, :], compare_op=ALU.not_equal, fill=1.0,
                                        base=0, pattern=[[-1, P]], channel_multiplier=1).then_inc(s_id, 1)
    core.stage_ends()


def stage_edges(core, src, dst):
    nc = core.nc
    ident, onesm, C = core.ident, core.ones, core.C
    R = 2
    GN = EJ // EG
    W = EG * EP
    with ExitStack() as ctx:
        ei = core.sb(ctx, "edge_ids", [EP, 2, EJ], mybir.dt.int32)
        ef = core.sb(ctx, "edge_ids_f", [EP, 2, EJ])
        cell = core.sb(ctx, "cell", [EP, EJ + EG])
        spare = core.sb(ctx, "spare", [EP, EG])
        rank = core.sb(ctx, "rank", [EP, EG, W])
        diag = core.sb(ctx, "diag", [EP, R, W])
        same = core.sb(ctx, "same", [EP, EG, W])
        here = core.sb(ctx, "here", [EP, R, EG])
        cnt = core.sb(ctx, "cnt", [EP, R, EG])
        away = core.sb(ctx, "away", [EP, EG])
        idx = core.sb(ctx, "idx", [EP, R, EG], U32)
        rows = core.ps(ctx, "rows", [EP, R, W // 500, 512])
        s_spare, s_cell, s_rank, s_dve, s_first = (core.sem(n) for n in (
            "spare_made", "cells_made", "rank_made", "dve", "first_cells"))
        s_here, s_diag, s_rows, s_idx = ([core.sem(n) for _ in range(R)] for n in (
            "here_made", "diag_made", "rows_made", "idx_made"))
        s_scat = [core.lasting_sem("scattered") for _ in range(R)]
        with nc.Block() as block:
            @block.gpsimd
            def _(pool):
                for r, e in enumerate((src, dst)):
                    pool.dma_start(ei[:, r, :], e.rearrange("(p j) -> p j", p=EP)).then_inc(s_scat[r], 16)
                nc.gpsimd.iota(spare[:, :], pattern=[[EP, EG]], base=CELLS, channel_multiplier=1,
                               allow_small_or_imprecise_dtypes=True).then_inc(s_spare, 1)
                nc.gpsimd.memset(rank[:, :, :], 1.0).then_inc(s_rank, 1)
                pool.wait_ge(s_rank, 1)
                nc.gpsimd.affine_select(out=rank[:, :, :], in_=rank[:, :, :], compare_op=ALU.is_ge, fill=DUP,
                                        base=0, pattern=[[-EP, EG], [1, W]], channel_multiplier=-1).then_inc(s_rank, 1)
                with pool.Fori(0, GN // R) as i:
                    for r in range(R):
                        pool.wait_ge(s_idx[r], i + 2)
                        pool.wait_ge(s_scat[r - 1], (i + (r > 0)) * (16 * EG) + 16)
                        bound = pool.snap(i + (CELLS + W - 1 + r))
                        for g in range(EG):
                            nc.gpsimd.indirect_dma_start(
                                out=C[:, :], out_offset=bass.IndirectOffsetOnAxis(idx[:, r, g:g + 1], 0),
                                in_=cnt[:, r, g:g + 1], in_offset=None, bounds_check=bound,
                                compute_op=ALU.add).then_inc(s_scat[r], 16)
                for r in range(R):
                    pool.wait_ge(s_scat[r], GN // R * 16 * EG + 16)

            @block.scalar
            def _(act):
                with act.Fori(0, GN // R) as i:
                    for r in range(R):
                        act.wait_ge(s_here[r], i + 1)
                        act.wait_ge(s_rows[r], i + 1)
                        for g in range(EG):
                            ins = nc.scalar.activation(diag[:, r, g * EP:(g + 1) * EP], ident[0:EP, 0:EP], ACT.Copy,
                                                       scale=here[:, r, g:g + 1])
                        ins.then_inc(s_diag[r], 1)

            @block.tensor
            def _(pe):
                for r in range(R):
                    nc.tensor.sem_inc(s_rows[r], 1)
                with pe.Fori(0, GN // R) as i:
                    for r in range(R):
                        pe.wait_ge(s_diag[r], i + 1)
                        pe.wait_ge(s_idx[r], i + 1)
                        for b in range(0, W, 500):
                            ins = nc.tensor.matmul(rows[:, r, b // 500, 0:500], onesm[0:EP, 0:EP], diag[:, r, b:b + 500],
                                                   start=True, stop=True)
                        ins.then_inc(s_rows[r], 1)

            @block.vector
            def _(dve):
                link = Chain(dve, s_dve)
                for r in range(R):
                    nc.vector.sem_inc(s_idx[r], 1)
                    dve.wait_ge(s_scat[r], 16)
                link(nc.vector.tensor_copy(ef[:, :, :], ei[:, :, :]))
                nc.vector.memset(cell[:, EJ:EJ + EG], 0.0).then_inc(s_cell, 1)
                nc.vector.scalar_tensor_tensor(out=cell[:, 0:EJ], in0=ef[:, 0, :], scalar=float(NP), in1=ef[:, 1, :],
                                               op0=ALU.mult, op1=ALU.add).then_inc(s_cell, 1)
                dve.wait_ge(s_cell, 2)
                dve.wait_ge(s_rank, 2)
                dve.wait_ge(s_spare, 1)
                nc.vector.tensor_copy(here[:, 0, :], cell[:, 0:EG]).then_inc(s_here[0], 1)
                with dve.Fori(0, GN // R) as i:
                    link.n, link.base = 0, i * (R * 3) + 1
                    for r in range(R):
                        q = (r + 1) % R
                        dve.wait_ge(s_idx[q], i + 1 + (q == 0))
                        nc.vector.tensor_copy(here[:, q, :], cell[:, bass.ds((i * R + r + 1) * EG, EG)]).then_inc(s_here[q], 1)
                        dve.wait_ge(s_here[r], i + 1)
                        dve.wait_ge(s_rows[r], i + 2)
                        dve.wait_ge(s_scat[r], i * (16 * EG) + 16)
                        for g in range(EG):
                            ins = nc.vector.scalar_tensor_tensor(
                                out=same[:, g, :].rearrange("p (b w) -> p b w", w=500), in0=rows[:, r, :, 0:500], scalar=here[:, r, g:g + 1],
                                in1=rank[:, g, :].rearrange("p (b w) -> p b w", w=500),
                                op0=ALU.is_equal, op1=ALU.mult, accum_out=cnt[:, r, g:g + 1])
                        link(ins)
                        link(nc.vector.tensor_tensor(away[:, :], spare[:, :], here[:, r, :], ALU.subtract))
                        link(nc.vector.scalar_tensor_tensor(out=away[:, :], in0=cnt[:, r, :], scalar=DUP, in1=away[:, :],
                                                            op0=ALU.is_ge, op1=ALU.mult))
                        nc.vector.tensor_tensor(idx[:, r, :], away[:, :], here[:, r, :], ALU.add).then_inc(s_idx[r], 1)
    core.stage_ends()


def stage_norm(core, src, dst, gamma=None, beta=None, times=1, park=None):
    nc, XT, ident = core.nc, core.XT, core.ident
    with ExitStack() as ctx:
        tmp = core.sb(ctx, "squares", [P, NT, F])
        mean = core.sb(ctx, "mean", [P, NT])
        var = core.sb(ctx, "var", [P, NT])
        std = core.sb(ctx, "std", [P, NT])
        gb = core.sb(ctx, "gamma_beta", [P, 2, F])
        flip = core.ps(ctx, "flip", [P, 8, 512])
        s_gb, s_dve, s_var, s_std, s_flip = (core.sem(n) for n in (
            "gamma_in", "dve", "var_made", "std_made", "flipped"))
        s_evac = [core.sem("evacuated_by_vector"), core.sem("evacuated_by_scalar")]
        s_norm, s_park = core.sem("norm_made"), core.sem("parked")
        turns = [(k, t0, min(4, NT - t0)) for k in range(KF) for t0 in range(0, NT, 4)]
        with nc.Block() as block:
            @block.sync
            def _(sp):
                if gamma is not None:
                    for k, row in enumerate((gamma, beta)):
                        sp.dma_start(gb[:, k, :], row.partition_broadcast(P)).then_inc(s_gb, 16)
                    sp.wait_ge(s_gb, 32)
                if park is not None:
                    sp.wait_ge(s_norm, 1)
                    sp.dma_start(park[0], dst[:, :, :]).then_inc(s_park, 16)
                    sp.dma_start(park[1], src[:, :, :]).then_inc(s_park, 16)
                    sp.wait_ge(s_park, 32)

            @block.vector
            def _(dve):
                link = Chain(dve, s_dve)
                a = src
                for n in range(times):
                    link(nc.vector.tensor_reduce(mean[:, :], a[:, :, :], AX.X, ALU.add))
                    link(nc.vector.tensor_scalar(mean[:, :], mean[:, :], -1.0 / F, None, ALU.mult))
                    link(nc.vector.tensor_tensor(dst[:, :, :], a[:, :, :], mean[:, :].unsqueeze(2).to_broadcast([P, NT, F]), ALU.add))
                    link(nc.vector.tensor_tensor(tmp[:, :, :], dst[:, :, :], dst[:, :, :], ALU.mult))
                    link(nc.vector.tensor_reduce(var[:, :], tmp[:, :, :], AX.X, ALU.add))
                    nc.vector.tensor_scalar(var[:, :], var[:, :], 1.0 / F, EPS, ALU.mult, ALU.add).then_inc(s_var, 1)
                    dve.wait_ge(s_std, n + 1)
                    link(nc.vector.reciprocal(std[:, :], std[:, :]))
                    link(nc.vector.tensor_tensor(dst[:, :, :], dst[:, :, :], std[:, :].unsqueeze(2).to_broadcast([P, NT, F]), ALU.mult))
                    a = dst
                if gamma is not None:
                    dve.wait_ge(s_gb, 32)
                    link(nc.vector.tensor_tensor(dst[:, :, :], dst[:, :, :], gb[:, 0:1, :].to_broadcast([P, NT, F]), ALU.mult))
                    link(nc.vector.tensor_tensor(dst[:, :, :], dst[:, :, :], gb[:, 1:2, :].to_broadcast([P, NT, F]), ALU.add))
                nc.vector.tensor_copy(mean[:, 0:1], dst[:, 0, 0:1]).then_inc(s_norm, 1)
                for n, (k, t0, m) in enumerate(turns):
                    if n % 2 == 0:
                        dve.wait_ge(s_flip, n + 1)
                        nc.vector.tensor_copy(XT[:, k, t0 * P:(t0 + m) * P], flip[:, n % 8, 0:m * P]).then_inc(s_evac[n % 2], 1)

            @block.scalar
            def _(act):
                for n in range(times):
                    act.wait_ge(s_var, n + 1)
                    nc.scalar.activation(std[:, :], var[:, :], ACT.Sqrt).then_inc(s_std, 1)
                for n, (k, t0, m) in enumerate(turns):
                    if n % 2:
                        act.wait_ge(s_flip, n + 1)
                        nc.scalar.copy(XT[:, k, t0 * P:(t0 + m) * P], flip[:, n % 8, 0:m * P]).then_inc(s_evac[n % 2], 1)

            @block.tensor
            def _(pe):
                pe.wait_ge(s_norm, 1)
                for n, (k, t0, m) in enumerate(turns):
                    if n >= 8:
                        pe.wait_ge(s_evac[n % 2], (n - 8) // 2 + 1)
                    for j in range(m):
                        ins = nc.tensor.transpose(flip[:, n % 8, j * P:(j + 1) * P], dst[:, t0 + j, k * P:(k + 1) * P],
                                                  ident[:, :])
                    ins.then_inc(s_flip, 1)
    core.stage_ends()


def stage_gat_weights(core, g, W, a_src, a_dst, H):
    nc, XT = core.nc, core.XT
    D = F // H
    R = g.rep
    wx, wdb, msg, kap, bias = g.wx, g.wdb, g.msg, g.kap, g.bias
    with ExitStack() as ctx:
        h = core.sb(ctx, "h", [P, NT, F + H])
        ab = core.sb(ctx, "a_rows", [P, 2, F])
        wa = core.sb(ctx, "w_times_a", [P, KF, F])
        wd = core.sb(ctx, "w_dst", [P, KF, H])
        es = core.sb(ctx, "es", [P, NT, H])
        pad = core.sb(ctx, "pad", [P, NT])
        top = core.sb(ctx, "top", [P, H])
        allm = core.sb(ctx, "greatest", [P, H])
        av = core.sb(ctx, "a_factor", [P, NT, H])
        bA = core.sb(ctx, "bias_a", [P, H])
        proj = core.ps(ctx, "proj", [P, 8, 512])
        s_w, s_dve, s_wx, s_proj, s_h, s_pad, s_top, s_all, s_bias, s_exp = (core.sem(n) for n in (
            "w_in", "dve", "wx_made", "projected", "h_made", "pad_made", "top_made", "greatest_made", "bias_made", "exp_made"))
        with nc.Block() as block:
            @block.sync
            def _(sp):
                sp.dma_start(wx[:, :, 0:F], W.rearrange("(k p) n -> p k n", p=P)).then_inc(s_w, 16)
                for k, row in enumerate((a_src, a_dst)):
                    sp.dma_start(ab[:, k, :], row.rearrange("h d -> (h d)").partition_broadcast(P)).then_inc(s_w, 16)
                sp.wait_ge(s_w, 48)

            @block.gpsimd
            def _(pool):
                nc.gpsimd.memset(pad[:, :], 0.0).then_inc(s_pad, 1)
                pool.wait_ge(s_pad, 1)
                nc.gpsimd.affine_select(out=pad[:, :], in_=pad[:, :], compare_op=ALU.is_ge, fill=-1e30, base=N - 1,
                                        pattern=[[-P, NT]], channel_multiplier=-1).then_inc(s_pad, 1)
                pool.wait_ge(s_top, 1)
                nc.gpsimd.partition_all_reduce(allm[:, :], top[:, :], P, RMAX).then_inc(s_all, 1)

            @block.vector
            def _(dve):
                link = Chain(dve, s_dve)
                dve.wait_ge(s_w, 48)
                for k, out in ((0, wx[:, :, F:F + H]), (1, wd[:, :, :])):
                    link(nc.vector.tensor_tensor(wa[:, :, :], wx[:, :, 0:F], ab[:, k:k + 1, :].to_broadcast([P, KF, F]), ALU.mult))
                    link(nc.vector.tensor_reduce(out, wa[:, :, :].rearrange("p k (h d) -> p k h d", h=H), AX.X, ALU.add))
                nc.vector.tensor_copy(wdb[:, :, :, :], wd[:, :, :].unsqueeze(3).to_broadcast([P, KF, H, P])).then_inc(s_wx, 1)
                dve.wait_ge(s_h, NT)
                dve.wait_ge(s_pad, 2)
                link(nc.vector.tensor_tensor(es[:, :, :], h[:, :, F:F + H], pad[:, :].unsqueeze(2).to_broadcast([P, NT, H]), ALU.add))
                nc.vector.tensor_reduce(top[:, :], es[:, :, :].rearrange("p t h -> p h t"), AX.X, ALU.max).then_inc(s_top, 1)
                dve.wait_ge(s_all, 1)
                link(nc.vector.tensor_tensor(es[:, :, :], h[:, :, F:F + H], allm[:, :].unsqueeze(1).to_broadcast([P, NT, H]), ALU.min))
                link(nc.vector.tensor_scalar(bA[:, :], allm[:, :], -0.2, BIAS_A, ALU.mult, ALU.add))
                nc.vector.tensor_scalar(bias[:, :], allm[:, :], -0.8, BIAS_K, ALU.mult, ALU.add).then_inc(s_bias, 1)
                dve.wait_ge(s_exp, 2 * H)
                m = msg[:, :, :, 0:D]
                link(nc.vector.tensor_tensor(m, h[:, :, 0:F].rearrange("p t (h d) -> p t h d", h=H),
                                             av[:, :, :].unsqueeze(3).to_broadcast([P, NT, H, D]), ALU.mult))
                link(nc.vector.tensor_copy(msg[:, :, :, D:D + R], av[:, :, :].unsqueeze(3).to_broadcast([P, NT, H, R])))

            @block.scalar
            def _(act):
                for t in range(NT):
                    act.wait_ge(s_proj, t + 1)
                    nc.scalar.copy(h[:, t, :], proj[:, t % 8, 0:F + H]).then_inc(s_h, 1)
                act.wait_ge(s_bias, 1)
                for j in range(H):
                    nc.scalar.activation(av[:, :, j], es[:, :, j], ACT.Exp, bias=bA[:, j:j + 1], scale=0.2).then_inc(s_exp, 1)
                    nc.scalar.activation(kap[:, :, j], es[:, :, j], ACT.Exp, bias=bias[:, j:j + 1], scale=0.8).then_inc(s_exp, 1)

            @block.tensor
            def _(pe):
                pe.wait_ge(s_wx, 1)
                for t in range(NT):
                    if t >= 8:
                        pe.wait_ge(s_h, t - 7)
                    for k in range(KF):
                        ins = nc.tensor.matmul(proj[:, t % 8, 0:F + H], XT[:, k, t * P:(t + 1) * P], wx[:, k, :],
                                               start=(k == 0), stop=(k == KF - 1))
                    ins.then_inc(s_proj, 1)
    core.stage_ends()


BIAS_A = 30.0
BIAS_K = 35.0
RHO_MAX = 1.5860134523134308e15


def load_counts(core, sp, cbuf, s_c, s_w, per):
    nc, C = core.nc, core.C
    rows = C[0:CELLS, 0:1].rearrange("(l t p d) o -> l p t (d o)", t=ST, p=P, d=NP)

    def load(slot, part, cols):
        sp.dma_start(cbuf[:, slot, :, :], rows[part][:, :, cols]).then_inc(s_c[slot], 16)

    def round_of_two(i, parts):
        for m in parts:
            sp.wait_ge(s_w, i * 2 * per + (m + 1) * (per // NL) + 1)
            n = m + 2
            load(n % 2, n % NL, bass.ds((2 * i + n // NL) * CH, CH))

    for n in range(2):
        load(n, n, slice(0, CH))
    with sp.Fori(0, NCH // 2 - 1) as i:
        round_of_two(i, range(2 * NL))
    round_of_two(NCH // 2 - 1, range(2 * NL - 2))


def wait_counts(eng, s_c, i, u, part):
    n = u * NL + part
    eng.wait_ge(s_c[n % 2], (i * NL + n // 2 + 1) * 16)


def stage_gat_aggregate(core, g, b, H):
    nc, XT = core.nc, core.XT
    D = F // H
    WR = 8
    RB = min(H, 4)
    per = NT * H
    row_at = {(5 + j) * H: j for j in range(H)}
    msg, kap, bias, wdb = g.msg, g.kap, g.bias, g.wdb
    with ExitStack() as ctx:
        cbuf = core.sb(ctx, "counts", [P, 2, ST, CH])
        rho = core.sb(ctx, "rho", [P, 2, H, CH])
        w = core.sb(ctx, "weights", [P, WR, CH])
        inv = core.sb(ctx, "inv", [P, KF, CH])
        y = core.sb(ctx, "y", [P, KF, CH])
        ey = core.sb(ctx, "exp_y", [P, KF, CH])
        bcol = core.sb(ctx, "bias_cols", [P, KF])
        less = core.sb(ctx, "minus_one", [P, 1])
        acc = core.ps(ctx, "acc", [P, 4, 512])
        row = core.ps(ctx, "row", [P, 4, 512])
        s_c = [core.sem("counts_in") for _ in range(2)]
        s_b, s_row, s_exp, s_rho, s_w, s_used, s_den, s_inv, s_raw, s_act, s_ey, s_y = (core.sem(n) for n in (
            "bias_in", "rows_made", "rho_raw", "rho_made", "w_made", "w_used", "den_copied", "inv_made", "acc_read",
            "act", "exp_y_made", "y_done"))

        def make_row(j, cols):
            for k in range(KF):
                ins = nc.tensor.matmul(row[:, j % RB, 0:CH], wdb[:, k, j, :], XT[:, k, cols], start=(k == 0), stop=(k == KF - 1))
            ins.then_inc(s_row, 1)

        def make_rho(j, u):
            nc.scalar.activation(rho[:, u, j, :], row[:, j % RB, 0:CH], ACT.Exp, bias=bias[:, j:j + 1],
                                 scale=-0.8).then_inc(s_exp, 1)

        def bound_rho(u):
            nc.vector.tensor_scalar(rho[:, u, :, :], rho[:, u, :, :], RHO_MAX, None, ALU.min).then_inc(s_rho, 1)

        with nc.Block() as block:
            @block.sync
            def _(sp):
                sp.dma_start(bcol[:, :], b.rearrange("(k p) -> p k", p=P), allow_slow_non_contiguous=True).then_inc(s_b, 16)
                load_counts(core, sp, cbuf, s_c, s_w, per)

            @block.tensor
            def _(pe):
                for j in range(H):
                    if j >= RB:
                        pe.wait_ge(s_exp, j - RB + 2)
                    make_row(j, slice(0, CH))
                with pe.Fori(0, NCH // 2) as i:
                    for u in range(2):
                        c = 2 * i + u
                        pe.wait_ge(s_raw, c + 1)
                        for n in range(per):
                            t, j = n // H, n % H
                            if n in row_at:
                                pe.wait_ge(s_exp, (c + 1) * H + row_at[n] - RB + 2)
                                make_row(row_at[n], bass.ds((c + 1) * CH, CH))
                            pe.wait_ge(s_w, c * per + n + 2)
                            if H == 1:
                                for q in range(3):
                                    ins = nc.tensor.matmul(acc[:, q, 0:CH], msg[:, t, 0, q * P:(q + 1) * P], w[:, n % WR, :],
                                                           start=(t == 0), stop=(t == NT - 1))
                            else:
                                o = 64 * (j % 2)
                                ins = nc.tensor.matmul(acc[o:o + 64, j // 2, 0:CH], msg[:, t, j, :], w[:, n % WR, :],
                                                       start=(t == 0), stop=(t == NT - 1))
                            ins.then_inc(s_used, 1)

            @block.scalar
            def _(act):
                link = Chain(act, s_act)
                nc.scalar.sem_inc(s_exp, 1)
                act.wait_ge(s_b, 32)
                for j in range(H):
                    act.wait_ge(s_row, j + 1)
                    make_rho(j, 0)
                with act.Fori(0, NCH // 2) as i:
                    for u in range(2):
                        c = 2 * i + u
                        act.wait_ge(s_w, c * per + 1)
                        for j in range(H):
                            act.wait_ge(s_row, (c + 1) * H + j + 1)
                            make_rho(j, 1 - u)
                        if H > 1:
                            for j in range(H):
                                o = 64 * (j % 2) + D
                                act.wait_ge(s_used, c * per + (NT - 1) * H + j + 1)
                                nc.scalar.copy(inv[D * (j % 4):D * (j % 4) + D, j // 4, :], acc[o:o + D, j // 2, 0:CH]
                                               ).then_inc(s_den, 1)
                        link.n, link.base = 0, c * 4
                        act.wait_ge(s_raw, c + 2)
                        for k in range(KF):
                            ins = nc.scalar.activation(y[:, k, :], y[:, k, :], ACT.Identity, bias=bcol[:, k:k + 1])
                        link(ins)
                        link(nc.scalar.activation(ey[:, :, :], y[:, :, :], ACT.Relu, scale=-1.0))
                        link(nc.scalar.activation(y[:, :, :], y[:, :, :], ACT.Relu))
                        link(nc.scalar.activation(y[:, :, :], y[:, :, :], ACT.Identity, bias=less[:, 0:1]))
                        nc.scalar.activation(ey[:, :, :], ey[:, :, :], ACT.Exp, scale=-1.0).then_inc(s_ey, 1)

            @block.gpsimd
            def _(pool):
                nc.gpsimd.sem_inc(s_y, 1)
                nc.gpsimd.memset(less[:, :], -1.0).then_inc(s_b, 16)
                with pool.Fori(0, NCH) as i:
                    pool.wait_ge(s_ey, i + 1)
                    first = pool.snap(i * CH)
                    nc.gpsimd.tensor_tensor(XT[:, :, bass.ds(first, CH)], y[:, :, :], ey[:, :, :], ALU.add).then_inc(s_y, 1)

            @block.vector
            def _(dve):
                nc.vector.sem_inc(s_w, 1)
                nc.vector.sem_inc(s_raw, 1)
                dve.wait_ge(s_exp, H + 1)
                bound_rho(0)
                with dve.Fori(0, NCH // 2) as i:
                    for u in range(2):
                        c = 2 * i + u
                        dve.wait_ge(s_rho, c + 1)
                        for n in range(per):
                            t, j = n // H, n % H
                            if n % (H * ST) == 0:
                                wait_counts(dve, s_c, i, u, t // ST)
                            if n >= WR:
                                dve.wait_ge(s_used, c * per + n - WR + 1)
                            nc.vector.scalar_tensor_tensor(out=w[:, n % WR, :], in0=rho[:, u, j, :], scalar=kap[:, t, j:j + 1],
                                                           in1=cbuf[:, (u * NL + t // ST) % 2, t % ST, :],
                                                           op0=ALU.max, op1=ALU.mult).then_inc(s_w, 1)
                        dve.wait_ge(s_exp, (c + 2) * H + 1)
                        bound_rho(1 - u)
                        dve.wait_ge(s_y, c + 1)
                        if H == 1:
                            dve.wait_ge(s_used, (c + 1) * per)
                            nc.vector.reciprocal(inv[:, 0, :], acc[:, 2, 0:CH]).then_inc(s_inv, 1)
                            dve.wait_ge(s_inv, c + 1)
                            nc.vector.tensor_tensor(y[:, :, :], acc[:, 0:KF, 0:CH], inv[:, 0:1, :].to_broadcast([P, KF, CH]),
                                                    ALU.mult).then_inc(s_raw, 1)
                        else:
                            dve.wait_ge(s_den, (c + 1) * H)
                            nc.vector.reciprocal(inv[:, :, :], inv[:, :, :]).then_inc(s_inv, 1)
                            dve.wait_ge(s_inv, c + 1)
                            for j in range(H):
                                o, r = 64 * (j % 2), D * (j % 4)
                                ins = nc.vector.tensor_tensor(y[r:r + D, j // 4, :], acc[o:o + D, j // 2, 0:CH],
                                                              inv[r:r + D, j // 4, :], ALU.mult)
                            ins.then_inc(s_raw, 1)
                        dve.wait_ge(s_raw, c + 2)
                dve.wait_ge(s_rho, NCH + 1)
    core.stage_ends()


class Gat:

    def __init__(self, core, ctx, H):
        D = F // H
        self.rep = P if H == 1 else D
        self.wx = core.sb(ctx, "wx", [P, KF, F + H])
        self.wdb = core.sb(ctx, "w_dst_columns", [P, KF, H, P])
        self.msg = core.sb(ctx, "messages", [P, NT, H, D + self.rep])
        self.kap = core.sb(ctx, "kappa", [P, NT, H])
        self.bias = core.sb(ctx, "bias_k", [P, H])


def stage_back(core, s_name="back"):
    nc, XT, X, ident = core.nc, core.XT, core.X, core.ident
    with ExitStack() as ctx:
        flip = core.ps(ctx, "flip", [P, 8, 512])
        s_flip, s_add = core.sem("flipped"), core.sem("added")
        with nc.Block() as block:
            @block.tensor
            def _(pe):
                for t in range(NT):
                    if t >= 8:
                        pe.wait_ge(s_add, t - 7)
                    for k in range(KF):
                        ins = nc.tensor.transpose(flip[:, t % 8, k * P:(k + 1) * P], XT[:, k, t * P:(t + 1) * P], ident[:, :])
                    ins.then_inc(s_flip, 1)

            @block.vector
            def _(dve):
                for t in range(NT):
                    dve.wait_ge(s_flip, t + 1)
                    nc.vector.tensor_tensor(X[:, t, :], X[:, t, :], flip[:, t % 8, 0:F], ALU.add).then_inc(s_add, 1)
    core.stage_ends()


def stage_ones_off(core):
    nc, C = core.nc, core.C
    with ExitStack() as ctx:
        d = core.sb(ctx, "diagonal", [P, NT])
        s_in, s_sub, s_out = core.sem("diag_in"), core.sem("diag_less"), core.sem("diag_out")
        diag = bass.AP(C.tensor, 0, [[NP + 1, NP], [1, 1]]).rearrange("(p t) o -> p t o", p=P)
        with nc.Block() as block:
            @block.sync
            def _(sp):
                sp.dma_start(d[:, :].unsqueeze(2), diag, allow_slow_non_contiguous=True).then_inc(s_in, 16)
                sp.wait_ge(s_sub, 1)
                sp.dma_start(diag, d[:, :].unsqueeze(2), allow_slow_non_contiguous=True).then_inc(s_out, 16)
                sp.wait_ge(s_out, 16)

            @block.vector
            def _(dve):
                dve.wait_ge(s_in, 16)
                nc.vector.tensor_scalar(d[:, :], d[:, :], -1.0, None, ALU.add).then_inc(s_sub, 1)
    core.stage_ends()


def top_two(nc, link, L, E_, vals, ids, idf, iota, w, wf, hot, exp_pair):
    for t in range(NT):
        link(nc.vector.max(vals[:, t, :], L[:, t, :]))
        link(nc.vector.max_index(ids[:, t, :], vals[:, t, :], L[:, t, :]))
    link(nc.vector.tensor_copy(idf[:, :, :], ids[:, :, 0:2]))
    link(nc.vector.tensor_tensor(w[:, :, :], vals[:, :, 0:2], vals[:, :, 0:1].to_broadcast([P, NT, 2]), ALU.subtract))
    exp_pair(w)
    link(nc.vector.tensor_reduce(vals[:, :, 7], w[:, :, :], AX.X, ALU.add))
    link(nc.vector.reciprocal(vals[:, :, 6], vals[:, :, 7]))
    link(nc.vector.tensor_tensor(w[:, :, :], w[:, :, :], vals[:, :, 6:7].to_broadcast([P, NT, 2]), ALU.mult))
    for j in range(2):
        link(nc.vector.tensor_tensor(hot[:, j, :, :], iota[:, :].unsqueeze(1).to_broadcast([P, NT, E_]),
                                     idf[:, :, j:j + 1].to_broadcast([P, NT, E_]), ALU.is_equal))
        link(nc.vector.tensor_tensor(hot[:, j, :, :], hot[:, j, :, :], w[:, :, j:j + 1].to_broadcast([P, NT, E_]), ALU.mult))
    link(nc.vector.tensor_tensor(wf[:, :, :], hot[:, 0, :, :], hot[:, 1, :, :], ALU.add))


def stage_route(core, Wr, br, b2, wf, E_, softmax_first):
    nc, XT, X, ident = core.nc, core.XT, core.X, core.ident
    EL = 8
    with ExitStack() as ctx:
        wr = core.sb(ctx, "w_router", [P, KF, E_])
        brb = core.sb(ctx, "b_router", [P, E_])
        b2s = core.sb(ctx, "b_out", [E_, F])
        L = core.sb(ctx, "logits", [P, NT, EL])
        vals = core.sb(ctx, "vals", [P, NT, 8])
        ids = core.sb(ctx, "ids", [P, NT, 8], U32)
        idf = core.sb(ctx, "ids_f", [P, NT, 2])
        iota = core.sb(ctx, "iota", [P, E_])
        w = core.sb(ctx, "pair", [P, NT, 2])
        hot = core.sb(ctx, "hot", [P, 2, NT, E_])
        one = core.sb(ctx, "per_node", [P, 2, NT])
        wft = core.sb(ctx, "weights_t", [E_, NT, P])
        lg = core.ps(ctx, "logits_ps", [P, 512])
        tp = core.ps(ctx, "flip", [P, 7, 512])
        s_w, s_lg, s_dve, s_pair, s_e, s_iota, s_wf, s_tp, s_wft, s_bias, s_add = (core.sem(n) for n in (
            "w_in", "logits_made", "dve", "pair_made", "exp_made", "iota", "wf_made", "flipped", "wft_made", "bias_made", "added"))
        with nc.Block() as block:
            @block.sync
            def _(sp):
                sp.dma_start(wr[:, :, :], Wr.rearrange("(k p) e -> p k e", p=P)).then_inc(s_w, 16)
                sp.dma_start(brb[:, :], br.partition_broadcast(P)).then_inc(s_w, 16)
                sp.dma_start(b2s[:, :], b2).then_inc(s_w, 16)
                sp.wait_ge(s_w, 48)

            @block.gpsimd
            def _(pool):
                nc.gpsimd.iota(iota[:, :], pattern=[[1, E_]], base=0, channel_multiplier=0,
                               allow_small_or_imprecise_dtypes=True).then_inc(s_iota, 1)

            @block.tensor
            def _(pe):
                pe.wait_ge(s_w, 48)
                for t in range(NT):
                    for k in range(KF):
                        ins = nc.tensor.matmul(lg[:, t * E_:(t + 1) * E_], XT[:, k, t * P:(t + 1) * P], wr[:, k, :],
                                               start=(k == 0), stop=(k == KF - 1))
                ins.then_inc(s_lg, 1)
                pe.wait_ge(s_wf, 1)
                for t in range(NT):
                    ins = nc.tensor.transpose(tp[0:E_, t // 4, (t % 4) * P:(t % 4 + 1) * P], wf[:, t, :], ident[:, :])
                ins.then_inc(s_tp, 1)
                for t in range(NT):
                    pe.wait_ge(s_wft, 7)
                    if t >= 7:
                        pe.wait_ge(s_add, t - 6)
                    nc.tensor.matmul(tp[:, t % 7, 0:F], wft[:, t, :], b2s[:, :], start=True, stop=True).then_inc(s_bias, 1)

            @block.scalar
            def _(act):
                if softmax_first:
                    act.wait_ge(s_pair, 1)
                    nc.scalar.activation(L[:, :, 0:E_], L[:, :, 0:E_], ACT.Exp).then_inc(s_e, 1)
                act.wait_ge(s_pair, 1 + softmax_first)
                nc.scalar.activation(w[:, :, :], w[:, :, :], ACT.Exp).then_inc(s_e, 1)

            @block.vector
            def _(dve):
                link = Chain(dve, s_dve)
                if E_ < EL:
                    link(nc.vector.memset(L[:, :, E_:EL], -1e30))
                dve.wait_ge(s_lg, 1)
                dve.wait_ge(s_w, 48)
                dve.wait_ge(s_iota, 1)
                real = L[:, :, 0:E_]
                link(nc.vector.tensor_tensor(real, lg[:, 0:NT * E_].rearrange("p (t e) -> p t e", e=E_),
                                             brb[:, :].unsqueeze(1).to_broadcast([P, NT, E_]), ALU.add))
                if softmax_first:
                    link(nc.vector.tensor_reduce(one[:, 0, :], real, AX.X, ALU.max))
                    nc.vector.tensor_tensor(real, real, one[:, 0, :].unsqueeze(2).to_broadcast([P, NT, E_]), ALU.subtract
                                            ).then_inc(s_pair, 1)
                    dve.wait_ge(s_e, 1)
                    link(nc.vector.tensor_reduce(one[:, 0, :], real, AX.X, ALU.add))
                    link(nc.vector.reciprocal(one[:, 1, :], one[:, 0, :]))
                    link(nc.vector.tensor_tensor(real, real, one[:, 1, :].unsqueeze(2).to_broadcast([P, NT, E_]), ALU.mult))

                def exp_pair(w):
                    nc.vector.tensor_copy(one[:, 0, :], w[:, :, 0]).then_inc(s_pair, 1)
                    dve.wait_ge(s_e, 1 + softmax_first)

                top_two(nc, link, L, E_, vals, ids, idf, iota, w, wf, hot, exp_pair)
                nc.vector.tensor_copy(one[:, 0, :], wf[:, :, 0]).then_inc(s_wf, 1)
                dve.wait_ge(s_tp, 1)
                for b in range(7):
                    m = min(4, NT - 4 * b)
                    nc.vector.tensor_copy(wft[:, 4 * b:4 * b + m, :], tp[0:E_, b, 0:m * P].rearrange("e (t p) -> e t p", p=P)
                                          ).then_inc(s_wft, 1)
                for t in range(NT):
                    dve.wait_ge(s_bias, t + 1)
                    nc.vector.tensor_tensor(X[:, t, :], X[:, t, :], tp[:, t % 7, 0:F], ALU.add).then_inc(s_add, 1)
    core.stage_ends()


class Net:

    def __init__(self, layers, column=None):
        self.layers, self.column = layers, column


def stage_nets(core, nets, wf=None, out_bias=None):
    nc, XT, X = core.nc, core.XT, core.X
    with ExitStack() as ctx:
        tiles, nload = [], 0
        for net in nets:
            lay = []
            for W, b, fn in net.layers:
                K, M = W.shape
                kp = min(K, P)
                wt = core.sb(ctx, "w", [kp, K // kp, M])
                bt = core.sb(ctx, "b", [min(M, P), -(-M // P)]) if b is not None else None
                nload += 1 + (b is not None)
                lay.append((wt, bt, fn, K // kp, kp, M))
            tiles.append(lay)
        width = max(-(-l[5] // P) for t in tiles for l in t[:-1])
        depth = max(len(t) - 1 for t in tiles)
        hbuf = core.sb(ctx, "hidden", [P, 2, depth, width, TN])
        yc = core.sb(ctx, "y", [P, TC, F])
        wc = core.sb(ctx, "weights_chunk", [P, TC, 8])
        ob = core.sb(ctx, "out_bias", [P, F])
        up = core.ps(ctx, "up", [P, 4, 512])
        down = core.ps(ctx, "down", [P, 4, 512])
        s_w, s_up, s_act, s_down, s_y, s_dve, s_x = (core.sem(n) for n in (
            "w_in", "up_made", "hidden_made", "down_made", "y_added", "dve", "x_added"))
        if out_bias is not None:
            nload += 1
        ups = [(e, l, m, hf) for e, t in enumerate(tiles) for l in range(len(t) - 1)
               for m in range(-(-t[l][5] // P)) for hf in range(2)]
        NU, ND = len(ups), len(tiles) * TC
        last_of = {}
        for n, (e, l, m, hf) in enumerate(ups):
            last_of[(e, l)] = n
        with nc.Block() as block:
            @block.sync
            def _(sp):
                with nc.allow_non_contiguous_dma(reason="bias columns"):
                    for net, t in zip(nets, tiles):
                        for (W, b, _), (wt, bt, _, _, kp, M) in zip(net.layers, t):
                            sp.dma_start(wt[:, :, :], W.rearrange("(k p) m -> p k m", p=kp)).then_inc(s_w, 16)
                            if b is not None:
                                sp.dma_start(bt[:, :], b.rearrange("(k p) -> p k", p=min(M, P))).then_inc(s_w, 16)
                    if out_bias is not None:
                        sp.dma_start(ob[:, :], out_bias.partition_broadcast(P)).then_inc(s_w, 16)
                sp.wait_ge(s_w, 16 * nload)

            @block.tensor
            def _(pe):
                pe.wait_ge(s_w, 16 * nload)
                nc.tensor.sem_inc(s_down, 1)
                with pe.Fori(0, NTC) as i:
                    def up_step(n):
                        e, l, m, hf = ups[n]
                        wt, bt, fn, nk, kp, M = tiles[e][l]
                        mw = min(P, M - m * P)
                        if l:
                            pe.wait_ge(s_act, i * NU + last_of[(e, l - 1)] + 2)
                        if n >= 4:
                            pe.wait_ge(s_act, i * NU + n - 2)
                        else:
                            pe.wait_ge(s_act, i * NU + 1)
                        for k in range(nk):
                            rhs = (XT[:, k, bass.ds(i * TN + hf * TH, TH)] if l == 0 else
                                   hbuf[0:kp, e % 2, l - 1, k, hf * TH:(hf + 1) * TH])
                            ins = nc.tensor.matmul(up[0:mw, n % 4, 0:TH], wt[:, k, m * P:m * P + mw], rhs,
                                                   start=(k == 0), stop=(k == nk - 1))
                        ins.then_inc(s_up, 1)

                    def down_step(e):
                        wt, _, _, nk, kp, _ = tiles[e][-1]
                        pe.wait_ge(s_act, i * NU + last_of[(e, len(tiles[e]) - 2)] + 2)
                        for j in range(TC):
                            n = e * TC + j
                            if n >= 4:
                                pe.wait_ge(s_y, i * ND + n - 2)
                            else:
                                pe.wait_ge(s_y, i * ND + 1)
                            for k in range(nk):
                                ins = nc.tensor.matmul(down[:, n % 4, 0:F],
                                                       hbuf[0:kp, e % 2, len(tiles[e]) - 2, k, j * P:(j + 1) * P], wt[:, k, :],
                                                       start=(k == 0), stop=(k == nk - 1))
                            ins.then_inc(s_down, 1)

                    for e in range(len(tiles)):
                        for n, u in enumerate(ups):
                            if u[0] == e:
                                up_step(n)
                        if e:
                            down_step(e - 1)
                    down_step(len(tiles) - 1)

            @block.scalar
            def _(act):
                act.wait_ge(s_w, 16 * nload)
                nc.scalar.sem_inc(s_act, 1)
                with act.Fori(0, NTC) as i:
                    for n, (e, l, m, hf) in enumerate(ups):
                        _, bt, fn, _, _, M = tiles[e][l]
                        mw = min(P, M - m * P)
                        act.wait_ge(s_up, i * NU + n + 1)
                        if e >= 2:
                            act.wait_ge(s_down, i * ND + (e - 1) * TC + 1)
                        else:
                            act.wait_ge(s_down, i * ND + 1)
                        nc.scalar.activation(hbuf[0:mw, e % 2, l, m, hf * TH:(hf + 1) * TH], up[0:mw, n % 4, 0:TH], fn,
                                             bias=bt[0:mw, m:m + 1]).then_inc(s_act, 1)

            @block.vector
            def _(dve):
                link = Chain(dve, s_dve)
                dve.wait_ge(s_w, 16 * nload)
                nc.vector.sem_inc(s_y, 1)
                nc.vector.sem_inc(s_x, 1)
                with dve.Fori(0, NTC) as i:
                    NLINK = 1
                    link.n, link.base = 0, i * NLINK
                    dve.wait_ge(s_x, i + 1)
                    if wf is not None:
                        link(nc.vector.tensor_copy(wc[:, :, 0:wf.shape[2]], wf[:, bass.ds(i * TC, TC), :]))
                    for e, net in enumerate(nets):
                        if e:
                            dve.wait_ge(s_y, i * ND + e * TC + 1)
                        for j in range(TC):
                            n = e * TC + j
                            dve.wait_ge(s_down, i * ND + n + 2)
                            o, y = down[:, n % 4, 0:F], yc[:, j, :]
                            if net.column is None and e == 0 and out_bias is not None:
                                ins = nc.vector.tensor_tensor(y, o, ob[:, :], ALU.add)
                            elif e == 0:
                                ins = nc.vector.tensor_scalar(y, o, wc[:, j, net.column:net.column + 1], None, ALU.mult)
                            else:
                                ins = nc.vector.scalar_tensor_tensor(out=y, in0=o, scalar=wc[:, j, net.column:net.column + 1],
                                                                     in1=y, op0=ALU.mult, op1=ALU.add)
                            ins.then_inc(s_y, 1)
                    dve.wait_ge(s_y, (i + 1) * ND + 1)
                    nc.vector.tensor_tensor(X[:, bass.ds(i * TC, TC), :], X[:, bass.ds(i * TC, TC), :], yc[:, :, :], ALU.add
                                            ).then_inc(s_x, 1)
    core.stage_ends()


def stage_kv(core, a, ks, msg):
    nc, XT = core.nc, core.XT
    HD, H, R = 32, 8, 4
    with ExitStack() as ctx:
        w = core.sb(ctx, "w_kv", [P, 2, KF, F])
        w4 = core.sb(ctx, "w_k_fourfold", [P, KF, H, 4, HD])
        b4 = core.sb(ctx, "b_k_fourfold", [P, H])
        bv = core.sb(ctx, "b_v", [P, F])
        less = core.sb(ctx, "less", [P, 2])
        whole = core.sb(ctx, "k_whole", [P, R, CH])
        left = core.sb(ctx, "k_left", [P, R, CH])
        second = core.sb(ctx, "k_second", [P, R, CH], BF16)
        ps = core.ps(ctx, "proj", [P, 8, 512])
        s_w, s_w4, s_ps, s_whole, s_left, s_second, s_ks, s_v, s_one = (core.sem(n) for n in (
            "w_in", "w4_made", "projected", "whole_made", "left_made", "second_made", "ks_made", "v_made", "ones_made"))
        kjobs = [(h, c) for h in range(H) for c in range(NCH)]
        NK = len(kjobs)
        with nc.Block() as block:
            @block.sync
            def _(sp):
                with nc.allow_non_contiguous_dma(reason="bias columns"):
                    for o, n in enumerate("kv"):
                        sp.dma_start(w[:, o, :, :], a["L1_gnn_W" + n].rearrange("(k p) m -> p k m", p=P)).then_inc(s_w, 16)
                    for g in range(4):
                        sp.dma_start(b4[g * HD:(g + 1) * HD, :], a["L1_gnn_bk"].rearrange("(h d) -> d h", d=HD)).then_inc(s_w, 16)
                sp.dma_start(bv[:, :], a["L1_gnn_bv"].partition_broadcast(P)).then_inc(s_w, 16)
                sp.wait_ge(s_w, 16 * 7)

            @block.gpsimd
            def _(pool):
                nc.gpsimd.memset(msg[:, :, :, HD:2 * HD], 1.0).then_inc(s_one, 1)

            @block.tensor
            def _(pe):
                pe.wait_ge(s_w4, 1)
                for n in range(NK + NT):
                    if n >= 8:
                        if n - 8 < NK:
                            pe.wait_ge(s_whole, n - 7)
                        else:
                            pe.wait_ge(s_v, n - 7 - NK)
                    for k in range(KF):
                        if n < NK:
                            h, c = kjobs[n]
                            ins = nc.tensor.matmul(ps[:, n % 8, 0:CH], w4[:, k, h, :, :].rearrange("p g d -> p (g d)"),
                                                   XT[:, k, c * CH:(c + 1) * CH], start=(k == 0), stop=(k == KF - 1))
                        else:
                            t = n - NK
                            ins = nc.tensor.matmul(ps[:, n % 8, 0:F], XT[:, k, t * P:(t + 1) * P], w[:, 1, k, :],
                                                   start=(k == 0), stop=(k == KF - 1))
                    ins.then_inc(s_ps, 1)

            @block.scalar
            def _(act):
                act.wait_ge(s_w, 16 * 7)
                for n in range(NK + 2):
                    if n < NK:
                        h, c = kjobs[n]
                        act.wait_ge(s_ps, n + 1)
                        if n >= R:
                            act.wait_ge(s_left, n - R + 1)
                        nc.scalar.activation(ks[:, h, c * CH:(c + 1) * CH], ps[:, n % 8, 0:CH], ACT.Identity, bias=b4[:, h:h + 1])
                        nc.scalar.activation(whole[:, n % R, :], ps[:, n % 8, 0:CH], ACT.Identity, bias=b4[:, h:h + 1]
                                             ).then_inc(s_whole, 1)
                    if n >= 2:
                        m = n - 2
                        act.wait_ge(s_left, m + 1)
                        if m >= R:
                            act.wait_ge(s_ks, m - R + 1)
                        nc.scalar.copy(second[:, m % R, :], left[:, m % R, :]).then_inc(s_second, 1)

            @block.vector
            def _(dve):
                link = Chain(dve, core.sem("dve"))
                link(nc.vector.memset(less[:, :], 0.0))
                for g, j in ((1, 0), (2, 0), (2, 1)):
                    link(nc.vector.memset(less[g * HD:(g + 1) * HD, j:j + 1], -1.0))
                dve.wait_ge(s_w, 16 * 7)
                for g in range(4):
                    ins = nc.vector.tensor_copy(w4[:, :, :, g, :], w[:, 0, :, :].rearrange("p k (h d) -> p k h d", d=HD))
                ins.then_inc(s_w4, 1)
                for n in range(NK + 2):
                    if n < NK:
                        h, c = kjobs[n]
                        dve.wait_ge(s_whole, n + 1)
                        if n >= R:
                            dve.wait_ge(s_ks, n - R + 1)
                        nc.vector.scalar_tensor_tensor(out=left[:, n % R, :], in0=ks[:, h, c * CH:(c + 1) * CH],
                                                       scalar=less[:, 0:1], in1=whole[:, n % R, :],
                                                       op0=ALU.mult, op1=ALU.add).then_inc(s_left, 1)
                    if n >= 2:
                        h, c = kjobs[n - 2]
                        m = (n - 2) % R
                        dve.wait_ge(s_second, n - 1)
                        nc.vector.scalar_tensor_tensor(out=ks[:, h, c * CH:(c + 1) * CH], in0=second[:, m, :],
                                                       scalar=less[:, 1:2], in1=left[:, m, :],
                                                       op0=ALU.mult, op1=ALU.add).then_inc(s_ks, 1)
                for t in range(NT):
                    dve.wait_ge(s_ps, NK + t + 1)
                    nc.vector.tensor_tensor(msg[:, t, :, :].rearrange("p q (e d) -> p q e d", d=HD)[:, :, 0:3:2, :],
                                            ps[:, (NK + t) % 8, 0:F].rearrange("p (q e d) -> p q e d", e=2, d=HD),
                                            bv[:, :].rearrange("p (q e d) -> p q e d", e=2, d=HD), ALU.add).then_inc(s_v, 1)
    core.stage_ends()


SCORE_HI = 22026.465794806718
SCORE_LO = 4.5399929762484854e-05


def stage_attention(core, a, ks, msg):
    nc, XT = core.nc, core.XT
    D, H = 32, 8
    WR, SR, LAG = 8, 4, 3
    per = NT * H
    proj_at, left_at, second_at, third_at = 60, 128, 140, 152
    items = []
    for n in range(per):
        items.append(("score", n))
        if n >= proj_at and (n - proj_at) % 8 == 0 and (n - proj_at) // 8 < H:
            items.append(("q", (n - proj_at) // 8))
    NI = len(items)
    at = {x: m for m, x in enumerate(items)}
    scratch = core.X[:, :, :].rearrange("p t f -> p (t f)")
    w = scratch[:, 0:WR * CH].rearrange("p (r c) -> p r c", c=CH)
    whole = scratch[:, WR * CH:(WR + H) * CH].rearrange("p (r c) -> p r c", c=CH)
    with ExitStack() as ctx:
        q_hi = core.sb(ctx, "q_first", [P, 2, H, CH], BF16)
        q_lo = core.sb(ctx, "q_rest", [P, 2, H, CH], BF16)
        ex = core.sb(ctx, "exps", [P, SR, CH])
        inv = core.sb(ctx, "inv", [P, KF, CH])
        w4 = core.sb(ctx, "w_q_fourfold", [P, KF, H, 4, D])
        b4 = core.sb(ctx, "b_q_fourfold", [P, H])
        acc = core.ps(ctx, "acc", [P, 4, 512])
        sc = core.ps(ctx, "scores", [P, SR, 512])
        s_c = [core.sem("counts_in") for _ in range(2)]
        s_b, s_wq, s_w4, s_sc, s_ex, s_cl, s_w, s_used, s_dve, s_y, s_left, s_second, s_q, s_den = (core.sem(n) for n in (
            "bias_in", "wq_in", "w4_made", "items_made", "items_read", "clipped", "w_made", "w_used", "dve", "y_done",
            "left_made", "second_made", "q_made", "den_copied"))
        cbuf = core.sb(ctx, "counts", [P, 2, ST, CH])
        wq = cbuf[:, 0, 0:2, 0:F]

        def project(j, bank, cols):
            for k in range(KF):
                ins = nc.tensor.matmul(sc[:, bank, 0:CH], w4[:, k, j, :, :].rearrange("p g d -> p (g d)"), XT[:, k, cols],
                                       start=(k == 0), stop=(k == KF - 1))
            return ins

        def read_q(j, bank, u):
            nc.scalar.activation(q_hi[:, u, j, :], sc[:, bank, 0:CH], ACT.Identity, bias=b4[:, j:j + 1])
            return nc.scalar.activation(whole[:, j, :], sc[:, bank, 0:CH], ACT.Identity, bias=b4[:, j:j + 1])

        def two(n):
            return slice(2 * n, 2 * n + 2)

        def left(n, u):
            return nc.vector.tensor_tensor(whole[:, two(n), :], whole[:, two(n), :], q_hi[:, u, two(n), :], ALU.subtract)

        def second(n, u):
            return nc.scalar.copy(q_lo[:, u, two(n), :], whole[:, two(n), :])

        def third(n, u):
            return nc.vector.tensor_tensor(q_lo[0:D, u, two(n), :], whole[0:D, two(n), :], q_lo[0:D, u, two(n), :], ALU.subtract)

        with nc.Block() as block:
            @block.sync
            def _(sp):
                with nc.allow_non_contiguous_dma(reason="bias columns"):
                    for g in range(4):
                        sp.dma_start(b4[g * D:(g + 1) * D, :], a["L1_gnn_bq"].rearrange("(h d) -> d h", d=D)).then_inc(s_b, 16)
                sp.dma_start(wq, a["L1_gnn_Wq"].rearrange("(k p) m -> p k m", p=P)).then_inc(s_wq, 16)
                sp.wait_ge(s_w4, 1)
                load_counts(core, sp, cbuf, s_c, s_w, per)

            @block.tensor
            def _(pe):
                nc.tensor.sem_inc(s_sc, 1)
                pe.wait_ge(s_w4, 1)
                for j in range(H):
                    if j >= SR:
                        pe.wait_ge(s_ex, j - SR + 2)
                    project(j, j % SR, slice(0, CH)).then_inc(s_sc, 1)
                with pe.Fori(0, NCH // 2) as i:
                    for u in range(2):
                        items0 = (2 * i + u) * NI + H
                        w0 = (2 * i + u) * per
                        pe.wait_ge(s_q, (2 * i + u) * 4 + 4)
                        pe.wait_ge(s_y, 2 * i + u + 1)
                        for m in range(NI + LAG):
                            if m < NI:
                                kind, n = items[m]
                                pe.wait_ge(s_ex, items0 + m - SR + 2)
                                if kind == "q":
                                    project(n, m % SR, bass.ds((2 * i + u + 1) * CH, CH)).then_inc(s_sc, 1)
                                else:
                                    t, j = n // H, n % H
                                    nc.tensor.matmul(sc[:, m % SR, 0:CH], ks[0:3 * D, j, t * P:(t + 1) * P], q_hi[0:3 * D, u, j, :],
                                                     start=True, stop=False)
                                    nc.tensor.matmul(sc[:, m % SR, 0:CH], ks[:, j, t * P:(t + 1) * P], q_lo[:, u, j, :],
                                                     start=False, stop=True).then_inc(s_sc, 1)
                            if m >= LAG and items[m - LAG][0] == "score":
                                n = items[m - LAG][1]
                                t, j = n // H, n % H
                                o, v = 64 * (j % 2), D * (j % 2)
                                pe.wait_ge(s_w, w0 + n + 2)
                                nc.tensor.matmul(acc[o:o + 64, j // 2, 0:CH], msg[:, t, j // 2, v:v + 2 * D], w[:, n % WR, :],
                                                 start=(t == 0), stop=(t == NT - 1)).then_inc(s_used, 1)

            @block.scalar
            def _(act):
                nc.scalar.sem_inc(s_ex, 1)
                act.wait_ge(s_b, 64)
                for j in range(H):
                    act.wait_ge(s_sc, j + 2)
                    read_q(j, j % SR, 0).then_inc(s_ex, 1)
                for n in range(4):
                    act.wait_ge(s_left, n + 1)
                    second(n, 0).then_inc(s_second, 1)
                with act.Fori(0, NCH // 2) as i:
                    for u in range(2):
                        items0, w0 = (2 * i + u) * NI + H, (2 * i + u) * per
                        for m, (kind, n) in enumerate(items):
                            act.wait_ge(s_sc, items0 + m + 2)
                            if kind == "q":
                                if n == 0:
                                    act.wait_ge(s_q, (2 * i + u) * 4 + 4)
                                read_q(n, m % SR, 1 - u).then_inc(s_ex, 1)
                                continue
                            if n >= SR:
                                act.wait_ge(s_w, w0 + n - SR + 2)
                            else:
                                act.wait_ge(s_w, w0 + 1)
                            nc.scalar.activation(ex[:, n % SR, :], sc[:, m % SR, 0:CH], ACT.Exp, scale=D ** -0.5).then_inc(s_ex, 1)
                            if n >= second_at and (n - second_at) % 3 == 0 and (n - second_at) // 3 < 4:
                                c = (n - second_at) // 3
                                act.wait_ge(s_left, (2 * i + u) * 4 + 4 + c + 1)
                                second(c, 1 - u).then_inc(s_second, 1)
                        for j in range(H):
                            o = 64 * (j % 2) + D * (1 - j % 2)
                            act.wait_ge(s_used, w0 + (NT - 1) * H + j + 1)
                            nc.scalar.copy(inv[D * (j % 4):D * (j % 4) + D, j // 4, :], acc[o:o + D, j // 2, 0:CH]).then_inc(s_den, 1)

            @block.vector
            def _(dve):
                link = Chain(dve, s_dve)
                for s in (s_w, s_y):
                    nc.vector.sem_inc(s, 1)
                dve.wait_ge(s_wq, 16)
                for g in range(4):
                    ins = nc.vector.tensor_copy(w4[:, :, :, g, :], wq.rearrange("p k (h d) -> p k h d", d=D))
                ins.then_inc(s_w4, 1)
                for n in range(4):
                    dve.wait_ge(s_ex, 2 * n + 3)
                    left(n, 0).then_inc(s_left, 1)
                for n in range(4):
                    dve.wait_ge(s_second, n + 1)
                    dve.wait_ge(s_left, n + 1)
                    third(n, 0).then_inc(s_q, 1)
                with dve.Fori(0, NCH // 2) as i:
                    for u in range(2):
                        items0, w0, q0 = (2 * i + u) * NI + H, (2 * i + u) * per, (2 * i + u) * 4 + 4
                        link.n, link.base = 0, (2 * i + u) * 2
                        for n in range(per + 1):
                            if n < per:
                                dve.wait_ge(s_ex, items0 + at[("score", n)] + 2)
                                nc.vector.tensor_scalar(ex[:, n % SR, :], ex[:, n % SR, :], SCORE_HI, SCORE_LO, ALU.min, ALU.max
                                                        ).then_inc(s_cl, 1)
                            if n:
                                m = n - 1
                                t = m // H
                                if m % (H * ST) == 0:
                                    wait_counts(dve, s_c, i, u, t // ST)
                                dve.wait_ge(s_cl, w0 + m + 1)
                                if m >= WR:
                                    dve.wait_ge(s_used, w0 + m - WR + 1)
                                nc.vector.tensor_tensor(w[:, m % WR, :], ex[:, m % SR, :],
                                                        cbuf[:, (u * NL + t // ST) % 2, t % ST, :], ALU.mult
                                                        ).then_inc(s_w, 1)
                            c = (n - left_at) // 3
                            if (n - left_at) % 3 == 0 and 0 <= c < 4:
                                dve.wait_ge(s_ex, items0 + at[("q", 2 * c + 1)] + 2)
                                left(c, 1 - u).then_inc(s_left, 1)
                            c = (n - third_at) // 3
                            if (n - third_at) % 3 == 0 and 0 <= c < 4:
                                dve.wait_ge(s_second, q0 + c + 1)
                                dve.wait_ge(s_left, q0 + c + 1)
                                third(c, 1 - u).then_inc(s_q, 1)
                        dve.wait_ge(s_den, (2 * i + u + 1) * H)
                        link(nc.vector.tensor_scalar(inv[:, :, :], inv[:, :, :], 1e-20, None, ALU.max))
                        link(nc.vector.reciprocal(inv[:, :, :], inv[:, :, :]))
                        for j in range(H):
                            o, r = 64 * (j % 2) + D * (j % 2), D * (j % 4)
                            ins = nc.vector.tensor_tensor(XT[r:r + D, j // 4, bass.ds((2 * i + u) * CH, CH)],
                                                          acc[o:o + D, j // 2, 0:CH], inv[r:r + D, j // 4, :], ALU.mult)
                        ins.then_inc(s_y, 1)
                        dve.wait_ge(s_y, 2 * i + u + 2)
                dve.wait_ge(s_q, 4 * NCH + 4)
    core.stage_ends()


def stage_out_proj(core, a, T, parked):
    nc, XT, X = core.nc, core.XT, core.X
    with ExitStack() as ctx:
        w = core.sb(ctx, "w_p", [P, KF, F])
        bp = core.sb(ctx, "b_p", [P, F])
        ps = core.ps(ctx, "proj", [P, 8, 512])
        s_w, s_ps, s_add, s_dve = core.sem("w_in"), core.sem("projected"), core.sem("added"), core.sem("dve")
        with nc.Block() as block:
            @block.sync
            def _(sp):
                sp.dma_start(w[:, :, :], a["L1_gnn_Wp"].rearrange("(k p) m -> p k m", p=P)).then_inc(s_w, 16)
                sp.dma_start(bp[:, :], a["L1_gnn_bp"].partition_broadcast(P)).then_inc(s_w, 16)
                sp.dma_start(T[:, :, :], parked[0]).then_inc(s_w, 16)
                sp.dma_start(X[:, :, :], parked[1]).then_inc(s_w, 16)
                sp.wait_ge(s_w, 64)

            @block.tensor
            def _(pe):
                pe.wait_ge(s_w, 64)
                for t in range(NT):
                    if t >= 8:
                        pe.wait_ge(s_add, t - 7)
                    for k in range(KF):
                        ins = nc.tensor.matmul(ps[:, t % 8, 0:F], XT[:, k, t * P:(t + 1) * P], w[:, k, :],
                                               start=(k == 0), stop=(k == KF - 1))
                    ins.then_inc(s_ps, 1)

            @block.vector
            def _(dve):
                link = Chain(dve, s_dve)
                dve.wait_ge(s_w, 64)
                link(nc.vector.tensor_tensor(T[:, :, :], T[:, :, :], bp[:, :].unsqueeze(1).to_broadcast([P, NT, F]), ALU.add))
                for t in range(NT):
                    dve.wait_ge(s_ps, t + 1)
                    nc.vector.tensor_tensor(T[:, t, :], T[:, t, :], ps[:, t % 8, 0:F], ALU.add).then_inc(s_add, 1)
                dve.wait_ge(s_add, NT)
                link(nc.vector.tensor_tensor(X[:, :, :], X[:, :, :], T[:, :, :], ALU.add))
    core.stage_ends()


def rest(core, a, stop):
    stage_ones_off(core)
    NE0, NE1 = a["L0_ffn_W1"].shape[0], a["L1_ffn_eW1"].shape[0]
    with ExitStack() as c:
        wf = core.sb(c, "expert_weights", [P, NT, NE0])
        with ExitStack() as c2:
            T = core.sb(c2, "t", [P, NT, F])
            stage_norm(core, core.X, T, a["L0_ffn_gamma"], a["L0_ffn_beta"], times=2)
        stage_route(core, a["L0_ffn_Wr"], a["L0_ffn_br"], a["L0_ffn_b2"], wf, NE0, 0)
        stage_nets(core, [Net([(a["L0_ffn_W1"][e], a["L0_ffn_b1"][e], ACT.Gelu), (a["L0_ffn_W2"][e], None, None)], e)
                          for e in range(NE0)], wf)
    if stop == "moe":
        return
    parked = core.nc.dram_tensor("parked", (2, P, NT, F), F32, kind="Internal").ap()
    with ExitStack() as c:
        T = core.sb(c, "t", [P, NT, F])
        stage_norm(core, core.X, T, park=parked)
    with ExitStack() as c:
        ks = core.sb(c, "k_stacks", [P, 8, NP], BF16)
        msg = core.sb(c, "values", [P, NT, 4, 96])
        stage_kv(core, a, ks, msg)
        stage_attention(core, a, ks, msg)
    with ExitStack() as c:
        T = core.sb(c, "t", [P, NT, F])
        stage_out_proj(core, a, T, parked)
        stage_norm(core, T, T, a["L1_gnn_ln_g"], a["L1_gnn_ln_b"])
    stage_nets(core, [Net([(a["L1_gnn_W1"], a["L1_gnn_b1"], ACT.Gelu), (a["L1_gnn_W2"], None, None)])],
               out_bias=a["L1_gnn_b2"])
    if stop == "attn":
        return
    with ExitStack() as c:
        wf = core.sb(c, "expert_weights", [P, NT, NE1])
        with ExitStack() as c2:
            T = core.sb(c2, "t", [P, NT, F])
            stage_norm(core, core.X, T)
        stage_route(core, a["L1_ffn_gW"], a["L1_ffn_gb"], a["L1_ffn_eb3"], wf, NE1, 1)
        shared = Net([(a["L1_ffn_sW1"], a["L1_ffn_sb1"], ACT.Relu), (a["L1_ffn_sW2"], a["L1_ffn_sb2"], ACT.Relu),
                      (a["L1_ffn_sW3"], None, None)])
        stage_nets(core, [shared] + [Net([(a["L1_ffn_eW1"][e], a["L1_ffn_eb1"][e], ACT.Relu),
                                          (a["L1_ffn_eW2"][e], a["L1_ffn_eb2"][e], ACT.Relu),
                                          (a["L1_ffn_eW3"][e], None, None)], e) for e in range(NE1)],
                   wf, out_bias=a["L1_ffn_sb3"])


_HOST_T = ("L1_gnn_Wq", "L1_gnn_Wk", "L1_gnn_Wv", "L1_gnn_Wp", "L1_gnn_W1", "L1_gnn_W2")


def stage_store(core, out):
    nc, X = core.nc, core.X
    s_out = core.sem("stored")
    with nc.Block() as block:
        @block.sync
        def _(sp):
            sp.dma_start(out[0:(NT - 1) * P, :].rearrange("(t p) f -> p t f", p=P), X[:, 0:NT - 1, :]).then_inc(s_out, 16)
            sp.dma_start(out[(NT - 1) * P:N, :], X[0:LAST, NT - 1, :]).then_inc(s_out, 16)
            sp.wait_ge(s_out, 32)
    core.stage_ends()


def program(nc, a, out, stop="all"):
    with ExitStack() as ctx:
        core = Core(nc, ctx)
        core.X = core.sb(ctx, "x", [P, NT, F])
        core.XT = core.sb(ctx, "xt", [P, KF, NP + CH])
        core.ident = core.sb(ctx, "identity", [P, P])
        core.ones = core.sb(ctx, "ones", [P, P])
        core.C = nc.dram_tensor("edge_counts", (CELLS + EG * EP + EJ, 1), F32, kind="Internal").ap()
        stage_load(core, a["x"])
        stage_edges(core, a["src"], a["dst"])
        with ExitStack() as c2:
            T = core.sb(c2, "t", [P, NT, F])
            stage_norm(core, core.X, T)
        for layer, H in (("1", F // 32), ("2", 1)):
            with ExitStack() as c2:
                g = Gat(core, c2, H)
                stage_gat_weights(core, g, a["L0_gnn_W" + layer], a["L0_gnn_a_src" + layer], a["L0_gnn_a_dst" + layer], H)
                stage_gat_aggregate(core, g, a["L0_gnn_b" + layer], H)
        stage_back(core)
        if stop != "gat":
            rest(core, a, stop)
        stage_store(core, out)


def kernel(**inputs):
    import numpy as _np
    import concourse.bacc as _bacc
    from concourse import mybir as _mybir
    from concourse.bass_utils import run_bass_kernel_spmd as _run

    nc = _bacc.Bacc("TRN2", target_bir_lowering=False, num_devices=1)
    arrays, args = {}, {}
    for name in inputs:
        v = _np.asarray(inputs[name])
        v = _np.ascontiguousarray(v.T if name in _HOST_T else v)
        arrays[f"in_{name}_dram"] = v
        args[name] = nc.dram_tensor(f"in_{name}_dram", v.shape, _mybir.dt.from_np(v.dtype), kind="ExternalInput").ap()
    out = nc.dram_tensor("out_0_dram", (N, F), _mybir.dt.float32, kind="ExternalOutput").ap()
    program(nc, args, out)
    return _run(nc, [arrays], core_ids=[0]).results[0]["out_0_dram"]
```

```python
from contextlib import ExitStack

import concourse.bass as bass
from concourse import mybir

P = 128
N = 3125
NT = -(-N // P)
NP = NT * P
LAST = N - (NT - 1) * P
F = 256
KF = F // P
HEADS = 8
E = 100000
EP = 125
EJ = E // EP
EG = 8
CELLS = NP * NP
CH = 400
NCH = NP // CH
ST = 5
NL = NT // ST
TC = 5
TN = TC * P
TH = TN // 2
NTC = NT // TC
AHEAD = max(CH, TN)
CLEARED_FIRST = 6
EPS = 1e-5
DUP = 4096.0

F32 = mybir.dt.float32
U32 = mybir.dt.uint32
BF16 = mybir.dt.bfloat16
ALU = mybir.AluOpType
ACT = mybir.ActivationFunctionType
AX = mybir.AxisListType
RMAX = bass.bass_isa.ReduceOp.max


class Chain:

    def __init__(self, eng, sem):
        self.eng, self.sem, self.n, self.base = eng, sem, 0, 0

    def __call__(self, ins):
        ins.then_inc(self.sem, 1)
        self.n += 1
        self.eng.wait_ge(self.sem, self.base + self.n)


class Core:

    def __init__(self, nc, ctx):
        self.nc, self.ctx, self.count, self.used = nc, ctx, 0, []

    def lasting_sem(self, name):
        self.count += 1
        return self.nc.alloc_semaphore(name=f"{name}_{self.count}")

    def sem(self, name):
        self.count += 1
        self.used.append(self.nc.alloc_semaphore(name=f"{name}_{self.count}"))
        return self.used[-1]

    def stage_ends(self):
        for s in self.used:
            self.nc.gpsimd.sem_clear(s)
            self.nc.release_semaphore(s)
        self.used = []

    def sb(self, ctx, name, shape, dt=F32):
        self.count += 1
        return ctx.enter_context(self.nc.sbuf_tensor(f"{name}_{self.count}", shape, dt))

    def ps(self, ctx, name, shape, dt=F32):
        self.count += 1
        return ctx.enter_context(self.nc.psum_tensor(f"{name}_{self.count}", shape, dt))


def clear_counts(core, eng, t0, t1):
    rows = core.C[0:CELLS, 0:1].rearrange("(t p d) o -> t p (d o)", p=P, d=NP)
    for t in range(t0, t1):
        eng.dma_start(rows[t], core.zero[:, :]).then_inc(core.s_clear, 16)


def stage_load(core, x_in):
    nc = core.nc
    X, ident, onescol, zero = core.X, core.ident, core.ones, core.zero
    with ExitStack() as ctx:
        s_zero, s_xpad, s_x, s_id = (core.sem(n) for n in ("zero_made", "x_pad_cleared", "x_in", "ident"))
        with nc.Block() as block:
            @block.sync
            def _(sp):
                sp.wait_ge(s_xpad, 1)
                sp.dma_start(X[:, 0:NT - 1, :], x_in[0:(NT - 1) * P, :].rearrange("(t p) f -> p t f", p=P)).then_inc(s_x, 16)
                sp.dma_start(X[0:LAST, NT - 1, :], x_in[(NT - 1) * P:N, :]).then_inc(s_x, 16)
                sp.wait_ge(s_zero, 1)
                clear_counts(core, sp, 0, CLEARED_FIRST)
                sp.wait_ge(s_x, 32)

            @block.vector
            def _(dve):
                nc.vector.memset(X[:, NT - 1, :], 0.0).then_inc(s_xpad, 1)
                nc.vector.memset(onescol[:, :], 1.0)
                nc.vector.memset(core.XT[:, :, NP:NP + AHEAD], 0.0)
                nc.vector.memset(zero[:, :], 0.0).then_inc(s_zero, 1)

            @block.gpsimd
            def _(pool):
                nc.gpsimd.memset(ident[:, :], 0.0).then_inc(s_id, 1)
                pool.wait_ge(s_id, 1)
                nc.gpsimd.affine_select(out=ident[:, :], in_=ident[:, :], compare_op=ALU.not_equal, fill=1.0,
                                        base=0, pattern=[[-1, P]], channel_multiplier=1).then_inc(s_id, 1)
    core.stage_ends()


def stage_edges(core, src, dst):
    nc = core.nc
    ident, onesm, C = core.ident, core.ones, core.C
    R = 2
    GN = EJ // EG
    W = EG * EP
    with ExitStack() as ctx:
        ei = core.sb(ctx, "edge_ids", [EP, 2, EJ], mybir.dt.int32)
        ef = core.sb(ctx, "edge_ids_f", [EP, 2, EJ])
        cell = core.sb(ctx, "cell", [EP, EJ + EG])
        spare = core.sb(ctx, "spare", [EP, EG])
        rank = core.sb(ctx, "rank", [EP, EG, W], BF16)
        diag = core.sb(ctx, "diag", [EP, R, W])
        same = core.sb(ctx, "same", [EP, EG, W])
        here = core.sb(ctx, "here", [EP, R, EG])
        cnt = core.sb(ctx, "cnt", [EP, R, EG])
        away = core.sb(ctx, "away", [EP, EG])
        idx = core.sb(ctx, "idx", [EP, R, EG], U32)
        rows = core.ps(ctx, "rows", [EP, R, W // 500, 512])
        s_set = core.sem("diagonal_set")
        s_spare, s_cell, s_rank, s_dve = (core.sem(n) for n in (
            "spare_made", "cells_made", "rank_made", "dve"))
        s_here, s_diag, s_rows, s_idx = ([core.sem(n) for _ in range(R)] for n in (
            "here_made", "diag_made", "rows_made", "idx_made"))
        s_scat = [core.lasting_sem("scattered") for _ in range(R)]
        with nc.Block() as block:
            @block.sync
            def _(sp):
                sp.wait_ge(core.s_clear, 16 * NT)
                loops = bass.AP(C.tensor, 0, [[NP + 1, NP], [1, 1]]).rearrange("(p t) o -> p t o", p=P)
                sp.dma_start(loops, core.ones[:, 0:NT].unsqueeze(2), allow_slow_non_contiguous=True).then_inc(s_set, 16)
                sp.wait_ge(s_set, 16)

            @block.gpsimd
            def _(pool):
                for r, e in enumerate((src, dst)):
                    pool.dma_start(ei[:, r, :], e.rearrange("(p j) -> p j", p=EP)).then_inc(s_scat[r], 16)
                nc.gpsimd.iota(spare[:, :], pattern=[[EP, EG]], base=CELLS, channel_multiplier=1,
                               allow_small_or_imprecise_dtypes=True).then_inc(s_spare, 1)
                nc.gpsimd.memset(rank[:, :, :], 1.0).then_inc(s_rank, 1)
                pool.wait_ge(s_rank, 1)
                nc.gpsimd.affine_select(out=rank[:, :, :], in_=rank[:, :, :], compare_op=ALU.is_ge, fill=DUP,
                                        base=0, pattern=[[-EP, EG], [1, W]], channel_multiplier=-1).then_inc(s_rank, 1)
                pool.wait_ge(s_set, 16)
                with pool.Fori(0, GN // R) as i:
                    for r in range(R):
                        pool.wait_ge(s_idx[r], i + 2)
                        pool.wait_ge(s_scat[r - 1], (i + (r > 0)) * (16 * EG) + 16)
                        bound = pool.snap(i + (CELLS + W - 1 + r))
                        for g in range(EG):
                            nc.gpsimd.indirect_dma_start(
                                out=C[:, :], out_offset=bass.IndirectOffsetOnAxis(idx[:, r, g:g + 1], 0),
                                in_=cnt[:, r, g:g + 1], in_offset=None, bounds_check=bound,
                                compute_op=ALU.add).then_inc(s_scat[r], 16)
                for r in range(R):
                    pool.wait_ge(s_scat[r], GN // R * 16 * EG + 16)

            @block.scalar
            def _(act):
                with act.Fori(0, GN // R) as i:
                    for r in range(R):
                        act.wait_ge(s_here[r], i + 1)
                        act.wait_ge(s_rows[r], i + 1)
                        for g in range(EG):
                            ins = nc.scalar.activation(diag[:, r, g * EP:(g + 1) * EP], ident[0:EP, 0:EP], ACT.Copy,
                                                       scale=here[:, r, g:g + 1])
                        ins.then_inc(s_diag[r], 1)

            @block.tensor
            def _(pe):
                for r in range(R):
                    nc.tensor.sem_inc(s_rows[r], 1)
                with pe.Fori(0, GN // R) as i:
                    for r in range(R):
                        pe.wait_ge(s_diag[r], i + 1)
                        pe.wait_ge(s_idx[r], i + 1)
                        for b in range(0, W, 500):
                            ins = nc.tensor.matmul(rows[:, r, b // 500, 0:500], onesm[0:EP, 0:EP], diag[:, r, b:b + 500],
                                                   start=True, stop=True)
                        ins.then_inc(s_rows[r], 1)

            @block.vector
            def _(dve):
                link = Chain(dve, s_dve)
                for r in range(R):
                    nc.vector.sem_inc(s_idx[r], 1)
                    dve.wait_ge(s_scat[r], 16)
                link(nc.vector.tensor_copy(ef[:, :, :], ei[:, :, :]))
                nc.vector.memset(cell[:, EJ:EJ + EG], 0.0).then_inc(s_cell, 1)
                nc.vector.scalar_tensor_tensor(out=cell[:, 0:EJ], in0=ef[:, 0, :], scalar=float(NP), in1=ef[:, 1, :],
                                               op0=ALU.mult, op1=ALU.add).then_inc(s_cell, 1)
                dve.wait_ge(s_cell, 2)
                dve.wait_ge(s_rank, 2)
                dve.wait_ge(s_spare, 1)
                nc.vector.tensor_copy(here[:, 0, :], cell[:, 0:EG]).then_inc(s_here[0], 1)
                with dve.Fori(0, GN // R) as i:
                    link.n, link.base = 0, i * (R * 3) + 1
                    for r in range(R):
                        q = (r + 1) % R
                        dve.wait_ge(s_idx[q], i + 1 + (q == 0))
                        nc.vector.tensor_copy(here[:, q, :], cell[:, bass.ds((i * R + r + 1) * EG, EG)]).then_inc(s_here[q], 1)
                        dve.wait_ge(s_here[r], i + 1)
                        dve.wait_ge(s_rows[r], i + 2)
                        dve.wait_ge(s_scat[r], i * (16 * EG) + 16)
                        for g in range(EG):
                            ins = nc.vector.scalar_tensor_tensor(
                                out=same[:, g, :].rearrange("p (b w) -> p b w", w=500), in0=rows[:, r, :, 0:500], scalar=here[:, r, g:g + 1],
                                in1=rank[:, g, :].rearrange("p (b w) -> p b w", w=500),
                                op0=ALU.is_equal, op1=ALU.mult, accum_out=cnt[:, r, g:g + 1])
                        link(ins)
                        link(nc.vector.tensor_tensor(away[:, :], spare[:, :], here[:, r, :], ALU.subtract))
                        link(nc.vector.scalar_tensor_tensor(out=away[:, :], in0=cnt[:, r, :], scalar=DUP, in1=away[:, :],
                                                            op0=ALU.is_ge, op1=ALU.mult))
                        nc.vector.tensor_tensor(idx[:, r, :], away[:, :], here[:, r, :], ALU.add).then_inc(s_idx[r], 1)
    core.stage_ends()


def stage_norm(core, src, dst, gamma=None, beta=None, times=1, park=None):
    nc, XT, ident = core.nc, core.XT, core.ident
    with ExitStack() as ctx:
        stats = core.sb(ctx, "stats", [P, NT, 6])
        mv = core.sb(ctx, "mean_and_variance", [P, NT, 2])
        std = core.sb(ctx, "std", [P, NT])
        gb = core.sb(ctx, "gamma_beta", [P, 2, KF])
        flip = core.ps(ctx, "flip", [P, 8, 512])
        s_gb, s_stats, s_dve, s_std, s_norm, s_flip, s_park = (core.sem(n) for n in (
            "gamma_in", "stats_made", "dve", "std_made", "tile_normed", "flipped", "parked"))
        s_evac = [core.sem("evacuated_by_vector"), core.sem("evacuated_by_scalar")]
        turns = [(k, t0, min(4, NT - t0)) for t0 in range(0, NT, 4) for k in range(KF)]

        def evacuate(eng, mine):
            if gamma is not None:
                eng.wait_ge(s_gb, 32)
            for n, (k, t0, m) in enumerate(turns):
                if n % 2 != mine:
                    continue
                eng.wait_ge(s_flip, n + 1)
                out, bank = XT[:, k, t0 * P:(t0 + m) * P], flip[:, n % 8, 0:m * P]
                if gamma is None:
                    ins = nc.scalar.copy(out, bank) if mine else nc.vector.tensor_copy(out, bank)
                elif mine:
                    ins = nc.scalar.activation(out, bank, ACT.Identity, scale=gb[:, 0, k:k + 1], bias=gb[:, 1, k:k + 1])
                else:
                    ins = nc.vector.tensor_scalar(out, bank, gb[:, 0, k:k + 1], gb[:, 1, k:k + 1], ALU.mult, ALU.add)
                ins.then_inc(s_evac[mine], 1)

        with nc.Block() as block:
            @block.sync
            def _(sp):
                if gamma is not None:
                    with nc.allow_non_contiguous_dma(reason="feature columns"):
                        for r, row in enumerate((gamma, beta)):
                            sp.dma_start(gb[:, r, :], row.rearrange("(k p) -> p k", p=P)).then_inc(s_gb, 16)
                    sp.wait_ge(s_gb, 32)
                if park is not None:
                    sp.dma_start(park[1], src[:, :, :]).then_inc(s_park, 16)
                    sp.wait_ge(s_norm, NT * times)
                    sp.dma_start(park[0], dst[:, :, :]).then_inc(s_park, 16)
                    sp.wait_ge(s_park, 32)

            @block.vector
            def _(dve):
                link = Chain(dve, s_dve)
                a = src
                for n in range(times):
                    for t in range(NT):
                        if n:
                            dve.wait_ge(s_norm, (n - 1) * NT + t + 1)
                        nc.vector.bn_stats(out=stats[:, t, :], in_=a[:, t, :]).then_inc(s_stats, 1)
                    for t in range(NT):
                        dve.wait_ge(s_stats, n * NT + t + 1)
                        ins = nc.vector.bn_aggr(out=mv[:, t, :], in_=stats[:, t, :])
                    link(ins)
                    link(nc.vector.tensor_scalar(std[:, :], mv[:, :, 1], EPS, None, ALU.add))
                    dve.wait_ge(s_std, n + 1)
                    link(nc.vector.reciprocal(std[:, :], std[:, :]))
                    for t in range(NT):
                        nc.vector.tensor_scalar(dst[:, t, :], a[:, t, :], mv[:, t, 0:1], std[:, t:t + 1],
                                                ALU.subtract, ALU.mult).then_inc(s_norm, 1)
                    a = dst
                evacuate(dve, 0)

            @block.scalar
            def _(act):
                for n in range(times):
                    act.wait_ge(s_dve, 3 * n + 2)
                    nc.scalar.activation(std[:, :], std[:, :], ACT.Sqrt).then_inc(s_std, 1)
                evacuate(act, 1)

            @block.tensor
            def _(pe):
                for n, (k, t0, m) in enumerate(turns):
                    pe.wait_ge(s_norm, (times - 1) * NT + t0 + m)
                    if n >= 8:
                        pe.wait_ge(s_evac[n % 2], (n - 8) // 2 + 1)
                    for j in range(m):
                        ins = nc.tensor.transpose(flip[:, n % 8, j * P:(j + 1) * P], dst[:, t0 + j, k * P:(k + 1) * P],
                                                  ident[:, :])
                    ins.then_inc(s_flip, 1)
    core.stage_ends()


def stage_gat_weights(core, g, W, a_src, a_dst, H, clear=False):
    nc, XT = core.nc, core.XT
    D = F // H
    R = g.rep
    wx, wdb, msg, kap, bias = g.wx, g.wdb, g.msg, g.kap, g.bias
    with ExitStack() as ctx:
        h = core.sb(ctx, "h", [P, NT, F + H])
        ab = core.sb(ctx, "a_rows", [P, 2, F])
        wa = core.sb(ctx, "w_times_a", [P, KF, F])
        wd = core.sb(ctx, "w_dst", [P, KF, H])
        es = core.sb(ctx, "es", [P, NT, H])
        pad = core.sb(ctx, "pad", [P, NT])
        top = core.sb(ctx, "top", [P, H])
        allm = core.sb(ctx, "greatest", [P, H])
        av = core.sb(ctx, "a_factor", [P, NT, H])
        bA = core.sb(ctx, "bias_a", [P, H])
        proj = core.ps(ctx, "proj", [P, 8, 512])
        s_w, s_dve, s_wx, s_proj, s_h, s_pad, s_top, s_all, s_bias, s_exp = (core.sem(n) for n in (
            "w_in", "dve", "wx_made", "projected", "h_made", "pad_made", "top_made", "greatest_made", "bias_made", "exp_made"))
        with nc.Block() as block:
            @block.sync
            def _(sp):
                sp.dma_start(wx[:, :, 0:F], W.rearrange("(k p) n -> p k n", p=P)).then_inc(s_w, 16)
                for k, row in enumerate((a_src, a_dst)):
                    sp.dma_start(ab[:, k, :], row.rearrange("h d -> (h d)").partition_broadcast(P)).then_inc(s_w, 16)
                if clear:
                    clear_counts(core, sp, CLEARED_FIRST, NT)
                sp.wait_ge(s_w, 48)

            @block.gpsimd
            def _(pool):
                nc.gpsimd.memset(pad[:, :], 0.0).then_inc(s_pad, 1)
                pool.wait_ge(s_pad, 1)
                nc.gpsimd.affine_select(out=pad[:, :], in_=pad[:, :], compare_op=ALU.is_ge, fill=-1e30, base=N - 1,
                                        pattern=[[-P, NT]], channel_multiplier=-1).then_inc(s_pad, 1)
                pool.wait_ge(s_top, 1)
                nc.gpsimd.partition_all_reduce(allm[:, :], top[:, :], P, RMAX).then_inc(s_all, 1)

            @block.vector
            def _(dve):
                link = Chain(dve, s_dve)
                dve.wait_ge(s_w, 48)
                for k, out in ((0, wx[:, :, F:F + H]), (1, wd[:, :, :])):
                    link(nc.vector.tensor_tensor(wa[:, :, :], wx[:, :, 0:F], ab[:, k:k + 1, :].to_broadcast([P, KF, F]), ALU.mult))
                    link(nc.vector.tensor_reduce(out, wa[:, :, :].rearrange("p k (h d) -> p k h d", h=H), AX.X, ALU.add))
                nc.vector.tensor_copy(wdb[:, :, :, :], wd[:, :, :].unsqueeze(3).to_broadcast([P, KF, H, P])).then_inc(s_wx, 1)
                dve.wait_ge(s_h, NT)
                dve.wait_ge(s_pad, 2)
                link(nc.vector.tensor_tensor(es[:, :, :], h[:, :, F:F + H], pad[:, :].unsqueeze(2).to_broadcast([P, NT, H]), ALU.add))
                nc.vector.tensor_reduce(top[:, :], es[:, :, :].rearrange("p t h -> p h t"), AX.X, ALU.max).then_inc(s_top, 1)
                dve.wait_ge(s_all, 1)
                link(nc.vector.tensor_tensor(es[:, :, :], h[:, :, F:F + H], allm[:, :].unsqueeze(1).to_broadcast([P, NT, H]), ALU.min))
                link(nc.vector.tensor_scalar(bA[:, :], allm[:, :], -0.2, BIAS_A, ALU.mult, ALU.add))
                nc.vector.tensor_scalar(bias[:, :], allm[:, :], -0.8, BIAS_K, ALU.mult, ALU.add).then_inc(s_bias, 1)
                dve.wait_ge(s_exp, 2 * H)
                m = msg[:, :, :, 0:D]
                link(nc.vector.tensor_tensor(m, h[:, :, 0:F].rearrange("p t (h d) -> p t h d", h=H),
                                             av[:, :, :].unsqueeze(3).to_broadcast([P, NT, H, D]), ALU.mult))
                link(nc.vector.tensor_copy(msg[:, :, :, D:D + R], av[:, :, :].unsqueeze(3).to_broadcast([P, NT, H, R])))

            @block.scalar
            def _(act):
                for t in range(NT):
                    act.wait_ge(s_proj, t + 1)
                    nc.scalar.copy(h[:, t, :], proj[:, t % 8, 0:F + H]).then_inc(s_h, 1)
                act.wait_ge(s_bias, 1)
                for j in range(H):
                    nc.scalar.activation(av[:, :, j], es[:, :, j], ACT.Exp, bias=bA[:, j:j + 1], scale=0.2).then_inc(s_exp, 1)
                    nc.scalar.activation(kap[:, :, j], es[:, :, j], ACT.Exp, bias=bias[:, j:j + 1], scale=0.8).then_inc(s_exp, 1)

            @block.tensor
            def _(pe):
                pe.wait_ge(s_wx, 1)
                for t in range(NT):
                    if t >= 8:
                        pe.wait_ge(s_h, t - 7)
                    for k in range(KF):
                        ins = nc.tensor.matmul(proj[:, t % 8, 0:F + H], XT[:, k, t * P:(t + 1) * P], wx[:, k, :],
                                               start=(k == 0), stop=(k == KF - 1))
                    ins.then_inc(s_proj, 1)
    core.stage_ends()


BIAS_A = 30.0
BIAS_K = 35.0
RHO_MAX = 1.5860134523134308e15


def load_counts(core, sp, cbuf, s_c, s_used, per, start=0):
    nc, C = core.nc, core.C
    rows = C[0:CELLS, 0:1].rearrange("(l t p d) o -> l p t (d o)", t=ST, p=P, d=NP)

    def load(slot, part, cols):
        sp.dma_start(cbuf[:, slot, :, :], rows[part][:, :, cols]).then_inc(s_c[slot], 16)

    def round_of_two(i, parts):
        for m in parts:
            sp.wait_ge(s_used, i * 2 * per + (m + 1) * (per // NL) + start)
            n = m + 2
            load(n % 2, n % NL, bass.ds((2 * i + n // NL) * CH, CH))

    for n in range(2):
        load(n, n, slice(0, CH))
    with sp.Fori(0, NCH // 2 - 1) as i:
        round_of_two(i, range(2 * NL))
    round_of_two(NCH // 2 - 1, range(2 * NL - 2))


def wait_counts(eng, s_c, i, u, part):
    n = u * NL + part
    eng.wait_ge(s_c[n % 2], (i * NL + n // 2 + 1) * 16)


def stage_gat_aggregate(core, g, b, H):
    nc, XT = core.nc, core.XT
    D = F // H
    WR = 8
    RB = 4
    MR = 4
    per = NT * H
    others = (3, 7)
    mine = [j for j in range(H) if j not in others]
    NO, ND = len(others), len(mine)
    STACK_AT, DIVIDE_AT, ELU_AT, ADD_AT, ROW_AT, RHO_AT = 1, 10, 17, 21, 5, 7
    msg, kap, bias, wdb = g.msg, g.kap, g.bias, g.wdb
    with ExitStack() as ctx:
        cbuf = core.sb(ctx, "counts", [P, 2, ST, CH])
        rho = core.sb(ctx, "rho", [P, 2, H, CH])
        w = core.sb(ctx, "weights", [P, WR, CH])
        sums = core.sb(ctx, "sums", [P, 4, CH])
        den = core.sb(ctx, "denominators", [P, KF, CH])
        y = core.sb(ctx, "y", [P, KF, CH])
        ey = core.sb(ctx, "exp_y", [P, KF, CH])
        bcol = core.sb(ctx, "bias_cols", [P, KF])
        less = core.sb(ctx, "minus_one", [P, 1])
        nkap = core.sb(ctx, "minus_kappa", [P, NT, H])
        mx = core.sb(ctx, "maxima", [P, MR, CH])
        acc = core.ps(ctx, "acc", [P, 4, 512])
        row = core.ps(ctx, "row", [P, 4, 512])
        s_c = [core.sem("counts_in") for _ in range(2)]
        s_b, s_set, s_relu, s_mx, s_wo, s_row, s_exp, s_rho, s_w, s_used, s_free, s_den, s_div, s_act, s_ey, s_y = (
            core.sem(n) for n in (
                "bias_in", "constants_set", "relu_made", "maxima_made", "other_w_made", "rows_made", "rho_raw",
                "rho_made", "w_made", "w_used", "acc_read", "stacked", "divided", "act", "exp_y_made", "y_done"))

        def make_row(j, cols):
            for k in range(KF):
                ins = nc.tensor.matmul(row[:, j % RB, 0:CH], wdb[:, k, j, :], XT[:, k, cols], start=(k == 0), stop=(k == KF - 1))
            ins.then_inc(s_row, 1)

        def make_rho(j, u):
            nc.scalar.activation(rho[:, u, j, :], row[:, j % RB, 0:CH], ACT.Exp, bias=bias[:, j:j + 1],
                                 scale=-0.8).then_inc(s_exp, 1)

        def bound_rho(u):
            nc.vector.tensor_scalar(rho[:, u, :, :], rho[:, u, :, :], RHO_MAX, None, ALU.min).then_inc(s_rho, 1)

        def stack(m):
            j = m % H
            r = D * (j % 4)
            o = 64 * (j % 2) + D * (m < H)
            to = den if m < H else y
            nc.scalar.copy(to[r:r + D, j // 4, :], sums[o:o + D, j // 2, :]).then_inc(s_den, 1)

        def divide(dve, m, c):
            if m == 0:
                dve.wait_ge(s_den, (c + 1) * (2 * H))
            if m < 4:
                part = den[:, m // 2, m % 2 * (CH // 2):(m % 2 + 1) * (CH // 2)]
                nc.vector.reciprocal(part, part).then_inc(s_div, 1)
            else:
                dve.wait_ge(s_div, c * 5 + 4)
                nc.vector.tensor_tensor(y[:, :, :], y[:, :, :], den[:, :, :], ALU.mult).then_inc(s_div, 1)

        def elu_parts(act, c):
            link = Chain(act, s_act)
            link.base = c * 4
            act.wait_ge(s_div, c * 5 + 5)
            for k in range(KF):
                ins = nc.scalar.activation(y[:, k, :], y[:, k, :], ACT.Identity, bias=bcol[:, k:k + 1])
            link(ins)
            link(nc.scalar.activation(ey[:, :, :], y[:, :, :], ACT.Relu, scale=-1.0))
            link(nc.scalar.activation(y[:, :, :], y[:, :, :], ACT.Relu))
            link(nc.scalar.activation(y[:, :, :], y[:, :, :], ACT.Identity, bias=less[:, 0:1]))
            nc.scalar.activation(ey[:, :, :], ey[:, :, :], ACT.Exp, scale=-1.0).then_inc(s_ey, 1)

        def add_parts(pool, c):
            pool.wait_ge(s_ey, c + 1)
            nc.gpsimd.tensor_tensor(core.XT_all[:, :, bass.ds(c * CH, CH)], y[:, :, :], ey[:, :, :], ALU.add).then_inc(s_y, 1)

        with nc.Block() as block:
            @block.sync
            def _(sp):
                sp.dma_start(bcol[:, :], b.rearrange("(k p) -> p k", p=P), allow_slow_non_contiguous=True).then_inc(s_b, 16)
                load_counts(core, sp, cbuf, s_c, s_used, per, WR)

            @block.tensor
            def _(pe):
                nc.tensor.sem_inc(s_used, WR)
                for j in range(H):
                    if j >= RB:
                        pe.wait_ge(s_exp, j - RB + 2)
                    make_row(j, slice(0, CH))
                with pe.Fori(0, NCH // 2) as i:
                    for u in range(2):
                        c = 2 * i + u
                        for n in range(per):
                            t, j = n // H, n % H
                            if j == 0 and 0 <= t - ROW_AT < H:
                                pe.wait_ge(s_exp, (c + 1) * H + (t - ROW_AT) - RB + 2)
                                make_row(t - ROW_AT, bass.ds((c + 1) * CH, CH))
                            if t == 0 and j % 2 == 0:
                                pe.wait_ge(s_free, c * 4 + j // 2 + 1)
                            if j in others:
                                pe.wait_ge(s_wo, (c * NT + t) * NO + others.index(j) + 2)
                            else:
                                pe.wait_ge(s_w, (c * NT + t) * ND + mine.index(j) + 2)
                            o = 64 * (j % 2)
                            nc.tensor.matmul(acc[o:o + 64, j // 2, 0:CH], msg[:, t, j, :], w[:, n % WR, :],
                                             start=(t == 0), stop=(t == NT - 1)).then_inc(s_used, 1)

            @block.scalar
            def _(act):
                nc.scalar.sem_inc(s_exp, 1)
                nc.scalar.sem_inc(s_free, 4)
                act.wait_ge(s_b, 16)
                act.wait_ge(s_set, 3)
                for j in range(H):
                    act.wait_ge(s_row, j + 1)
                    make_rho(j, 0)
                with act.Fori(0, NCH // 2) as i:
                    for u in range(2):
                        c = 2 * i + u
                        act.wait_ge(s_w, c * NT * ND + 1)
                        act.wait_ge(s_rho, c + 1)
                        for t in range(NT):
                            for q, j in enumerate(others):
                                m = t * NO + q
                                act.wait_ge(s_wo, c * NT * NO + max(m - MR, -1) + 2)
                                nc.scalar.activation(mx[:, m % MR, :], rho[:, u, j, :], ACT.Relu, bias=nkap[:, t, j:j + 1]
                                                     ).then_inc(s_relu, 1)
                                act.wait_ge(s_relu, c * NT * NO + m + 1)
                                nc.scalar.activation(mx[:, m % MR, :], mx[:, m % MR, :], ACT.Identity, bias=kap[:, t, j:j + 1]
                                                     ).then_inc(s_mx, 1)
                            if t == STACK_AT:
                                act.wait_ge(s_free, c * 4 + 4)
                                act.wait_ge(s_y, c + 1)
                            if 0 <= t - STACK_AT < H:
                                stack(2 * (t - STACK_AT))
                                stack(2 * (t - STACK_AT) + 1)
                            if 0 <= t - RHO_AT < H:
                                act.wait_ge(s_row, (c + 1) * H + (t - RHO_AT) + 1)
                                make_rho(t - RHO_AT, 1 - u)
                            if t == ELU_AT:
                                elu_parts(act, c)
                        act.wait_ge(s_den, (c + 1) * (2 * H))
                        for q in range(4):
                            act.wait_ge(s_used, WR + c * per + (NT - 1) * H + 2 * q + 2)
                            nc.scalar.copy(sums[:, q, :], acc[:, q, 0:CH]).then_inc(s_free, 1)
                act.wait_ge(s_free, NCH * 4 + 4)
                act.wait_ge(s_y, NCH + 1)
                for m in range(2 * H):
                    stack(m)
                elu_parts(act, NCH)

            @block.gpsimd
            def _(pool):
                nc.gpsimd.sem_inc(s_y, 1)
                nc.gpsimd.sem_inc(s_wo, 1)
                with pool.Fori(0, NCH // 2) as i:
                    for u in range(2):
                        c = 2 * i + u
                        for t in range(NT):
                            for q, j in enumerate(others):
                                m, n = t * NO + q, t * H + j
                                if q == 0 and t % ST == 0:
                                    wait_counts(pool, s_c, i, u, t // ST)
                                pool.wait_ge(s_mx, c * NT * NO + m + 1)
                                pool.wait_ge(s_used, c * per + n + 1)
                                nc.gpsimd.tensor_tensor(w[:, n % WR, :], mx[:, m % MR, :], cbuf[:, (u * NL + t // ST) % 2, t % ST, :],
                                                        ALU.mult).then_inc(s_wo, 1)
                            if t == ADD_AT:
                                add_parts(pool, c)
                add_parts(pool, NCH)
                pool.wait_ge(s_y, NCH + 2)

            @block.vector
            def _(dve):
                nc.vector.sem_inc(s_w, 1)
                nc.vector.memset(less[:, :], -1.0).then_inc(s_set, 1)
                nc.vector.memset(sums[:, :, :], 1.0).then_inc(s_set, 1)
                nc.vector.tensor_scalar(nkap[:, :, :], kap[:, :, :], -1.0, None, ALU.mult).then_inc(s_set, 1)
                dve.wait_ge(s_exp, H + 1)
                bound_rho(0)
                with dve.Fori(0, NCH // 2) as i:
                    for u in range(2):
                        c = 2 * i + u
                        dve.wait_ge(s_rho, c + 1)
                        for n in range(per):
                            t, j = n // H, n % H
                            if n % (H * ST) == 0:
                                wait_counts(dve, s_c, i, u, t // ST)
                            if j == 0 and 0 <= t - DIVIDE_AT < 5:
                                divide(dve, t - DIVIDE_AT, c)
                            if j in others:
                                continue
                            dve.wait_ge(s_used, c * per + n + 1)
                            nc.vector.scalar_tensor_tensor(out=w[:, n % WR, :], in0=rho[:, u, j, :], scalar=kap[:, t, j:j + 1],
                                                           in1=cbuf[:, (u * NL + t // ST) % 2, t % ST, :],
                                                           op0=ALU.max, op1=ALU.mult).then_inc(s_w, 1)
                        dve.wait_ge(s_exp, (c + 2) * H + 1)
                        bound_rho(1 - u)
                for m in range(5):
                    divide(dve, m, NCH)
                dve.wait_ge(s_rho, NCH + 1)
    core.stage_ends()


class Gat:

    def __init__(self, core, ctx, H):
        D = F // H
        self.rep = 1 if H == 1 else D
        self.wx = core.sb(ctx, "wx", [P, KF, F + H])
        self.wdb = core.sb(ctx, "w_dst_columns", [P, KF, H, P])
        self.msg = core.sb(ctx, "messages", [P, NT, H, D + self.rep])
        self.kap = core.sb(ctx, "kappa", [P, NT, H])
        self.bias = core.sb(ctx, "bias_k", [P, H])


def stage_gat_one_head(core, g, b):
    nc, XT, X = core.nc, core.XT, core.X
    WR = 6
    ROW_AT = 18
    msg, kap, bias, wdb = g.msg, g.kap, g.bias, g.wdb
    with ExitStack() as ctx:
        cbuf = core.sb(ctx, "counts", [P, NL, ST, TN])
        rho = core.sb(ctx, "rho", [P, 2, TH])
        w = core.sb(ctx, "weights", [P, WR, TN])
        inv = core.sb(ctx, "inv", [P, TC])
        y = core.sb(ctx, "y", [P, TC, F])
        ey = core.sb(ctx, "exp_y", [P, TC, F])
        brow = core.sb(ctx, "bias_row", [P, F])
        less = core.sb(ctx, "minus_one", [P, 1])
        acc = core.ps(ctx, "acc", [P, TC, 512])
        row = core.ps(ctx, "row", [P, 2, 512])
        s_c = [core.sem("counts_in") for _ in range(NL)]
        s_b, s_less, s_row, s_exp, s_rho, s_w, s_used, s_inv, s_raw, s_act, s_ey, s_elu, s_y = (core.sem(n) for n in (
            "bias_in", "minus_one_set", "row_made", "rho_raw", "rho_made", "w_made", "w_used", "inv_made", "acc_read",
            "act", "exp_y_made", "elu_made", "y_done"))

        def make_row(first):
            for h in range(2):
                for k in range(KF):
                    ins = nc.tensor.matmul(row[:, h, 0:TH], wdb[:, k, 0, :], XT[:, k, bass.ds(first + h * TH, TH)],
                                           start=(k == 0), stop=(k == KF - 1))
            ins.then_inc(s_row, 1)

        def make_rho():
            nc.scalar.activation(rho[:, :, :], row[:, :, 0:TH], ACT.Exp, bias=bias[:, 0:1], scale=-0.8).then_inc(s_exp, 1)

        def bound_rho():
            nc.vector.tensor_scalar(rho[:, :, :], rho[:, :, :], RHO_MAX, None, ALU.min).then_inc(s_rho, 1)

        with nc.Block() as block:
            @block.sync
            def _(sp):
                rows = core.C[0:CELLS, 0:1].rearrange("(l t p d) o -> l p t (d o)", t=ST, p=P, d=NP)
                sp.dma_start(brow[:, :], b.partition_broadcast(P)).then_inc(s_b, 16)
                for n in range(NL):
                    sp.dma_start(cbuf[:, n, :, :], rows[n][:, :, 0:TN]).then_inc(s_c[n], 16)
                with sp.Fori(1, NTC) as i:
                    for n in range(NL):
                        sp.wait_ge(s_used, i * NT - NT + ST * (n + 1))
                        sp.dma_start(cbuf[:, n, :, :], rows[n][:, :, bass.ds(i * TN, TN)]).then_inc(s_c[n], 16)

            @block.tensor
            def _(pe):
                make_row(0)
                with pe.Fori(0, NTC) as i:
                    pe.wait_ge(s_raw, i + 1)
                    for t in range(NT):
                        if t == ROW_AT:
                            pe.wait_ge(s_exp, i + 1)
                            make_row((i + 1) * TN)
                        pe.wait_ge(s_w, i * NT + t + 1)
                        for d in range(TC):
                            ins = nc.tensor.matmul(acc[:, d, 0:F + 1], w[:, t % WR, d * P:(d + 1) * P], msg[:, t, 0, :],
                                                   start=(t == 0), stop=(t == NT - 1))
                        ins.then_inc(s_used, 1)

            @block.scalar
            def _(act):
                link = Chain(act, s_act)
                act.wait_ge(s_less, 1)
                act.wait_ge(s_row, 1)
                make_rho()
                with act.Fori(0, NTC) as i:
                    act.wait_ge(s_row, i + 2)
                    act.wait_ge(s_w, (i + 1) * NT)
                    make_rho()
                    link.n, link.base = 0, i * 3
                    act.wait_ge(s_raw, i + 2)
                    link(nc.scalar.activation(ey[:, :, :], y[:, :, :], ACT.Relu, scale=-1.0))
                    link(nc.scalar.activation(y[:, :, :], y[:, :, :], ACT.Relu))
                    link(nc.scalar.activation(y[:, :, :], y[:, :, :], ACT.Identity, bias=less[:, 0:1]))
                    nc.scalar.activation(ey[:, :, :], ey[:, :, :], ACT.Exp, scale=-1.0).then_inc(s_ey, 1)

            @block.gpsimd
            def _(pool):
                nc.gpsimd.sem_inc(s_y, 1)
                nc.gpsimd.memset(less[:, :], -1.0).then_inc(s_less, 1)
                with pool.Fori(0, NTC) as i:
                    pool.wait_ge(s_ey, i + 1)
                    nc.gpsimd.tensor_tensor(y[:, :, :], y[:, :, :], ey[:, :, :], ALU.add).then_inc(s_elu, 1)
                    pool.wait_ge(s_elu, i + 1)
                    nodes = X[:, bass.ds(i * TC, TC), :]
                    nc.gpsimd.tensor_tensor(nodes, nodes, y[:, :, :], ALU.add).then_inc(s_y, 1)
                pool.wait_ge(s_y, NTC + 1)

            @block.vector
            def _(dve):
                nc.vector.sem_inc(s_raw, 1)
                dve.wait_ge(s_b, 16)
                dve.wait_ge(s_exp, 1)
                bound_rho()
                with dve.Fori(0, NTC) as i:
                    dve.wait_ge(s_rho, i + 1)
                    for t in range(NT):
                        if t % ST == 0:
                            dve.wait_ge(s_c[t // ST], (i + 1) * 16)
                        if t >= WR:
                            dve.wait_ge(s_used, i * NT + t - WR + 1)
                        nc.vector.scalar_tensor_tensor(out=w[:, t % WR, :], in0=rho[:, :, :].rearrange("p h d -> p (h d)"),
                                                       scalar=kap[:, t, 0:1], in1=cbuf[:, t // ST, t % ST, :],
                                                       op0=ALU.max, op1=ALU.mult).then_inc(s_w, 1)
                    dve.wait_ge(s_exp, i + 2)
                    bound_rho()
                    dve.wait_ge(s_y, i + 1)
                    dve.wait_ge(s_used, (i + 1) * NT)
                    nc.vector.reciprocal(inv[:, :], acc[:, :, F]).then_inc(s_inv, 1)
                    dve.wait_ge(s_inv, i + 1)
                    for d in range(TC):
                        ins = nc.vector.scalar_tensor_tensor(out=y[:, d, :], in0=acc[:, d, 0:F], scalar=inv[:, d:d + 1],
                                                             in1=brow[:, :], op0=ALU.mult, op1=ALU.add)
                    ins.then_inc(s_raw, 1)
                dve.wait_ge(s_rho, NTC + 1)
    core.stage_ends()


def stage_ones_off(core):
    nc, C = core.nc, core.C
    with ExitStack() as ctx:
        d = core.sb(ctx, "diagonal", [P, NT])
        s_in, s_sub, s_out = core.sem("diag_in"), core.sem("diag_less"), core.sem("diag_out")
        diag = bass.AP(C.tensor, 0, [[NP + 1, NP], [1, 1]]).rearrange("(p t) o -> p t o", p=P)
        with nc.Block() as block:
            @block.sync
            def _(sp):
                sp.dma_start(d[:, :].unsqueeze(2), diag, allow_slow_non_contiguous=True).then_inc(s_in, 16)
                sp.wait_ge(s_sub, 1)
                sp.dma_start(diag, d[:, :].unsqueeze(2), allow_slow_non_contiguous=True).then_inc(s_out, 16)
                sp.wait_ge(s_out, 16)

            @block.vector
            def _(dve):
                dve.wait_ge(s_in, 16)
                nc.vector.tensor_scalar(d[:, :], d[:, :], -1.0, None, ALU.add).then_inc(s_sub, 1)
    core.stage_ends()


def top_two(nc, link, L, E_, vals, ids, idf, iota, w, wf, hot, exp_pair):
    for t in range(NT):
        ins = nc.vector.max(vals[:, t, :], L[:, t, :])
    link(ins)
    for t in range(NT):
        ins = nc.vector.max_index(ids[:, t, :], vals[:, t, :], L[:, t, :])
    link(ins)
    link(nc.vector.tensor_copy(idf[:, :, :], ids[:, :, 0:2]))
    link(nc.vector.tensor_tensor(w[:, :, :], vals[:, :, 0:2], vals[:, :, 0:1].to_broadcast([P, NT, 2]), ALU.subtract))
    exp_pair(w)
    link(nc.vector.tensor_reduce(vals[:, :, 7], w[:, :, :], AX.X, ALU.add))
    link(nc.vector.reciprocal(vals[:, :, 6], vals[:, :, 7]))
    link(nc.vector.tensor_tensor(w[:, :, :], w[:, :, :], vals[:, :, 6:7].to_broadcast([P, NT, 2]), ALU.mult))
    for j in range(2):
        link(nc.vector.tensor_tensor(hot[:, j, :, :], iota[:, :].unsqueeze(1).to_broadcast([P, NT, E_]),
                                     idf[:, :, j:j + 1].to_broadcast([P, NT, E_]), ALU.is_equal))
        link(nc.vector.tensor_tensor(hot[:, j, :, :], hot[:, j, :, :], w[:, :, j:j + 1].to_broadcast([P, NT, E_]), ALU.mult))
    link(nc.vector.tensor_tensor(wf[:, :, :], hot[:, 0, :, :], hot[:, 1, :, :], ALU.add))


def stage_route(core, Wr, br, b2, wf, E_, softmax_first):
    nc, XT, X, ident = core.nc, core.XT, core.X, core.ident
    EL = 8
    with ExitStack() as ctx:
        wr = core.sb(ctx, "w_router", [P, KF, E_])
        brb = core.sb(ctx, "b_router", [P, E_])
        b2s = core.sb(ctx, "b_out", [E_, F])
        L = core.sb(ctx, "logits", [P, NT, EL])
        vals = core.sb(ctx, "vals", [P, NT, 8])
        ids = core.sb(ctx, "ids", [P, NT, 8], U32)
        idf = core.sb(ctx, "ids_f", [P, NT, 2])
        iota = core.sb(ctx, "iota", [P, E_])
        w = core.sb(ctx, "pair", [P, NT, 2])
        hot = core.sb(ctx, "hot", [P, 2, NT, E_])
        one = core.sb(ctx, "per_node", [P, 2, NT])
        wft = core.sb(ctx, "weights_t", [E_, NT, P])
        lg = core.ps(ctx, "logits_ps", [P, 512])
        tp = core.ps(ctx, "flip", [P, 7, 512])
        s_w, s_lg, s_dve, s_pair, s_e, s_iota, s_wf, s_tp, s_wft, s_bias, s_add = (core.sem(n) for n in (
            "w_in", "logits_made", "dve", "pair_made", "exp_made", "iota", "wf_made", "flipped", "wft_made", "bias_made", "added"))
        with nc.Block() as block:
            @block.sync
            def _(sp):
                sp.dma_start(wr[:, :, :], Wr.rearrange("(k p) e -> p k e", p=P)).then_inc(s_w, 16)
                sp.dma_start(brb[:, :], br.partition_broadcast(P)).then_inc(s_w, 16)
                sp.dma_start(b2s[:, :], b2).then_inc(s_w, 16)
                sp.wait_ge(s_w, 48)

            @block.gpsimd
            def _(pool):
                nc.gpsimd.iota(iota[:, :], pattern=[[1, E_]], base=0, channel_multiplier=0,
                               allow_small_or_imprecise_dtypes=True).then_inc(s_iota, 1)

            @block.tensor
            def _(pe):
                pe.wait_ge(s_w, 48)
                for t in range(NT):
                    for k in range(KF):
                        ins = nc.tensor.matmul(lg[:, t * E_:(t + 1) * E_], XT[:, k, t * P:(t + 1) * P], wr[:, k, :],
                                               start=(k == 0), stop=(k == KF - 1))
                ins.then_inc(s_lg, 1)
                pe.wait_ge(s_wf, 1)
                for t in range(NT):
                    ins = nc.tensor.transpose(tp[0:E_, t // 4, (t % 4) * P:(t % 4 + 1) * P], wf[:, t, :], ident[:, :])
                ins.then_inc(s_tp, 1)
                for t in range(NT):
                    pe.wait_ge(s_wft, 7)
                    if t >= 7:
                        pe.wait_ge(s_add, t - 6)
                    nc.tensor.matmul(tp[:, t % 7, 0:F], wft[:, t, :], b2s[:, :], start=True, stop=True).then_inc(s_bias, 1)

            @block.scalar
            def _(act):
                if softmax_first:
                    act.wait_ge(s_pair, 1)
                    nc.scalar.activation(L[:, :, 0:E_], L[:, :, 0:E_], ACT.Exp).then_inc(s_e, 1)
                act.wait_ge(s_pair, 1 + softmax_first)
                nc.scalar.activation(w[:, :, :], w[:, :, :], ACT.Exp).then_inc(s_e, 1)

            @block.vector
            def _(dve):
                link = Chain(dve, s_dve)
                if E_ < EL:
                    link(nc.vector.memset(L[:, :, E_:EL], -1e30))
                dve.wait_ge(s_lg, 1)
                dve.wait_ge(s_w, 48)
                dve.wait_ge(s_iota, 1)
                real = L[:, :, 0:E_]
                link(nc.vector.tensor_tensor(real, lg[:, 0:NT * E_].rearrange("p (t e) -> p t e", e=E_),
                                             brb[:, :].unsqueeze(1).to_broadcast([P, NT, E_]), ALU.add))
                if softmax_first:
                    link(nc.vector.tensor_reduce(one[:, 0, :], real, AX.X, ALU.max))
                    nc.vector.tensor_tensor(real, real, one[:, 0, :].unsqueeze(2).to_broadcast([P, NT, E_]), ALU.subtract
                                            ).then_inc(s_pair, 1)
                    dve.wait_ge(s_e, 1)
                    link(nc.vector.tensor_reduce(one[:, 0, :], real, AX.X, ALU.add))
                    link(nc.vector.reciprocal(one[:, 1, :], one[:, 0, :]))
                    link(nc.vector.tensor_tensor(real, real, one[:, 1, :].unsqueeze(2).to_broadcast([P, NT, E_]), ALU.mult))

                def exp_pair(w):
                    nc.vector.tensor_copy(one[:, 0, :], w[:, :, 0]).then_inc(s_pair, 1)
                    dve.wait_ge(s_e, 1 + softmax_first)

                top_two(nc, link, L, E_, vals, ids, idf, iota, w, wf, hot, exp_pair)
                nc.vector.tensor_copy(one[:, 0, :], wf[:, :, 0]).then_inc(s_wf, 1)
                dve.wait_ge(s_tp, 1)
                for b in range(7):
                    m = min(4, NT - 4 * b)
                    nc.vector.tensor_copy(wft[:, 4 * b:4 * b + m, :], tp[0:E_, b, 0:m * P].rearrange("e (t p) -> e t p", p=P)
                                          ).then_inc(s_wft, 1)
                for t in range(NT):
                    dve.wait_ge(s_bias, t + 1)
                    nc.vector.tensor_tensor(X[:, t, :], X[:, t, :], tp[:, t % 7, 0:F], ALU.add).then_inc(s_add, 1)
    core.stage_ends()


class Net:

    def __init__(self, layers, column=None):
        self.layers, self.column = layers, column


def stage_nets(core, nets, wf=None, out_bias=None):
    nc, XT, X = core.nc, core.XT, core.X
    with ExitStack() as ctx:
        tiles, nload = [], 0
        for net in nets:
            lay = []
            for W, b, fn in net.layers:
                K, M = W.shape
                kp = min(K, P)
                wt = core.sb(ctx, "w", [kp, K // kp, M])
                bt = core.sb(ctx, "b", [min(M, P), -(-M // P)]) if b is not None else None
                nload += 1 + (b is not None)
                lay.append((wt, bt, fn, K // kp, kp, M))
            tiles.append(lay)
        width = max(-(-l[5] // P) for t in tiles for l in t[:-1])
        depth = max(len(t) - 1 for t in tiles)
        hbuf = core.sb(ctx, "hidden", [P, 2, depth, width, TN])
        yc = core.sb(ctx, "y", [P, TC, F])
        wc = core.sb(ctx, "weights_chunk", [P, TC, 8])
        ob = core.sb(ctx, "out_bias", [P, F])
        up = core.ps(ctx, "up", [P, 4, 512])
        down = core.ps(ctx, "down", [P, 4, 512])
        s_w, s_up, s_act, s_down, s_y, s_dve, s_x = (core.sem(n) for n in (
            "w_in", "up_made", "hidden_made", "down_made", "y_added", "dve", "x_added"))
        if out_bias is not None:
            nload += 1
        ups = [(e, l, m, hf) for e, t in enumerate(tiles) for l in range(len(t) - 1)
               for m in range(-(-t[l][5] // P)) for hf in range(2)]
        NU, ND = len(ups), len(tiles) * TC
        last_of = {}
        for n, (e, l, m, hf) in enumerate(ups):
            last_of[(e, l)] = n
        with nc.Block() as block:
            @block.sync
            def _(sp):
                with nc.allow_non_contiguous_dma(reason="bias columns"):
                    for net, t in zip(nets, tiles):
                        for (W, b, _), (wt, bt, _, _, kp, M) in zip(net.layers, t):
                            sp.dma_start(wt[:, :, :], W.rearrange("(k p) m -> p k m", p=kp)).then_inc(s_w, 16)
                            if b is not None:
                                sp.dma_start(bt[:, :], b.rearrange("(k p) -> p k", p=min(M, P))).then_inc(s_w, 16)
                    if out_bias is not None:
                        sp.dma_start(ob[:, :], out_bias.partition_broadcast(P)).then_inc(s_w, 16)
                sp.wait_ge(s_w, 16 * nload)

            @block.tensor
            def _(pe):
                pe.wait_ge(s_w, 16 * nload)
                nc.tensor.sem_inc(s_down, 1)
                with pe.Fori(0, NTC) as i:
                    def up_step(n):
                        e, l, m, hf = ups[n]
                        wt, bt, fn, nk, kp, M = tiles[e][l]
                        mw = min(P, M - m * P)
                        if l:
                            pe.wait_ge(s_act, i * NU + last_of[(e, l - 1)] + 2)
                        if n >= 4:
                            pe.wait_ge(s_act, i * NU + n - 2)
                        else:
                            pe.wait_ge(s_act, i * NU + 1)
                        for k in range(nk):
                            rhs = (XT[:, k, bass.ds(i * TN + hf * TH, TH)] if l == 0 else
                                   hbuf[0:kp, e % 2, l - 1, k, hf * TH:(hf + 1) * TH])
                            ins = nc.tensor.matmul(up[0:mw, n % 4, 0:TH], wt[:, k, m * P:m * P + mw], rhs,
                                                   start=(k == 0), stop=(k == nk - 1))
                        ins.then_inc(s_up, 1)

                    def down_step(e):
                        wt, _, _, nk, kp, _ = tiles[e][-1]
                        pe.wait_ge(s_act, i * NU + last_of[(e, len(tiles[e]) - 2)] + 2)
                        for j in range(TC):
                            n = e * TC + j
                            if n >= 4:
                                pe.wait_ge(s_y, i * ND + n - 2)
                            else:
                                pe.wait_ge(s_y, i * ND + 1)
                            for k in range(nk):
                                ins = nc.tensor.matmul(down[:, n % 4, 0:F],
                                                       hbuf[0:kp, e % 2, len(tiles[e]) - 2, k, j * P:(j + 1) * P], wt[:, k, :],
                                                       start=(k == 0), stop=(k == nk - 1))
                            ins.then_inc(s_down, 1)

                    for e in range(len(tiles)):
                        for n, u in enumerate(ups):
                            if u[0] == e:
                                up_step(n)
                        if e:
                            down_step(e - 1)
                    down_step(len(tiles) - 1)

            @block.scalar
            def _(act):
                act.wait_ge(s_w, 16 * nload)
                nc.scalar.sem_inc(s_act, 1)
                with act.Fori(0, NTC) as i:
                    for n, (e, l, m, hf) in enumerate(ups):
                        _, bt, fn, _, _, M = tiles[e][l]
                        mw = min(P, M - m * P)
                        act.wait_ge(s_up, i * NU + n + 1)
                        if e >= 2:
                            act.wait_ge(s_down, i * ND + (e - 1) * TC + 1)
                        else:
                            act.wait_ge(s_down, i * ND + 1)
                        nc.scalar.activation(hbuf[0:mw, e % 2, l, m, hf * TH:(hf + 1) * TH], up[0:mw, n % 4, 0:TH], fn,
                                             bias=bt[0:mw, m:m + 1]).then_inc(s_act, 1)

            @block.vector
            def _(dve):
                link = Chain(dve, s_dve)
                dve.wait_ge(s_w, 16 * nload)
                nc.vector.sem_inc(s_y, 1)
                nc.vector.sem_inc(s_x, 1)
                with dve.Fori(0, NTC) as i:
                    NLINK = 1
                    link.n, link.base = 0, i * NLINK
                    dve.wait_ge(s_x, i + 1)
                    if wf is not None:
                        link(nc.vector.tensor_copy(wc[:, :, 0:wf.shape[2]], wf[:, bass.ds(i * TC, TC), :]))
                    for e, net in enumerate(nets):
                        if e:
                            dve.wait_ge(s_y, i * ND + e * TC + 1)
                        for j in range(TC):
                            n = e * TC + j
                            dve.wait_ge(s_down, i * ND + n + 2)
                            o, y = down[:, n % 4, 0:F], yc[:, j, :]
                            if net.column is None and e == 0 and out_bias is not None:
                                ins = nc.vector.tensor_tensor(y, o, ob[:, :], ALU.add)
                            elif e == 0:
                                ins = nc.vector.tensor_scalar(y, o, wc[:, j, net.column:net.column + 1], None, ALU.mult)
                            else:
                                ins = nc.vector.scalar_tensor_tensor(out=y, in0=o, scalar=wc[:, j, net.column:net.column + 1],
                                                                     in1=y, op0=ALU.mult, op1=ALU.add)
                            ins.then_inc(s_y, 1)
                    dve.wait_ge(s_y, (i + 1) * ND + 1)
                    nc.vector.tensor_tensor(X[:, bass.ds(i * TC, TC), :], X[:, bass.ds(i * TC, TC), :], yc[:, :, :], ALU.add
                                            ).then_inc(s_x, 1)
    core.stage_ends()


def stage_kv(core, a, ks, msg):
    nc, XT = core.nc, core.XT
    HD, H, R = 32, 8, 4
    with ExitStack() as ctx:
        w = core.sb(ctx, "w_kv", [P, 2, KF, F])
        w4 = core.sb(ctx, "w_k_fourfold", [P, KF, H, 4, HD])
        b4 = core.sb(ctx, "b_k_fourfold", [P, H])
        bv = core.sb(ctx, "b_v", [P, F])
        less = core.sb(ctx, "less", [P, 2])
        whole = core.sb(ctx, "k_whole", [P, R, CH])
        left = core.sb(ctx, "k_left", [P, R, CH])
        second = core.sb(ctx, "k_second", [P, R, CH], BF16)
        ps = core.ps(ctx, "proj", [P, 8, 512])
        s_w, s_w4, s_ps, s_whole, s_left, s_second, s_ks, s_v, s_one = (core.sem(n) for n in (
            "w_in", "w4_made", "projected", "whole_made", "left_made", "second_made", "ks_made", "v_made", "ones_made"))
        kjobs = [(h, c) for h in range(H) for c in range(NCH)]
        NK = len(kjobs)
        with nc.Block() as block:
            @block.sync
            def _(sp):
                with nc.allow_non_contiguous_dma(reason="bias columns"):
                    for o, n in enumerate("kv"):
                        sp.dma_start(w[:, o, :, :], a["L1_gnn_W" + n].rearrange("(k p) m -> p k m", p=P)).then_inc(s_w, 16)
                    for g in range(4):
                        sp.dma_start(b4[g * HD:(g + 1) * HD, :], a["L1_gnn_bk"].rearrange("(h d) -> d h", d=HD)).then_inc(s_w, 16)
                sp.dma_start(bv[:, :], a["L1_gnn_bv"].partition_broadcast(P)).then_inc(s_w, 16)
                sp.wait_ge(s_w, 16 * 7)

            @block.gpsimd
            def _(pool):
                nc.gpsimd.memset(msg[:, :, :, HD:2 * HD], 1.0).then_inc(s_one, 1)

            @block.tensor
            def _(pe):
                pe.wait_ge(s_w4, 1)
                for n in range(NK + NT):
                    if n >= 8:
                        if n - 8 < NK:
                            pe.wait_ge(s_whole, n - 7)
                        else:
                            pe.wait_ge(s_v, n - 7 - NK)
                    for k in range(KF):
                        if n < NK:
                            h, c = kjobs[n]
                            ins = nc.tensor.matmul(ps[:, n % 8, 0:CH], w4[:, k, h, :, :].rearrange("p g d -> p (g d)"),
                                                   XT[:, k, c * CH:(c + 1) * CH], start=(k == 0), stop=(k == KF - 1))
                        else:
                            t = n - NK
                            ins = nc.tensor.matmul(ps[:, n % 8, 0:F], XT[:, k, t * P:(t + 1) * P], w[:, 1, k, :],
                                                   start=(k == 0), stop=(k == KF - 1))
                    ins.then_inc(s_ps, 1)

            @block.scalar
            def _(act):
                act.wait_ge(s_w, 16 * 7)
                for n in range(NK + 2):
                    if n < NK:
                        h, c = kjobs[n]
                        act.wait_ge(s_ps, n + 1)
                        if n >= R:
                            act.wait_ge(s_left, n - R + 1)
                        nc.scalar.activation(ks[:, h, c * CH:(c + 1) * CH], ps[:, n % 8, 0:CH], ACT.Identity, bias=b4[:, h:h + 1])
                        nc.scalar.activation(whole[:, n % R, :], ps[:, n % 8, 0:CH], ACT.Identity, bias=b4[:, h:h + 1]
                                             ).then_inc(s_whole, 1)
                    if n >= 2:
                        m = n - 2
                        act.wait_ge(s_left, m + 1)
                        if m >= R:
                            act.wait_ge(s_ks, m - R + 1)
                        nc.scalar.copy(second[:, m % R, :], left[:, m % R, :]).then_inc(s_second, 1)

            @block.vector
            def _(dve):
                link = Chain(dve, core.sem("dve"))
                link(nc.vector.memset(less[:, :], 0.0))
                for g, j in ((1, 0), (2, 0), (2, 1)):
                    link(nc.vector.memset(less[g * HD:(g + 1) * HD, j:j + 1], -1.0))
                dve.wait_ge(s_w, 16 * 7)
                for g in range(4):
                    ins = nc.vector.tensor_copy(w4[:, :, :, g, :], w[:, 0, :, :].rearrange("p k (h d) -> p k h d", d=HD))
                ins.then_inc(s_w4, 1)
                for n in range(NK + 2):
                    if n < NK:
                        h, c = kjobs[n]
                        dve.wait_ge(s_whole, n + 1)
                        if n >= R:
                            dve.wait_ge(s_ks, n - R + 1)
                        nc.vector.scalar_tensor_tensor(out=left[:, n % R, :], in0=ks[:, h, c * CH:(c + 1) * CH],
                                                       scalar=less[:, 0:1], in1=whole[:, n % R, :],
                                                       op0=ALU.mult, op1=ALU.add).then_inc(s_left, 1)
                    if n >= 2:
                        h, c = kjobs[n - 2]
                        m = (n - 2) % R
                        dve.wait_ge(s_second, n - 1)
                        nc.vector.scalar_tensor_tensor(out=ks[:, h, c * CH:(c + 1) * CH], in0=second[:, m, :],
                                                       scalar=less[:, 1:2], in1=left[:, m, :],
                                                       op0=ALU.mult, op1=ALU.add).then_inc(s_ks, 1)
                for t in range(NT):
                    dve.wait_ge(s_ps, NK + t + 1)
                    nc.vector.tensor_tensor(msg[:, t, :, :].rearrange("p q (e d) -> p q e d", d=HD)[:, :, 0:3:2, :],
                                            ps[:, (NK + t) % 8, 0:F].rearrange("p (q e d) -> p q e d", e=2, d=HD),
                                            bv[:, :].rearrange("p (q e d) -> p q e d", e=2, d=HD), ALU.add).then_inc(s_v, 1)
    core.stage_ends()


CLIP = 10.0
EXP_HI = 22026.465794806718
EXP_LO = 4.5399929762484854e-05


def stage_attention(core, a, ks, msg):
    nc, XT = core.nc, core.XT
    D, H = 32, 8
    HP = H // 2
    WR, SR, LAG = 4, 2, 4
    per = NT * HP
    by_act = [n for n in range(per) if n % 2 == 0 and not (n < 9 or 30 <= n < 40)]
    by_dve = [n for n in range(per) if n not in by_act]
    proj_at, left_at, second_at, third_at = 30, 60, 68, 76
    items = []
    for n in range(per):
        items.append(("score", n))
        if n >= proj_at and (n - proj_at) % 4 == 0 and (n - proj_at) // 4 < HP:
            items.append(("q", (n - proj_at) // 4))
    NI = len(items)
    at = {x: m for m, x in enumerate(items)}
    scratch = core.X[:, :, :].rearrange("p t f -> p (t f)")
    w = scratch[:, 0:WR * 2 * CH].rearrange("p (r e c) -> p r e c", e=2, c=CH)
    whole = scratch[:, WR * 2 * CH:(WR * 2 + H) * CH].rearrange("p (r c) -> p r c", c=CH)
    sums, den, num = whole[:, 0:4, :], whole[:, 4:6, :], whole[:, 6:8, :]
    stack_at, recip_at = 1, 18
    with ExitStack() as ctx:
        q_hi = core.sb(ctx, "q_first", [P, 2, H, CH], BF16)
        q_lo = core.sb(ctx, "q_rest", [P, 2, H, CH], BF16)
        ex = core.sb(ctx, "exps", [P, WR, 2, CH])
        w4 = core.sb(ctx, "w_q_fourfold", [P, KF, H, 4, D])
        b4 = core.sb(ctx, "b_q_fourfold", [P, H])
        ten = core.sb(ctx, "plus_minus_clip", [P, 2])
        acc = core.ps(ctx, "acc", [P, 4, 512])
        sc = core.ps(ctx, "scores", [P, SR, 2, 512])
        s_c = [core.sem("counts_in") for _ in range(2)]
        s_b, s_ten, s_wq, s_w4, s_sc, s_read, s_ex, s_cl, s_w, s_used, s_free, s_y, s_div, s_left, s_second, s_q, s_den = (
            core.sem(n) for n in ("bias_in", "clip_set", "wq_in", "w4_made", "items_made", "items_read", "bounded_exps_made",
                                  "exps_bounded", "w_made", "w_used", "acc_read", "y_done", "divided", "left_made", "second_made",
                                  "q_made", "den_copied"))
        cbuf = core.sb(ctx, "counts", [P, 2, ST, CH])
        wq = cbuf[:, 0, 0:2, 0:F]

        def project(n, slot, cols):
            for e in range(2):
                for k in range(KF):
                    ins = nc.tensor.matmul(sc[:, slot, e, 0:CH], w4[:, k, 2 * n + e, :, :].rearrange("p g d -> p (g d)"),
                                           XT[:, k, cols], start=(k == 0), stop=(k == KF - 1))
            return ins

        def read_q(n, slot, u):
            for e in range(2):
                j = 2 * n + e
                nc.scalar.activation(q_hi[:, u, j, :], sc[:, slot, e, 0:CH], ACT.Identity, bias=b4[:, j:j + 1])
                ins = nc.scalar.activation(whole[:, j, :], sc[:, slot, e, 0:CH], ACT.Identity, bias=b4[:, j:j + 1])
            return ins

        def two(n):
            return slice(2 * n, 2 * n + 2)

        def left(n, u):
            return nc.vector.tensor_tensor(whole[:, two(n), :], whole[:, two(n), :], q_hi[:, u, two(n), :], ALU.subtract)

        def second(n, u):
            return nc.scalar.copy(q_lo[:, u, two(n), :], whole[:, two(n), :])

        def third(n, u):
            return nc.vector.tensor_tensor(q_lo[0:D, u, two(n), :], whole[0:D, two(n), :], q_lo[0:D, u, two(n), :], ALU.subtract)

        def stack(m):
            j = m % H
            r = D * (j % 4)
            o = 64 * (j % 2) + D * (j % 2 ^ (m < H))
            to = den if m < H else num
            nc.scalar.copy(to[r:r + D, j // 4, :], sums[o:o + D, j // 2, :]).then_inc(s_den, 1)

        def divide(dve, m, c):
            if m == 0:
                dve.wait_ge(s_den, c * 2 * H + 2 * H)
                nc.vector.tensor_scalar(den, den, 1e-20, None, ALU.max).then_inc(s_div, 1)
                dve.wait_ge(s_div, c * 5 + 1)
            if m < 4:
                part = den[:, m // 2, m % 2 * (CH // 2):(m % 2 + 1) * (CH // 2)]
                nc.vector.reciprocal(part, part).then_inc(s_div, 1)
            else:
                dve.wait_ge(s_div, c * 5 + 5)
                nc.vector.tensor_tensor(core.XT_all[:, :, bass.ds(c * CH, CH)], num, den, ALU.mult).then_inc(s_y, 1)

        with nc.Block() as block:
            @block.sync
            def _(sp):
                with nc.allow_non_contiguous_dma(reason="bias columns"):
                    for g in range(4):
                        sp.dma_start(b4[g * D:(g + 1) * D, :], a["L1_gnn_bq"].rearrange("(h d) -> d h", d=D)).then_inc(s_b, 16)
                sp.dma_start(wq, a["L1_gnn_Wq"].rearrange("(k p) m -> p k m", p=P)).then_inc(s_wq, 16)
                sp.wait_ge(s_w4, 1)
                load_counts(core, sp, cbuf, s_c, s_used, per)

            @block.tensor
            def _(pe):
                nc.tensor.sem_inc(s_sc, 1)
                pe.wait_ge(s_w4, 1)
                for n in range(HP):
                    if n >= SR:
                        pe.wait_ge(s_read, n - SR + 2)
                    project(n, n % SR, slice(0, CH)).then_inc(s_sc, 1)
                with pe.Fori(0, NCH // 2) as i:
                    for u in range(2):
                        c = 2 * i + u
                        items0 = c * NI + HP
                        w0 = c * per
                        pe.wait_ge(s_q, c * HP + HP)
                        for m in range(NI + LAG):
                            if m < NI:
                                kind, n = items[m]
                                pe.wait_ge(s_read, items0 + m - SR + 2)
                                if kind == "q":
                                    project(n, m % SR, bass.ds((c + 1) * CH, CH)).then_inc(s_sc, 1)
                                else:
                                    t = n // HP
                                    for e in range(2):
                                        j = 2 * (n % HP) + e
                                        nc.tensor.matmul(sc[:, m % SR, e, 0:CH], ks[0:3 * D, j, t * P:(t + 1) * P],
                                                         q_hi[0:3 * D, u, j, :], start=True, stop=False)
                                        ins = nc.tensor.matmul(sc[:, m % SR, e, 0:CH], ks[:, j, t * P:(t + 1) * P],
                                                               q_lo[:, u, j, :], start=False, stop=True)
                                    ins.then_inc(s_sc, 1)
                            if m >= LAG and items[m - LAG][0] == "score":
                                n = items[m - LAG][1]
                                t, q = n // HP, n % HP
                                if t == 0:
                                    pe.wait_ge(s_free, c * HP + q + 1)
                                pe.wait_ge(s_w, w0 + n + 2)
                                for e in range(2):
                                    ins = nc.tensor.matmul(acc[64 * e:64 * e + 64, q, 0:CH], msg[:, t, q, D * e:D * e + 2 * D],
                                                           w[:, n % WR, e, :], start=(t == 0), stop=(t == NT - 1))
                                ins.then_inc(s_used, 1)

            @block.scalar
            def _(act):
                nc.scalar.sem_inc(s_read, 1)
                nc.scalar.sem_inc(s_free, HP)
                act.wait_ge(s_b, 64)
                act.wait_ge(s_ten, 1)
                for n in range(HP):
                    act.wait_ge(s_sc, n + 2)
                    read_q(n, n % SR, 0).then_inc(s_read, 1)
                for n in range(HP):
                    act.wait_ge(s_left, n + 1)
                    second(n, 0).then_inc(s_second, 1)
                with act.Fori(0, NCH // 2) as i:
                    for u in range(2):
                        c = 2 * i + u
                        items0, w0 = c * NI + HP, c * per
                        for m, (kind, n) in enumerate(items):
                            act.wait_ge(s_sc, items0 + m + 2)
                            if kind == "q":
                                if n == 0:
                                    act.wait_ge(s_y, c + 1)
                                read_q(n, m % SR, 1 - u).then_inc(s_read, 1)
                                continue
                            if stack_at <= n < stack_at + 2 * H:
                                if n == stack_at:
                                    act.wait_ge(s_free, c * HP + HP)
                                    act.wait_ge(s_q, c * HP + HP)
                                stack(n - stack_at)
                            act.wait_ge(s_w, w0 + max(n - WR, -1) + 2)
                            out, score = ex[:, n % WR, :, :], sc[:, m % SR, :, 0:CH]
                            if n in by_act:
                                nc.scalar.activation(out, score, ACT.Relu, bias=ten[:, 0:1], scale=D ** -0.5).then_inc(s_read, 1)
                                act.wait_ge(s_read, items0 + m + 2)
                                nc.scalar.activation(out, out, ACT.Exp, bias=ten[:, 1:2]).then_inc(s_ex, 1)
                            else:
                                nc.scalar.activation(out, score, ACT.Exp, scale=D ** -0.5).then_inc(s_read, 1)
                            if n >= second_at and (n - second_at) % 2 == 0 and (n - second_at) // 2 < HP:
                                b = (n - second_at) // 2
                                act.wait_ge(s_left, (c + 1) * HP + b + 1)
                                second(b, 1 - u).then_inc(s_second, 1)
                        act.wait_ge(s_q, (c + 1) * HP + HP)
                        act.wait_ge(s_y, c + 1)
                        for q in range(HP):
                            act.wait_ge(s_used, w0 + (NT - 1) * HP + q + 1)
                            nc.scalar.copy(sums[:, q, :], acc[:, q, 0:CH]).then_inc(s_free, 1)
                act.wait_ge(s_free, NCH * HP + HP)
                for m in range(2 * H):
                    stack(m)

            @block.vector
            def _(dve):
                nc.vector.sem_inc(s_w, 1)
                nc.vector.memset(ten[:, 0:1], CLIP)
                nc.vector.memset(ten[:, 1:2], -CLIP).then_inc(s_ten, 1)
                dve.wait_ge(s_wq, 16)
                for g in range(4):
                    ins = nc.vector.tensor_copy(w4[:, :, :, g, :], wq.rearrange("p k (h d) -> p k h d", d=D))
                ins.then_inc(s_w4, 1)
                for n in range(HP):
                    dve.wait_ge(s_read, n + 2)
                    left(n, 0).then_inc(s_left, 1)
                for n in range(HP):
                    dve.wait_ge(s_second, n + 1)
                    dve.wait_ge(s_left, n + 1)
                    third(n, 0).then_inc(s_q, 1)
                with dve.Fori(0, NCH // 2) as i:
                    for u in range(2):
                        c = 2 * i + u
                        items0, w0 = c * NI + HP, c * per
                        for n in range(per):
                            t, out = n // HP, ex[:, n % WR, :, :]
                            if n % (HP * ST) == 0:
                                wait_counts(dve, s_c, i, u, t // ST)
                            if n in by_act:
                                dve.wait_ge(s_ex, c * len(by_act) + by_act.index(n) + 1)
                            else:
                                dve.wait_ge(s_read, items0 + at[("score", n)] + 2)
                                nc.vector.tensor_scalar(out, out, EXP_HI, EXP_LO, ALU.min, ALU.max).then_inc(s_cl, 1)
                                dve.wait_ge(s_cl, c * len(by_dve) + by_dve.index(n) + 1)
                            if n >= WR:
                                dve.wait_ge(s_used, w0 + n - WR + 1)
                            counts = cbuf[:, (u * NL + t // ST) % 2, t % ST:t % ST + 1, :].to_broadcast([P, 2, CH])
                            if n in by_act:
                                ins = nc.vector.scalar_tensor_tensor(out=w[:, n % WR, :, :], in0=out, scalar=EXP_HI, in1=counts,
                                                                     op0=ALU.min, op1=ALU.mult)
                            else:
                                ins = nc.vector.tensor_tensor(w[:, n % WR, :, :], out, counts, ALU.mult)
                            ins.then_inc(s_w, 1)
                            if (n - recip_at) % 2 == 0 and 0 <= (n - recip_at) // 2 < 5:
                                divide(dve, (n - recip_at) // 2, c)
                            b = (n - left_at) // 2
                            if (n - left_at) % 2 == 0 and 0 <= b < HP:
                                dve.wait_ge(s_read, items0 + at[("q", b)] + 2)
                                left(b, 1 - u).then_inc(s_left, 1)
                            b = (n - third_at) // 2
                            if (n - third_at) % 2 == 0 and 0 <= b < HP:
                                dve.wait_ge(s_second, (c + 1) * HP + b + 1)
                                dve.wait_ge(s_left, (c + 1) * HP + b + 1)
                                third(b, 1 - u).then_inc(s_q, 1)
                for m in range(5):
                    divide(dve, m, NCH)
                dve.wait_ge(s_y, NCH + 1)
                dve.wait_ge(s_q, HP * NCH + HP)
    core.stage_ends()


def stage_out_proj(core, a, T, parked):
    nc, XT, X = core.nc, core.XT, core.X
    with ExitStack() as ctx:
        w = core.sb(ctx, "w_p", [P, KF, F])
        bp = core.sb(ctx, "b_p", [P, F])
        ps = core.ps(ctx, "proj", [P, 8, 512])
        s_w, s_t, s_x, s_ps, s_add, s_dve = (core.sem(n) for n in ("w_in", "t_in", "x_in", "projected", "added", "dve"))
        with nc.Block() as block:
            @block.sync
            def _(sp):
                sp.dma_start(w[:, :, :], a["L1_gnn_Wp"].rearrange("(k p) m -> p k m", p=P)).then_inc(s_w, 16)
                sp.dma_start(bp[:, :], a["L1_gnn_bp"].partition_broadcast(P)).then_inc(s_w, 16)
                sp.dma_start(T[:, :, :], parked[0]).then_inc(s_t, 16)
                sp.dma_start(X[:, :, :], parked[1]).then_inc(s_x, 16)
                sp.wait_ge(s_x, 16)

            @block.tensor
            def _(pe):
                pe.wait_ge(s_w, 32)
                for t in range(NT):
                    if t >= 8:
                        pe.wait_ge(s_add, t - 7)
                    for k in range(KF):
                        ins = nc.tensor.matmul(ps[:, t % 8, 0:F], XT[:, k, t * P:(t + 1) * P], w[:, k, :],
                                               start=(k == 0), stop=(k == KF - 1))
                    ins.then_inc(s_ps, 1)

            @block.vector
            def _(dve):
                link = Chain(dve, s_dve)
                dve.wait_ge(s_w, 32)
                dve.wait_ge(s_t, 16)
                link(nc.vector.tensor_tensor(T[:, :, :], T[:, :, :], bp[:, :].unsqueeze(1).to_broadcast([P, NT, F]), ALU.add))
                for t in range(NT):
                    dve.wait_ge(s_ps, t + 1)
                    nc.vector.tensor_tensor(T[:, t, :], T[:, t, :], ps[:, t % 8, 0:F], ALU.add).then_inc(s_add, 1)
                dve.wait_ge(s_add, NT)
                dve.wait_ge(s_x, 16)
                link(nc.vector.tensor_tensor(X[:, :, :], X[:, :, :], T[:, :, :], ALU.add))
    core.stage_ends()


def after_gat(core, a):
    stage_ones_off(core)
    NE0, NE1 = a["L0_ffn_W1"].shape[0], a["L1_ffn_eW1"].shape[0]
    with ExitStack() as c:
        wf = core.sb(c, "expert_weights", [P, NT, NE0])
        with ExitStack() as c2:
            T = core.sb(c2, "t", [P, NT, F])
            stage_norm(core, core.X, T, a["L0_ffn_gamma"], a["L0_ffn_beta"], times=2)
        stage_route(core, a["L0_ffn_Wr"], a["L0_ffn_br"], a["L0_ffn_b2"], wf, NE0, 0)
        stage_nets(core, [Net([(a["L0_ffn_W1"][e], a["L0_ffn_b1"][e], ACT.Gelu), (a["L0_ffn_W2"][e], None, None)], e)
                          for e in range(NE0)], wf)
    parked = core.nc.dram_tensor("parked", (2, P, NT, F), F32, kind="Internal").ap()
    with ExitStack() as c:
        T = core.sb(c, "t", [P, NT, F])
        stage_norm(core, core.X, T, park=parked)
    with ExitStack() as c:
        ks = core.sb(c, "k_stacks", [P, 8, NP], BF16)
        msg = core.sb(c, "values", [P, NT, 4, 96])
        stage_kv(core, a, ks, msg)
        stage_attention(core, a, ks, msg)
    with ExitStack() as c:
        T = core.sb(c, "t", [P, NT, F])
        stage_out_proj(core, a, T, parked)
        stage_norm(core, T, T, a["L1_gnn_ln_g"], a["L1_gnn_ln_b"])
    stage_nets(core, [Net([(a["L1_gnn_W1"], a["L1_gnn_b1"], ACT.Gelu), (a["L1_gnn_W2"], None, None)])],
               out_bias=a["L1_gnn_b2"])
    with ExitStack() as c:
        wf = core.sb(c, "expert_weights", [P, NT, NE1])
        with ExitStack() as c2:
            T = core.sb(c2, "t", [P, NT, F])
            stage_norm(core, core.X, T)
        stage_route(core, a["L1_ffn_gW"], a["L1_ffn_gb"], a["L1_ffn_eb3"], wf, NE1, 1)
        shared = Net([(a["L1_ffn_sW1"], a["L1_ffn_sb1"], ACT.Relu), (a["L1_ffn_sW2"], a["L1_ffn_sb2"], ACT.Relu),
                      (a["L1_ffn_sW3"], None, None)])
        stage_nets(core, [shared] + [Net([(a["L1_ffn_eW1"][e], a["L1_ffn_eb1"][e], ACT.Relu),
                                          (a["L1_ffn_eW2"][e], a["L1_ffn_eb2"][e], ACT.Relu),
                                          (a["L1_ffn_eW3"][e], None, None)], e) for e in range(NE1)],
                   wf, out_bias=a["L1_ffn_sb3"])


_HOST_T = ("L1_gnn_Wq", "L1_gnn_Wk", "L1_gnn_Wv", "L1_gnn_Wp", "L1_gnn_W1", "L1_gnn_W2")


def stage_store(core, out):
    nc, X = core.nc, core.X
    s_out = core.sem("stored")
    with nc.Block() as block:
        @block.sync
        def _(sp):
            sp.dma_start(out[0:(NT - 1) * P, :].rearrange("(t p) f -> p t f", p=P), X[:, 0:NT - 1, :]).then_inc(s_out, 16)
            sp.dma_start(out[(NT - 1) * P:N, :], X[0:LAST, NT - 1, :]).then_inc(s_out, 16)
            sp.wait_ge(s_out, 32)
    core.stage_ends()


def program(nc, a, out):
    with ExitStack() as ctx:
        core = Core(nc, ctx)
        core.X = core.sb(ctx, "x", [P, NT, F])
        core.XT_all = core.sb(ctx, "xt", [P, KF, CH + NP + AHEAD])
        core.XT = core.XT_all[:, :, CH:CH + NP + AHEAD]
        core.ident = core.sb(ctx, "identity", [P, P])
        core.ones = core.sb(ctx, "ones", [P, P])
        core.C = nc.dram_tensor("edge_counts", (CELLS + EG * EP + EJ, 1), F32, kind="Internal").ap()
        core.s_clear = core.lasting_sem("c_cleared")
        with ExitStack() as c2:
            g = Gat(core, c2, HEADS)
            with ExitStack() as c3:
                core.zero = core.sb(c3, "zero", [P, NP])
                stage_load(core, a["x"])
                with ExitStack() as c4:
                    T = core.sb(c4, "t", [P, NT, F])
                    stage_norm(core, core.X, T)
                stage_gat_weights(core, g, a["L0_gnn_W1"], a["L0_gnn_a_src1"], a["L0_gnn_a_dst1"], HEADS, clear=True)
                stage_edges(core, a["src"], a["dst"])
            stage_gat_aggregate(core, g, a["L0_gnn_b1"], HEADS)
        with ExitStack() as c2:
            g = Gat(core, c2, 1)
            stage_gat_weights(core, g, a["L0_gnn_W2"], a["L0_gnn_a_src2"], a["L0_gnn_a_dst2"], 1)
            stage_gat_one_head(core, g, a["L0_gnn_b2"])
        after_gat(core, a)
        stage_store(core, out)


def kernel(**inputs):
    import numpy as _np
    import concourse.bacc as _bacc
    from concourse import mybir as _mybir
    from concourse.bass_utils import run_bass_kernel_spmd as _run

    nc = _bacc.Bacc("TRN2", target_bir_lowering=False, num_devices=1)
    arrays, args = {}, {}
    for name in inputs:
        v = _np.asarray(inputs[name])
        v = _np.ascontiguousarray(v.T if name in _HOST_T else v)
        arrays[f"in_{name}_dram"] = v
        args[name] = nc.dram_tensor(f"in_{name}_dram", v.shape, _mybir.dt.from_np(v.dtype), kind="ExternalInput").ap()
    out = nc.dram_tensor("out_0_dram", (N, F), _mybir.dt.float32, kind="ExternalOutput").ap()
    program(nc, args, out)
    return _run(nc, [arrays], core_ids=[0]).results[0]["out_0_dram"]
```
